# Optimizing a Trainium2 kernel written in Bass

```python
import numpy as np
import jax
import jax.numpy as jnp

def _softmax(x, axis=-1):
    return jax.nn.softmax(x, axis=axis)

def _gelu(x):
    return jax.nn.gelu(x, approximate=True)

def _silu(x):
    return jax.nn.silu(x)

def _sigmoid(x):
    return jax.nn.sigmoid(x)

def _layernorm(x, axis=-1, eps=1e-05):
    m = jnp.mean(x, axis=axis, keepdims=True)
    v = jnp.var(x, axis=axis, keepdims=True)
    return (x - m) / jnp.sqrt(v + eps)

def _scatter_add(tgt, idx, src, axis=0):
    return tgt.at[idx].add(src)

def _segment_sum(src, seg, n):
    return jax.ops.segment_sum(src, seg, n)
kernel_name = 'mk_xattn_ffn_d4_seqx_r4_17c9f3'

def setup_inputs(seed: int=0):
    np.random.seed(seed)
    _w = jnp.asarray

    def _rec_inputs():
        import jax
        import jax.numpy as jnp
        _rk = jax.random.key(seed)
        x = -0.0005207 + 1.001 * jax.random.normal(jax.random.fold_in(_rk, 1), (2, 512, 256), jnp.float32)
        _lenS = 512 - jax.random.randint(jax.random.fold_in(_rk, 7), (2,), 0, max(1, 512 // 4) + 1, jnp.int32)
        _lenS2 = 1024 - jax.random.randint(jax.random.fold_in(_rk, 8), (2,), 0, max(1, 1024 // 4) + 1, jnp.int32)
        _ctx_1024P = jax.random.normal(jax.random.fold_in(_rk, 11), (2, 16, 256), jnp.float32)
        _ctx_1024c = jax.random.dirichlet(jax.random.fold_in(_rk, 511), 0.3 * jnp.ones((16,), jnp.float32), (2, 1024))
        _ctx_1024t = jnp.einsum('bsk,bkd->bsd', _ctx_1024c, _ctx_1024P)
        _ctx_1024t = _ctx_1024t * jax.lax.rsqrt(jnp.mean(jnp.square(_ctx_1024t)) + 1e-12) * 0.953939
        ctx_1024 = -1.52775e-05 + 0.999936 * (_ctx_1024t + 0.3 * jax.random.normal(jax.random.fold_in(_rk, 611), (2, 1024, 256), jnp.float32))
        return (x, ctx_1024)
    x, ctx_1024 = _rec_inputs()

    def _L0_xattn_setup():
        import jax, jax.numpy as jnp
        import numpy as np
        DIM = 256
        HEADS = 16
        DHEAD = 64
        INNER = HEADS * DHEAD
        EPS = 1e-05

        def layer_norm(x, g, b):
            mu = jnp.mean(x, axis=-1, keepdims=True)
            var = jnp.mean(jnp.square(x - mu), axis=-1, keepdims=True)
            return (x - mu) * jax.lax.rsqrt(var + EPS) * g + b

        def apply_rope(x, cos, sin):
            d2 = x.shape[-1] // 2
            x1, x2 = (x[..., :d2], x[..., d2:])
            return jnp.concatenate([x1 * cos - x2 * sin, x2 * cos + x1 * sin], axis=-1)
        key = jax.random.key(seed)
        ks = jax.random.split(key, 10)
        B, N, S = (8, 64, 1024)
        latents = jax.random.normal(ks[0], (B, N, DIM), dtype=jnp.float32)
        context = jax.random.normal(ks[1], (B, S, DIM), dtype=jnp.float32)
        cos = jax.random.uniform(ks[2], (S, DHEAD // 2), dtype=jnp.float32)
        sin = jax.random.uniform(ks[3], (S, DHEAD // 2), dtype=jnp.float32)
        init = lambda k, shp, fan_in: jax.random.normal(k, shp, dtype=jnp.float32) / np.sqrt(fan_in)
        return {'latents': latents, 'context': context, 'cos': cos, 'sin': sin, 'ln_lat_g': jnp.ones((DIM,), jnp.float32), 'ln_lat_b': jnp.zeros((DIM,), jnp.float32), 'ln_ctx_g': jnp.ones((DIM,), jnp.float32), 'ln_ctx_b': jnp.zeros((DIM,), jnp.float32), 'Wq': init(ks[4], (DIM, INNER), DIM), 'Wkv': init(ks[5], (DIM, 2 * INNER), DIM), 'Wo': init(ks[6], (INNER, DIM), INNER), 'bo': jnp.zeros((DIM,), jnp.float32)}
    _L0_xattn_all = _L0_xattn_setup()
    _L0_xattn_in = {k: v for k, v in _L0_xattn_all.items() if k in ('cos', 'sin', 'ln_lat_g', 'ln_lat_b', 'ln_ctx_g', 'ln_ctx_b', 'Wq', 'Wkv', 'Wo', 'bo')}
    del _L0_xattn_all

    def _L0_ffn_setup():
        import jax, jax.numpy as jnp
        import numpy as np
        B, S, DIM, FFN, E = (4, 512, 256, 1024, 8)
        key = jax.random.key(seed)
        k0, k1, k2, k3 = jax.random.split(key, 4)
        scale = 0.02
        return {'hidden_states': jax.random.normal(k0, (B, S, DIM), jnp.float32), 'router_w': jax.random.normal(k1, (DIM, E), jnp.float32) * scale, 'router_b': jnp.zeros((E,), jnp.float32), 'w1': jax.random.normal(k2, (E, DIM, 2 * FFN), jnp.float32) * scale, 'w2': jax.random.normal(k3, (E, FFN, DIM), jnp.float32) * scale}
    _L0_ffn_all = _L0_ffn_setup()
    _L0_ffn_in = {k: v for k, v in _L0_ffn_all.items() if k in ('router_w', 'router_b', 'w1', 'w2')}
    del _L0_ffn_all

    def _L1_xattn_setup():
        import jax, jax.numpy as jnp
        import numpy as np
        DIM = 256
        HEAD_DIM = 64
        NUM_HEADS = 8
        INNER = HEAD_DIM * NUM_HEADS
        ROT_DIM = HEAD_DIM
        ROPE_BASE = 10000.0
        EPS = 1e-05

        def layer_norm(x, g, b):
            mu = jnp.mean(x, axis=-1, keepdims=True)
            var = jnp.var(x, axis=-1, keepdims=True)
            return (x - mu) * jax.lax.rsqrt(var + EPS) * g + b

        def rope_rotate_k(k):
            n = k.shape[1]
            half = ROT_DIM // 2
            inv_freq = 1.0 / ROPE_BASE ** (jnp.arange(0, ROT_DIM, 2, dtype=jnp.float32) / ROT_DIM)
            theta = jnp.arange(n, dtype=jnp.float32)[:, None] * inv_freq[None, :]
            angles = jnp.concatenate([theta, theta], axis=-1)
            cos = jnp.cos(angles)[None, :, None, :].astype(k.dtype)
            sin = jnp.sin(angles)[None, :, None, :].astype(k.dtype)
            k_rope, k_pass = (k[..., :ROT_DIM], k[..., ROT_DIM:])
            neg_half = jnp.concatenate([-k_rope[..., half:], k_rope[..., :half]], axis=-1)
            k_rope = k_rope * cos + neg_half * sin
            return jnp.concatenate([k_rope, k_pass], axis=-1)
        key = jax.random.key(seed)
        ks = jax.random.split(key, 5)
        b, n, m = (8, 2048, 64)
        s = 1.0 / np.sqrt(DIM)
        return {'x': jax.random.normal(ks[0], (b, n, DIM), jnp.float32), 'latents': jax.random.normal(ks[1], (b, m, DIM), jnp.float32), 'gamma_x': jnp.ones((DIM,), jnp.float32), 'beta_x': jnp.zeros((DIM,), jnp.float32), 'gamma_l': jnp.ones((DIM,), jnp.float32), 'beta_l': jnp.zeros((DIM,), jnp.float32), 'Wq': jax.random.normal(ks[2], (DIM, INNER), jnp.float32) * s, 'Wkv': jax.random.normal(ks[3], (DIM, 2 * INNER), jnp.float32) * s, 'Wo': jax.random.normal(ks[4], (INNER, DIM), jnp.float32) * (1.0 / np.sqrt(INNER))}
    _L1_xattn_all = _L1_xattn_setup()
    _L1_xattn_in = {k: v for k, v in _L1_xattn_all.items() if k in ('gamma_x', 'beta_x', 'gamma_l', 'beta_l', 'Wq', 'Wkv', 'Wo')}
    del _L1_xattn_all

    def _L1_ffn_setup():
        import jax, jax.numpy as jnp
        import numpy as np
        S, B, D, FF, E = (256, 2, 256, 512, 8)
        key = jax.random.key(seed)
        ks = jax.random.split(key, 8)
        s = 0.02
        return {'hidden_states': jax.random.normal(ks[0], (S, B, D), dtype=jnp.float32), 'router_w': jax.random.normal(ks[1], (E, D), dtype=jnp.float32) * s, 'expert_gate': jax.random.normal(ks[2], (E, D, FF), dtype=jnp.float32) * s, 'expert_up': jax.random.normal(ks[3], (E, D, FF), dtype=jnp.float32) * s, 'expert_down': jax.random.normal(ks[4], (E, FF, D), dtype=jnp.float32) * s, 'shared_gate': jax.random.normal(ks[5], (D, FF), dtype=jnp.float32) * s, 'shared_up': jax.random.normal(ks[6], (D, FF), dtype=jnp.float32) * s, 'shared_down': jax.random.normal(ks[7], (FF, D), dtype=jnp.float32) * s}
    _L1_ffn_all = _L1_ffn_setup()
    _L1_ffn_in = {k: v for k, v in _L1_ffn_all.items() if k in ('router_w', 'expert_gate', 'expert_up', 'expert_down', 'shared_gate', 'shared_up', 'shared_down')}
    del _L1_ffn_all

    def _L2_xattn_setup():
        import jax, jax.numpy as jnp
        import numpy as np
        N_EMBD = 256
        N_HEAD = 16
        HEAD_DIM = N_EMBD // N_HEAD
        key = jax.random.key(seed)
        ks = jax.random.split(key, 8)
        B, T, T_ctx, C = (2, 512, 512, N_EMBD)
        s = 1.0 / np.sqrt(C)
        return {'x': jax.random.normal(ks[0], (B, T, C), dtype=jnp.float32), 'context': jax.random.normal(ks[1], (B, T_ctx, C), dtype=jnp.float32), 'Wq': jax.random.normal(ks[2], (C, C), dtype=jnp.float32) * s, 'bq': jnp.zeros((C,), dtype=jnp.float32), 'Wkv': jax.random.normal(ks[3], (C, 2 * C), dtype=jnp.float32) * s, 'bkv': jnp.zeros((2 * C,), dtype=jnp.float32), 'Wp': jax.random.normal(ks[4], (C, C), dtype=jnp.float32) * s, 'bp': jnp.zeros((C,), dtype=jnp.float32)}
    _L2_xattn_all = _L2_xattn_setup()
    _L2_xattn_in = {k: v for k, v in _L2_xattn_all.items() if k in ('Wq', 'bq', 'Wkv', 'bkv', 'Wp', 'bp')}
    del _L2_xattn_all

    def _L2_ffn_setup():
        import jax, jax.numpy as jnp
        import numpy as np
        D_MODEL = 256
        NUM_EXPERTS = 8
        TOP_K = 2
        key = jax.random.key(seed)
        k_x, k_g, k_w1, k_w2 = jax.random.split(key, 4)
        B, S, D, E = (4, 512, D_MODEL, NUM_EXPERTS)
        s_in = 1.0 / np.sqrt(D)
        s_hid = 1.0 / np.sqrt(4 * D)
        return {'x': jax.random.normal(k_x, (B, S, D), dtype=jnp.float32), 'gate_w': jax.random.uniform(k_g, (E, D), jnp.float32, -s_in, s_in), 'w1': jax.random.uniform(k_w1, (E, 4 * D, D), jnp.float32, -s_in, s_in), 'w2': jax.random.uniform(k_w2, (E, D, 4 * D), jnp.float32, -s_hid, s_hid)}
    _L2_ffn_all = _L2_ffn_setup()
    _L2_ffn_in = {k: v for k, v in _L2_ffn_all.items() if k in ('gate_w', 'w1', 'w2')}
    del _L2_ffn_all

    def _L3_xattn_setup():
        import jax, jax.numpy as jnp
        import numpy as np
        NUM_HEADS = 16

        def _rope_tables(seq_len, head_dim, dtype):
            inv_freq = 1.0 / 10000.0 ** (jnp.arange(0, head_dim, 2, dtype=jnp.float32) / head_dim)
            freqs = jnp.arange(seq_len, dtype=jnp.float32)[:, None] * inv_freq[None, :]
            emb = jnp.concatenate([freqs, freqs], axis=-1)
            return (jnp.cos(emb).astype(dtype), jnp.sin(emb).astype(dtype))

        def _rotate_half(t):
            d = t.shape[-1] // 2
            return jnp.concatenate([-t[..., d:], t[..., :d]], axis=-1)

        def _apply_rope(t):
            cos, sin = _rope_tables(t.shape[2], t.shape[3], t.dtype)
            return t * cos[None, None] + _rotate_half(t) * sin[None, None]

        def _forward(x, context, Wq, Wkv, Wo, bo):
            B, Nq, C = x.shape
            Nkv = context.shape[1]
            H = NUM_HEADS
            hd = C // H
            scale = hd ** (-0.5)
            q = (x @ Wq).reshape(B, Nq, H, hd).transpose(0, 2, 1, 3)
            kv = (context @ Wkv).reshape(B, Nkv, 2, H, hd).transpose(2, 0, 3, 1, 4)
            k, v = (kv[0], kv[1])
            q = _apply_rope(q)
            k = _apply_rope(k)
            attn = jnp.einsum('bhqd,bhkd->bhqk', q, k) * scale
            attn = jax.nn.softmax(attn, axis=-1)
            out = jnp.einsum('bhqk,bhkd->bhqd', attn, v)
            out = out.transpose(0, 2, 1, 3).reshape(B, Nq, C)
            return out @ Wo + bo
        key = jax.random.key(seed)
        ks = jax.random.split(key, 6)
        B, N, C = (2, 512, 256)
        s = C ** (-0.5)
        return {'x': jax.random.normal(ks[0], (B, N, C), dtype=jnp.float32), 'context': jax.random.normal(ks[1], (B, N, C), dtype=jnp.float32), 'Wq': jax.random.normal(ks[2], (C, C), dtype=jnp.float32) * s, 'Wkv': jax.random.normal(ks[3], (C, 2 * C), dtype=jnp.float32) * s, 'Wo': jax.random.normal(ks[4], (C, C), dtype=jnp.float32) * s, 'bo': jnp.zeros((C,), dtype=jnp.float32)}
    _L3_xattn_all = _L3_xattn_setup()
    _L3_xattn_in = {k: v for k, v in _L3_xattn_all.items() if k in ('Wq', 'Wkv', 'Wo', 'bo')}
    del _L3_xattn_all

    def _L3_ffn_setup():
        import jax, jax.numpy as jnp
        import numpy as np
        EPS = float(jnp.finfo(jnp.float32).eps)
        TOP_K = 2

        def rmsnorm(x, w):
            return x * jax.lax.rsqrt(jnp.mean(x * x, axis=-1, keepdims=True) + EPS) * w
        B, T, D_IN, D_MODEL, D_FF, D_OUT, E = (8, 256, 256, 256, 1024, 256, 8)
        STD = 0.02
        key = jax.random.key(seed)
        ks = jax.random.split(key, 8)
        return {'s': jax.random.normal(ks[0], (B, T, D_IN), dtype=jnp.float32), 'W_in': STD * jax.random.normal(ks[1], (D_MODEL, D_IN), dtype=jnp.float32), 'in_norm_w': jnp.ones((D_MODEL,), dtype=jnp.float32), 'Wr': STD * jax.random.normal(ks[2], (E, D_MODEL), dtype=jnp.float32), 'expert_bias': jnp.zeros((E,), dtype=jnp.float32), 'Wg': STD * jax.random.normal(ks[3], (E, D_FF, D_MODEL), dtype=jnp.float32), 'Wu': STD * jax.random.normal(ks[4], (E, D_FF, D_MODEL), dtype=jnp.float32), 'Wd': STD * jax.random.normal(ks[5], (E, D_MODEL, D_FF), dtype=jnp.float32), 'enorm_w': jnp.ones((E, D_MODEL), dtype=jnp.float32), 'out_norm_w': jnp.ones((D_MODEL,), dtype=jnp.float32), 'W_out': STD * jax.random.normal(ks[6], (D_OUT, D_MODEL), dtype=jnp.float32)}
    _L3_ffn_all = _L3_ffn_setup()
    _L3_ffn_in = {k: v for k, v in _L3_ffn_all.items() if k in ('W_in', 'in_norm_w', 'Wr', 'expert_bias', 'Wg', 'Wu', 'Wd', 'enorm_w', 'out_norm_w', 'W_out')}
    del _L3_ffn_all
    return {'x': x, 'ctx_1024': ctx_1024, 'L0_xattn_cos': _L0_xattn_in['cos'], 'L0_xattn_sin': _L0_xattn_in['sin'], 'L0_xattn_ln_lat_g': _L0_xattn_in['ln_lat_g'], 'L0_xattn_ln_lat_b': _L0_xattn_in['ln_lat_b'], 'L0_xattn_ln_ctx_g': _L0_xattn_in['ln_ctx_g'], 'L0_xattn_ln_ctx_b': _L0_xattn_in['ln_ctx_b'], 'L0_xattn_Wq': _L0_xattn_in['Wq'], 'L0_xattn_Wkv': _L0_xattn_in['Wkv'], 'L0_xattn_Wo': _L0_xattn_in['Wo'], 'L0_xattn_bo': _L0_xattn_in['bo'], 'L0_ffn_router_w': _L0_ffn_in['router_w'], 'L0_ffn_router_b': _L0_ffn_in['router_b'], 'L0_ffn_w1': _L0_ffn_in['w1'], 'L0_ffn_w2': _L0_ffn_in['w2'], 'L1_xattn_gamma_x': _L1_xattn_in['gamma_x'], 'L1_xattn_beta_x': _L1_xattn_in['beta_x'], 'L1_xattn_gamma_l': _L1_xattn_in['gamma_l'], 'L1_xattn_beta_l': _L1_xattn_in['beta_l'], 'L1_xattn_Wq': _L1_xattn_in['Wq'], 'L1_xattn_Wkv': _L1_xattn_in['Wkv'], 'L1_xattn_Wo': _L1_xattn_in['Wo'], 'L1_ffn_router_w': _L1_ffn_in['router_w'], 'L1_ffn_expert_gate': _L1_ffn_in['expert_gate'], 'L1_ffn_expert_up': _L1_ffn_in['expert_up'], 'L1_ffn_expert_down': _L1_ffn_in['expert_down'], 'L1_ffn_shared_gate': _L1_ffn_in['shared_gate'], 'L1_ffn_shared_up': _L1_ffn_in['shared_up'], 'L1_ffn_shared_down': _L1_ffn_in['shared_down'], 'L2_xattn_Wq': _L2_xattn_in['Wq'], 'L2_xattn_bq': _L2_xattn_in['bq'], 'L2_xattn_Wkv': _L2_xattn_in['Wkv'], 'L2_xattn_bkv': _L2_xattn_in['bkv'], 'L2_xattn_Wp': _L2_xattn_in['Wp'], 'L2_xattn_bp': _L2_xattn_in['bp'], 'L2_ffn_gate_w': _L2_ffn_in['gate_w'], 'L2_ffn_w1': _L2_ffn_in['w1'], 'L2_ffn_w2': _L2_ffn_in['w2'], 'L3_xattn_Wq': _L3_xattn_in['Wq'], 'L3_xattn_Wkv': _L3_xattn_in['Wkv'], 'L3_xattn_Wo': _L3_xattn_in['Wo'], 'L3_xattn_bo': _L3_xattn_in['bo'], 'L3_ffn_W_in': _L3_ffn_in['W_in'], 'L3_ffn_in_norm_w': _L3_ffn_in['in_norm_w'], 'L3_ffn_Wr': _L3_ffn_in['Wr'], 'L3_ffn_expert_bias': _L3_ffn_in['expert_bias'], 'L3_ffn_Wg': _L3_ffn_in['Wg'], 'L3_ffn_Wu': _L3_ffn_in['Wu'], 'L3_ffn_Wd': _L3_ffn_in['Wd'], 'L3_ffn_enorm_w': _L3_ffn_in['enorm_w'], 'L3_ffn_out_norm_w': _L3_ffn_in['out_norm_w'], 'L3_ffn_W_out': _L3_ffn_in['W_out']}

def reference(x, ctx_1024, L0_xattn_cos, L0_xattn_sin, L0_xattn_ln_lat_g, L0_xattn_ln_lat_b, L0_xattn_ln_ctx_g, L0_xattn_ln_ctx_b, L0_xattn_Wq, L0_xattn_Wkv, L0_xattn_Wo, L0_xattn_bo, L0_ffn_router_w, L0_ffn_router_b, L0_ffn_w1, L0_ffn_w2, L1_xattn_gamma_x, L1_xattn_beta_x, L1_xattn_gamma_l, L1_xattn_beta_l, L1_xattn_Wq, L1_xattn_Wkv, L1_xattn_Wo, L1_ffn_router_w, L1_ffn_expert_gate, L1_ffn_expert_up, L1_ffn_expert_down, L1_ffn_shared_gate, L1_ffn_shared_up, L1_ffn_shared_down, L2_xattn_Wq, L2_xattn_bq, L2_xattn_Wkv, L2_xattn_bkv, L2_xattn_Wp, L2_xattn_bp, L2_ffn_gate_w, L2_ffn_w1, L2_ffn_w2, L3_xattn_Wq, L3_xattn_Wkv, L3_xattn_Wo, L3_xattn_bo, L3_ffn_W_in, L3_ffn_in_norm_w, L3_ffn_Wr, L3_ffn_expert_bias, L3_ffn_Wg, L3_ffn_Wu, L3_ffn_Wd, L3_ffn_enorm_w, L3_ffn_out_norm_w, L3_ffn_W_out):
    import jax
    import jax.numpy as jnp

    def _L0_xattn_ref(latents, context, cos, sin, ln_lat_g, ln_lat_b, ln_ctx_g, ln_ctx_b, Wq, Wkv, Wo, bo):
        import jax, jax.numpy as jnp
        import numpy as np
        DIM = 256
        HEADS = 16
        DHEAD = 64
        INNER = HEADS * DHEAD
        EPS = 1e-05

        def layer_norm(x, g, b):
            mu = jnp.mean(x, axis=-1, keepdims=True)
            var = jnp.mean(jnp.square(x - mu), axis=-1, keepdims=True)
            return (x - mu) * jax.lax.rsqrt(var + EPS) * g + b

        def apply_rope(x, cos, sin):
            d2 = x.shape[-1] // 2
            x1, x2 = (x[..., :d2], x[..., d2:])
            return jnp.concatenate([x1 * cos - x2 * sin, x2 * cos + x1 * sin], axis=-1)
        b, n, _ = latents.shape
        s = context.shape[1]
        lat = layer_norm(latents, ln_lat_g, ln_lat_b)
        ctx = layer_norm(context, ln_ctx_g, ln_ctx_b)
        q = (lat @ Wq).reshape(b, n, HEADS, DHEAD).transpose(0, 2, 1, 3)
        kv = ctx @ Wkv
        k, v = jnp.split(kv, 2, axis=-1)
        k = k.reshape(b, s, HEADS, DHEAD).transpose(0, 2, 1, 3)
        v = v.reshape(b, s, HEADS, DHEAD).transpose(0, 2, 1, 3)
        k = apply_rope(k, cos[None, None], sin[None, None])
        scale = DHEAD ** (-0.5)
        attn = jnp.einsum('bhnd,bhsd->bhns', q, k) * scale
        attn = jnp.clip(attn, -11.0, 11.0)
        attn = jax.nn.softmax(attn, axis=-1)
        out = jnp.einsum('bhns,bhsd->bhnd', attn, v)
        out = out.transpose(0, 2, 1, 3).reshape(b, n, INNER)
        return out @ Wo + bo

    def _L0_ffn_ref(hidden_states, router_w, router_b, w1, w2):
        import jax, jax.numpy as jnp
        import numpy as np
        B, S, DIM, FFN, E = (4, 512, 256, 1024, 8)
        b, s, d = hidden_states.shape
        x = hidden_states.reshape(-1, d)
        logits = x @ router_w + router_b
        route = jax.nn.softmax(logits, axis=1)
        max_prob = jnp.max(route, axis=1, keepdims=True)
        max_ind = jnp.argmax(route, axis=1)
        out = jnp.zeros_like(x)
        num_experts = w1.shape[0]
        for e in range(num_experts):
            h = x @ w1[e]
            a, g = jnp.split(h, 2, axis=1)
            y = jax.nn.silu(a) * g @ w2[e]
            out = jnp.where((max_ind == e)[:, None], y, out)
        out = out * max_prob
        return out.reshape(b, s, d)

    def _L1_xattn_ref(x, latents, gamma_x, beta_x, gamma_l, beta_l, Wq, Wkv, Wo):
        import jax, jax.numpy as jnp
        import numpy as np
        DIM = 256
        HEAD_DIM = 64
        NUM_HEADS = 8
        INNER = HEAD_DIM * NUM_HEADS
        ROT_DIM = HEAD_DIM
        ROPE_BASE = 10000.0
        EPS = 1e-05

        def layer_norm(x, g, b):
            mu = jnp.mean(x, axis=-1, keepdims=True)
            var = jnp.var(x, axis=-1, keepdims=True)
            return (x - mu) * jax.lax.rsqrt(var + EPS) * g + b

        def rope_rotate_k(k):
            n = k.shape[1]
            half = ROT_DIM // 2
            inv_freq = 1.0 / ROPE_BASE ** (jnp.arange(0, ROT_DIM, 2, dtype=jnp.float32) / ROT_DIM)
            theta = jnp.arange(n, dtype=jnp.float32)[:, None] * inv_freq[None, :]
            angles = jnp.concatenate([theta, theta], axis=-1)
            cos = jnp.cos(angles)[None, :, None, :].astype(k.dtype)
            sin = jnp.sin(angles)[None, :, None, :].astype(k.dtype)
            k_rope, k_pass = (k[..., :ROT_DIM], k[..., ROT_DIM:])
            neg_half = jnp.concatenate([-k_rope[..., half:], k_rope[..., :half]], axis=-1)
            k_rope = k_rope * cos + neg_half * sin
            return jnp.concatenate([k_rope, k_pass], axis=-1)
        b, n, _ = x.shape
        m = latents.shape[1]
        h, d = (NUM_HEADS, HEAD_DIM)
        scale = d ** (-0.5)
        xn = layer_norm(x, gamma_x, beta_x)
        ln = layer_norm(latents, gamma_l, beta_l)
        q = (ln @ Wq).reshape(b, m, h, d)
        kv_x = xn @ Wkv
        k_x, v_x = (kv_x[..., :INNER], kv_x[..., INNER:])
        kv_l = ln @ Wkv
        k_l, v_l = (kv_l[..., :INNER], kv_l[..., INNER:])
        k_x = k_x.reshape(b, n, h, d)
        v_x = v_x.reshape(b, n, h, d)
        k_x = rope_rotate_k(k_x)
        q = jnp.transpose(q, (0, 2, 1, 3)) * scale
        k_x = jnp.transpose(k_x, (0, 2, 1, 3))
        v_x = jnp.transpose(v_x, (0, 2, 1, 3))
        k_l = jnp.transpose(k_l.reshape(b, m, h, d), (0, 2, 1, 3))
        v_l = jnp.transpose(v_l.reshape(b, m, h, d), (0, 2, 1, 3))
        k = jnp.concatenate([k_x, k_l], axis=2)
        v = jnp.concatenate([v_x, v_l], axis=2)
        sim = jnp.einsum('bhid,bhjd->bhij', q, k)
        attn = jax.nn.softmax(sim, axis=-1)
        out = jnp.einsum('bhij,bhjd->bhid', attn, v)
        out = jnp.transpose(out, (0, 2, 1, 3)).reshape(b, m, INNER)
        return out @ Wo

    def _L1_ffn_ref(hidden_states, router_w, expert_gate, expert_up, expert_down, shared_gate, shared_up, shared_down):
        import jax, jax.numpy as jnp
        import numpy as np
        S, B, D, FF, E = (256, 2, 256, 512, 8)
        seq, bs, d = hidden_states.shape
        n_experts = expert_gate.shape[0]
        x = hidden_states.reshape(-1, d)
        logits = jnp.einsum('td,ed->te', x, router_w)
        top_logit = jnp.max(logits, axis=-1)
        top_idx = jnp.argmax(logits, axis=-1)
        score = jax.nn.sigmoid(top_logit)
        onehot = jax.nn.one_hot(top_idx, n_experts, dtype=x.dtype)
        xs = x * score[:, None]
        g = jnp.einsum('td,edf->etf', xs, expert_gate)
        u = jnp.einsum('td,edf->etf', xs, expert_up)
        h = jax.nn.silu(g) * u
        eo = jnp.einsum('etf,efd->etd', h, expert_down)
        moe_out = jnp.einsum('te,etd->td', onehot, eo)
        sh = jax.nn.silu(x @ shared_gate) * (x @ shared_up) @ shared_down
        return (moe_out + sh).reshape(seq, bs, d)

    def _L2_xattn_ref(x, context, Wq, bq, Wkv, bkv, Wp, bp):
        import jax, jax.numpy as jnp
        import numpy as np
        N_EMBD = 256
        N_HEAD = 16
        HEAD_DIM = N_EMBD // N_HEAD
        B, T, C = x.shape
        T_ctx = context.shape[1]
        H, D = (N_HEAD, C // N_HEAD)
        q = (x @ Wq + bq).reshape(B, T, H, D).transpose(0, 2, 1, 3)
        kv = context @ Wkv + bkv
        k, v = jnp.split(kv, 2, axis=-1)
        k = k.reshape(B, T_ctx, H, D).transpose(0, 2, 1, 3)
        v = v.reshape(B, T_ctx, H, D).transpose(0, 2, 1, 3)
        att = jnp.einsum('bhtd,bhsd->bhts', q, k) * (1.0 / jnp.sqrt(jnp.asarray(D, q.dtype)))
        causal = jnp.arange(T)[:, None] >= jnp.arange(T_ctx)[None, :]
        att = jnp.where(causal[None, None], att, jnp.asarray(-jnp.inf, att.dtype))
        att = jax.nn.softmax(att, axis=-1)
        y = jnp.einsum('bhts,bhsd->bhtd', att, v)
        y = y.transpose(0, 2, 1, 3).reshape(B, T, C)
        return y @ Wp + bp

    def _L2_ffn_ref(x, gate_w, w1, w2):
        import jax, jax.numpy as jnp
        import numpy as np
        D_MODEL = 256
        NUM_EXPERTS = 8
        TOP_K = 2
        gate_logits = jnp.einsum('bsd,ed->bse', x, gate_w)
        top_v, top_i = jax.lax.top_k(gate_logits, TOP_K)
        gates = jax.nn.softmax(top_v, axis=-1)
        combine = jnp.sum(jax.nn.one_hot(top_i, NUM_EXPERTS, dtype=x.dtype) * gates[..., None], axis=-2)
        out = jnp.zeros_like(x)
        for e in range(NUM_EXPERTS):
            h = jax.nn.relu(jnp.einsum('bsd,fd->bsf', x, w1[e]))
            y = jnp.einsum('bsf,df->bsd', h, w2[e])
            out = out + combine[..., e, None] * y
        return out

    def _L3_xattn_ref(x, context, Wq, Wkv, Wo, bo):
        import jax, jax.numpy as jnp
        import numpy as np
        NUM_HEADS = 16

        def _rope_tables(seq_len, head_dim, dtype):
            inv_freq = 1.0 / 10000.0 ** (jnp.arange(0, head_dim, 2, dtype=jnp.float32) / head_dim)
            freqs = jnp.arange(seq_len, dtype=jnp.float32)[:, None] * inv_freq[None, :]
            emb = jnp.concatenate([freqs, freqs], axis=-1)
            return (jnp.cos(emb).astype(dtype), jnp.sin(emb).astype(dtype))

        def _rotate_half(t):
            d = t.shape[-1] // 2
            return jnp.concatenate([-t[..., d:], t[..., :d]], axis=-1)

        def _apply_rope(t):
            cos, sin = _rope_tables(t.shape[2], t.shape[3], t.dtype)
            return t * cos[None, None] + _rotate_half(t) * sin[None, None]

        def _forward(x, context, Wq, Wkv, Wo, bo):
            B, Nq, C = x.shape
            Nkv = context.shape[1]
            H = NUM_HEADS
            hd = C // H
            scale = hd ** (-0.5)
            q = (x @ Wq).reshape(B, Nq, H, hd).transpose(0, 2, 1, 3)
            kv = (context @ Wkv).reshape(B, Nkv, 2, H, hd).transpose(2, 0, 3, 1, 4)
            k, v = (kv[0], kv[1])
            q = _apply_rope(q)
            k = _apply_rope(k)
            attn = jnp.einsum('bhqd,bhkd->bhqk', q, k) * scale
            attn = jax.nn.softmax(attn, axis=-1)
            out = jnp.einsum('bhqk,bhkd->bhqd', attn, v)
            out = out.transpose(0, 2, 1, 3).reshape(B, Nq, C)
            return out @ Wo + bo
        return _forward(x, context, Wq, Wkv, Wo, bo)

    def _L3_ffn_ref(s, W_in, in_norm_w, Wr, expert_bias, Wg, Wu, Wd, enorm_w, out_norm_w, W_out):
        import jax, jax.numpy as jnp
        import numpy as np
        EPS = float(jnp.finfo(jnp.float32).eps)
        TOP_K = 2

        def rmsnorm(x, w):
            return x * jax.lax.rsqrt(jnp.mean(x * x, axis=-1, keepdims=True) + EPS) * w
        B, T, _ = s.shape
        x = s.reshape(B * T, -1)
        h = rmsnorm(x @ W_in.T, in_norm_w)
        logits = h @ Wr.T
        _, idx = jax.lax.top_k(logits + expert_bias, TOP_K)
        sel = jnp.take_along_axis(logits, idx, axis=-1)
        g_topk = jax.nn.softmax(sel, axis=-1)
        N = logits.shape[0]
        gates = jnp.zeros_like(logits).at[jnp.arange(N)[:, None], idx].set(g_topk)
        out = jnp.zeros_like(h)
        for e in range(Wg.shape[0]):
            gate = jax.nn.silu(h @ Wg[e].T)
            up = h @ Wu[e].T
            oe = rmsnorm(gate * up @ Wd[e].T, enorm_w[e])
            out = out + gates[:, e:e + 1] * oe
        s_hat = rmsnorm(out, out_norm_w) @ W_out.T
        return s_hat.reshape(B, T, -1)
    x = x + _L0_xattn_ref(_layernorm(x, axis=-1), ctx_1024, L0_xattn_cos, L0_xattn_sin, L0_xattn_ln_lat_g, L0_xattn_ln_lat_b, L0_xattn_ln_ctx_g, L0_xattn_ln_ctx_b, L0_xattn_Wq, L0_xattn_Wkv, L0_xattn_Wo, L0_xattn_bo)
    x = x + _L0_ffn_ref(_layernorm(x, axis=-1), L0_ffn_router_w, L0_ffn_router_b, L0_ffn_w1, L0_ffn_w2)
    x = x + _L1_xattn_ref(ctx_1024, _layernorm(x, axis=-1), L1_xattn_gamma_x, L1_xattn_beta_x, L1_xattn_gamma_l, L1_xattn_beta_l, L1_xattn_Wq, L1_xattn_Wkv, L1_xattn_Wo)
    x = x + _L1_ffn_ref(_layernorm(x, axis=-1), L1_ffn_router_w, L1_ffn_expert_gate, L1_ffn_expert_up, L1_ffn_expert_down, L1_ffn_shared_gate, L1_ffn_shared_up, L1_ffn_shared_down)
    x = x + _L2_xattn_ref(_layernorm(x, axis=-1), ctx_1024, L2_xattn_Wq, L2_xattn_bq, L2_xattn_Wkv, L2_xattn_bkv, L2_xattn_Wp, L2_xattn_bp)
    x = x + _L2_ffn_ref(_layernorm(x, axis=-1), L2_ffn_gate_w, L2_ffn_w1, L2_ffn_w2)
    x = x + _L3_xattn_ref(_layernorm(x, axis=-1), ctx_1024, L3_xattn_Wq, L3_xattn_Wkv, L3_xattn_Wo, L3_xattn_bo)
    x = x + _L3_ffn_ref(_layernorm(x, axis=-1), L3_ffn_W_in, L3_ffn_in_norm_w, L3_ffn_Wr, L3_ffn_expert_bias, L3_ffn_Wg, L3_ffn_Wu, L3_ffn_Wd, L3_ffn_enorm_w, L3_ffn_out_norm_w, L3_ffn_W_out)
    return x

_drawn_inputs = setup_inputs


def setup_inputs(seed=0):
    import zlib

    import numpy as np

    out = dict(_drawn_inputs(seed))
    spreads = {'L0_xattn_ln_lat_g': (1.0, 0.2),
     'L0_xattn_ln_lat_b': (0.0, 0.302),
     'L0_xattn_ln_ctx_g': (1.0, 0.2),
     'L0_xattn_ln_ctx_b': (0.0, 0.1),
     'L0_xattn_bo': (0.0, 0.1),
     'L0_ffn_router_b': (0.0, 0.8),
     'L1_xattn_gamma_x': (1.0, 0.2),
     'L1_xattn_beta_x': (0.0, 0.1),
     'L1_xattn_gamma_l': (1.0, 0.2),
     'L1_xattn_beta_l': (0.0, 0.1),
     'L2_xattn_bq': (0.0, 0.366),
     'L2_xattn_bkv': (0.0, 0.1),
     'L2_xattn_bp': (0.0, 0.1),
     'L3_xattn_bo': (0.0, 0.1),
     'L3_ffn_in_norm_w': (1.0, 0.2),
     'L3_ffn_expert_bias': (0.0, 0.1),
     'L3_ffn_enorm_w': (1.0, 0.539),
     'L3_ffn_out_norm_w': (1.0, 0.2)}
    factors = {'L0_xattn_cos': 3.035,
     'L0_xattn_sin': 3.037,
     'L0_ffn_router_w': 3.703,
     'L0_ffn_w1': 3.692,
     'L0_ffn_w2': 3.675,
     'L1_ffn_router_w': 3.279,
     'L1_ffn_expert_gate': 3.435,
     'L1_ffn_expert_up': 3.759,
     'L1_ffn_expert_down': 3.446,
     'L1_ffn_shared_gate': 3.033,
     'L1_ffn_shared_up': 2.864,
     'L1_ffn_shared_down': 3.085}
    for name, (base, spread) in spreads.items():
        noise = np.random.default_rng([zlib.crc32(name.encode()), seed]).standard_normal(out[name].shape)
        drawn = base * np.exp(spread * noise) if base else spread * noise
        out[name] = jnp.asarray(drawn.astype(out[name].dtype))
    for name, factor in factors.items():
        out[name] = (out[name] * factor).astype(out[name].dtype)
    return out
```

```python
from contextlib import ExitStack

import numpy as np

import concourse.bass as bass
from concourse import mybir

F32 = mybir.dt.float32
ALU = mybir.AluOpType
ACT = mybir.ActivationFunctionType
AX = mybir.AxisListType

P = 128
D = 256
NT = 8
B = 2
EPS = 1e-5
EPS3 = float(np.finfo(np.float32).eps)
CLIP_LO = float(np.exp(np.float64(-11.0)))
CLIP_HI = float(np.exp(np.float64(11.0)))
NEG = -1e30


class Tok:

    __slots__ = ("key", "n", "used")

    def __init__(self, key, n):
        self.key, self.n, self.used = key, n, False


class Queues:

    ENGINES = ("tensor", "vector", "scalar", "gpsimd", "sync")

    def __init__(self, nc, ctx):
        self.nc, self.ctx = nc, ctx
        self.ops = {e: [] for e in self.ENGINES}
        self.sems, self.counts = {}, {}

    def add(self, eng, fn, waits):
        t = Tok(eng, len(self.ops[eng]))
        flat = [w for w in waits if w is not None]
        for w in flat:
            w.used = True
        self.ops[eng].append((fn, flat, t, None))
        return t

    def dma(self, name, fn, waits, eng="sync"):
        self.counts[name] = self.counts.get(name, 0) + 16
        t = Tok("d_" + name, self.counts[name])
        flat = [w for w in waits if w is not None]
        for w in flat:
            w.used = True
        self.ops[eng].append((fn, flat, None, "d_" + name))
        return t

    def sem(self, key):
        if key not in self.sems:
            self.sems[key] = self.ctx.enter_context(self.nc.semaphore("s_" + key))
        return self.sems[key]

    def emit(self):
        for e in self.ENGINES:
            n = 0
            for _, _, t, d in self.ops[e]:
                if t is not None and t.used:
                    n += 1
                    t.n = n
            self.sem(e)
            for _, _, _, d in self.ops[e]:
                if d:
                    self.sem(d)
        block = self.ctx.enter_context(self.nc.Block())
        for e in self.ENGINES:
            into = {"tensor": block.tensor, "vector": block.vector, "scalar": block.scalar,
                            "gpsimd": block.gpsimd, "sync": block.sync}[e]
            into(self.body(e))

    def body(self, e):
        def run(eng):
            known = {}
            for fn, waits, t, d in self.ops[e]:
                need = {}
                for w in waits:
                    need[w.key] = max(need.get(w.key, 0), w.n)
                for key, v in need.items():
                    if known.get(key, 0) < v:
                        eng.wait_ge(self.sem(key), v)
                        known[key] = v
                ins = fn(eng)
                if d:
                    ins.then_inc(self.sem(d), 16)
                elif t.used:
                    ins.then_inc(self.sem(e), 1)
        return run


class Ring:

    def __init__(self, bufs):
        self.bufs, self.rel, self.n = bufs, [[] for _ in bufs], 0

    def get(self):
        i = self.n % len(self.bufs)
        self.n += 1
        return self.bufs[i], self.rel[i], i

    def done(self, i, *toks):
        self.rel[i] = list(toks)


def build(nc, T, OUT, stop=99):
    ctx = ExitStack()
    with ctx:
        q = Queues(nc, ctx)
        AR = ctx.enter_context(nc.sbuf_tensor("arena", [P, 51968], F32))
        PS = ctx.enter_context(nc.psum_tensor("psum", [P, 4096], F32))

        def pe(fn, *w):
            return q.add("tensor", fn, w)

        def dve(fn, *w):
            return q.add("vector", fn, w)

        def act(fn, *w):
            return q.add("scalar", fn, w)

        pool_last = [None]

        def pool(fn, *w):
            pool_last[0] = q.add("gpsimd", fn, (pool_last[0],) + w)
            return pool_last[0]

        def load(name, dst, src, *w):
            return q.dma(name, lambda e: e.dma_start(dst, src), w)

        def view(off, cnt, pat=None, **kw):
            v = AR[:, off:off + cnt]
            return v.rearrange(pat, **kw) if pat else v

        def bank(i, n=512):
            return PS[:, 512 * i:512 * i + n]

        RA = Ring([PS[:, 0:1024], PS[:, 1024:2048]])
        RB = Ring([bank(i) for i in range(4, 8)])

        X = view(0, 2048, "p (t d) -> p t d", d=D)
        XN = view(2048, 2048, "p (t d) -> p t d", d=D)
        XNT = view(4096, 2048, "p (k n) -> p k n", k=2)
        ID = view(6144, 128)
        at = [6272]

        def small(cnt, pat=None, **kw):
            at[0] += cnt
            assert at[0] <= 7168
            return view(at[0] - cnt, cnt, pat, **kw)

        VEC = small(T["vec"].shape[1])
        ST = small(96, "p (t s) -> p t s", s=6)
        MV = small(32, "p (t s) -> p t s", s=2)
        VE = small(16)
        RS = small(16)
        MHALF = small(16)
        LG = small(64, "p (t e) -> p t e", e=8)
        LB = small(64, "p (t e) -> p t e", e=8)
        OH1 = small(64, "p (t e) -> p t e", e=8)
        OH2 = small(64, "p (t e) -> p t e", e=8)
        GATE = small(64, "p (t e) -> p t e", e=8)
        REV = small(64, "p (t e) -> p t e", e=8)
        RT = small(64, "p (s t) -> p s t", t=8)
        MS = small(16, "p (r t) -> p r t", t=4)
        GR = small(16, "p (r t) -> p r t", t=4)
        HAT = view(7168, 4096, "p (k n) -> p k n", k=2)

        xin = T["x"].rearrange("b (t p) d -> p (b t) d", p=P)
        t_x = load("x", X, xin)
        t_vec = load("vec", VEC, T["vec"])
        CTX = view(20000, 4096, "p (t d) -> p t d", d=D)
        t_ctx = load("ctx", CTX, T["ctx"].rearrange("b (t p) d -> p (b t) d", p=P))
        t_rev = load("rev", REV.rearrange("p t e -> p (t e)"), T["rev"])
        t = pool(lambda e: e.memset(ID, 0.0))
        t_id = pool(lambda e: e.affine_select(out=ID, in_=ID, compare_op=ALU.not_equal, fill=1.0, base=0,
                                              pattern=[[-1, P]], channel_multiplier=1), t)
        t_mh = pool(lambda e: e.memset(MHALF, -0.5))

        xt = [t_x] * NT

        def norm(src, dst, n, eps, src_t, free):
            for i in range(n):
                a = dve(lambda e, i=i: e.bn_stats(ST[:, i, :], src[:, i, :]), src_t[i], *free)
            for i in range(n):
                a = dve(lambda e, i=i: e.bn_aggr(MV[:, i, :], ST[:, i, :]), a if i == 0 else None)
            b = pool(lambda e: e.tensor_scalar(VE[:, 0:n], MV[:, 0:n, 1], eps, None, ALU.add), a)
            b = pool(lambda e: e.tensor_tensor(RS[:, 0:n], VE[:, 0:n], MHALF[:, 0:n], ALU.pow), b, t_mh)
            out = []
            for i in range(n):
                out.append(dve(lambda e, i=i: e.tensor_scalar(dst[:, i, :], src[:, i, :], MV[:, i, 0:1],
                                                              RS[:, i:i + 1], ALU.subtract, ALU.mult), a, b))
            return out

        def turn(src, dst, n, src_t, free, gain=None):
            out = []
            for c in range(n // 4):
                for k in range(2):
                    s, w, r = RB.get()
                    for j in range(4):
                        i = 4 * c + j
                        m = pe(lambda e, s=s, i=i, j=j, k=k: e.transpose(
                            s[:, 128 * j:128 * j + 128], src[:, i, 128 * k:128 * k + 128], ID),
                            src_t[i], t_id, *w)
                    d = dst[:, k, 512 * c:512 * c + 512]
                    if gain:
                        o = dve(lambda e, d=d, s=s, k=k: e.tensor_scalar(
                            d, s, gain[0][:, k:k + 1], gain[1][:, k:k + 1], ALU.mult, ALU.add), m, t_vec, *free)
                    elif k == 0:
                        o = act(lambda e, d=d, s=s: e.activation(d, s, ACT.Copy), m, *free)
                    else:
                        o = dve(lambda e, d=d, s=s: e.tensor_copy(d, s), m, *free)
                    RB.done(r, o)
                    out.append(o)
            last_pe = m
            return out, last_pe

        def vec(i):
            return VEC[:, 2 * i:2 * i + 2]

        V_LATG, V_LATB, V_CTXG, V_CTXB, V_GX, V_BX, V_GL, V_BL = range(8)
        BQ = VEC[:, 16:20]
        BK = VEC[:, 20:24]
        SGN = VEC[:, 24:25]
        ONE16 = VEC[:, 25:26]

        G0 = 11264
        PT_OFF, OT_OFF, TAB_OFF, W_OFF = 36864, 40960, 43008, 46080
        TMP = [view(2048 + 1024 * i, 1024, "p (h n) -> p h n", h=2) for i in range(2)]

        def attention64(layer, lat_t, lat_free, ctx_t, CT, tab_t, w_free, g_free):
            own = layer == 1
            S = 1536 if own else 1024
            nk = S // P
            gsz = 4 * S + 2048 + nk * 384
            KT = [view(G0 + gsz * i, 4 * S, "p (h n) -> p h n", h=4) for i in range(2)]
            QT = [view(G0 + gsz * i + 4 * S, 2048, "p (h n) -> p h n", h=4) for i in range(2)]
            VA = [view(G0 + gsz * i + 4 * S + 2048, nk * 384, "p (t q c) -> p t q c", q=2, c=192)
                  for i in range(2)]
            PT = Ring([view(PT_OFF + 1024 * i, 1024, "p (a n) -> p a n", a=2) for i in range(4)])
            OT = [view(OT_OFF + 1024 * i, 1024, "p (q n) -> p q n", q=2) for i in range(2)]
            COS, SIN = view(TAB_OFF, 1024), view(TAB_OFF + 1024, 1024)
            W = [view(W_OFF + 2560 * i, 2560) for i in range(2)]
            TR = Ring(TMP)
            for i in range(2):
                TR.done(i, *lat_free)
            nhg = 2 if own else 4
            steps = [(hg, b) for hg in range(nhg) for b in range(B)]
            init = []
            for i in range(2):
                init.append(pool(lambda e, i=i: e.memset(KT[i][64:65, :, :], 1.0), *g_free))
                init.append(pool(lambda e, i=i: e.memset(VA[i][:, :, :, 64:128], 1.0), *g_free))
                init.append(pool(lambda e, i=i: e.memset(QT[i][64:65, :, :], 0.0), *g_free))
            w_t, w_rel = {}, {}
            grel = [list(g_free), list(g_free)]
            gtok = {}
            otrel = [list(g_free), list(g_free)]
            negm = {}

            def wload(hg):
                w_t[hg] = load(f"wa{hg % 2}", W[hg % 2], T[f"l{layer}_w"][hg], *(w_free if hg < 2 else w_rel[hg - 2]))

            wload(0)
            if nhg > 1:
                wload(1)

            def wsl(hg, j):
                return W[hg % 2][:, 512 * j:512 * j + 512].rearrange("p (k n) -> p k n", k=2)

            def proj(n):
                hg, b = steps[n]
                i = n % 2
                toks = list(init)
                wt = w_t[hg]
                for p in range(2):
                    s, w, r = RB.get()
                    for k in range(2):
                        m = pe(lambda e, s=s, k=k, p=p: e.matmul(
                            s, wsl(hg, 0)[:, k, 128 * p:128 * p + 128], XNT[:, k, 512 * b:512 * b + 512],
                            start=(k == 0), stop=(k == 1)), wt, *lat_t, *w)
                    for h in range(2):
                        o = act(lambda e, s=s, h=h, p=p: e.activation(
                            QT[i][0:64, 2 * p + h, :], s[64 * h:64 * h + 64, :], ACT.Copy), m, *grel[i])
                    RB.done(r, o)
                toks.append(o)
                for p in range(2):
                    for c in range(2):
                        s, w, r = RA.get()
                        for j in range(2):
                            for k in range(2):
                                m = pe(lambda e, s=s, k=k, p=p, c=c, j=j: e.matmul(
                                    s[:, 512 * j:512 * j + 512], wsl(hg, 1 + j)[:, k, 128 * p:128 * p + 128],
                                    CT[:, k, 1024 * b + 512 * c:1024 * b + 512 * c + 512],
                                    start=(k == 0), stop=(k == 1)), wt, *ctx_t, *w)
                        tm, tw, tr = TR.get()
                        a1 = dve(lambda e, s=s, tm=tm, c=c: e.tensor_tensor(
                            tm[:, 0, :], s[:, 0:512], COS[:, 512 * c:512 * c + 512], ALU.mult), m, *tab_t, *tw)
                        a2 = dve(lambda e, s=s, tm=tm, c=c: e.tensor_tensor(
                            tm[:, 1, :], s[:, 512:1024], SIN[:, 512 * c:512 * c + 512], ALU.mult), m)
                        RA.done(r, a2)
                        o1 = pool(lambda e, tm=tm, p=p, c=c: e.tensor_tensor(
                            KT[i][0:64, 2 * p, 512 * c:512 * c + 512], tm[0:64, 0, :], tm[0:64, 1, :], ALU.add),
                            a2, *grel[i])
                        o2 = dve(lambda e, tm=tm, p=p, c=c: e.tensor_tensor(
                            KT[i][0:64, 2 * p + 1, 512 * c:512 * c + 512], tm[64:128, 0, :], tm[64:128, 1, :],
                            ALU.add), a2, *grel[i])
                        TR.done(tr, o1, o2)
                    if own:
                        s, w, r = RB.get()
                        for k in range(2):
                            m = pe(lambda e, s=s, k=k, p=p: e.matmul(
                                s, wsl(hg, 1)[:, k, 128 * p:128 * p + 128], XNT[:, k, 512 * b:512 * b + 512],
                                start=(k == 0), stop=(k == 1)), wt, *w)
                        for h in range(2):
                            o = act(lambda e, s=s, h=h, p=p: e.activation(
                                KT[i][0:64, 2 * p + h, 1024:1536], s[64 * h:64 * h + 64, :], ACT.Copy), m, *grel[i])
                        RB.done(r, o)
                        toks.append(o)
                toks += [o1, o2]
                for t in range(nk):
                    s, w, r = RB.get()
                    for k in range(2):
                        m = pe(lambda e, s=s, k=k, t=t: e.matmul(
                            s[:, 0:256],
                            CT[:, k, 1024 * b + 128 * t:1024 * b + 128 * t + 128] if t < 8 else
                            XNT[:, k, 512 * b + 128 * (t - 8):512 * b + 128 * (t - 8) + 128],
                            wsl(hg, 3)[:, k, :], start=(k == 0), stop=(k == 1)), wt, *w)
                    dst = VA[i][:, t].rearrange("p q (s c) -> p q s c", c=64)[:, :, 0:3:2, :]
                    src = s[:, 0:256].rearrange("p (q s c) -> p q s c", q=2, s=2)
                    o = act(lambda e, dst=dst, src=src: e.activation(dst, src, ACT.Copy), m, *grel[i])
                    RB.done(r, o)
                toks.append(o)
                gtok[n] = toks
                return m

            NM = [NMX[:, 0:16], NMX[:, 16:32]]
            MXC = NMX[:, 32:64].rearrange("p (x c) -> p x c", c=2)
            mrel = []

            def rowmax(n):
                nonlocal mrel
                i = n % 2
                for h in range(4):
                    for t in range(4):
                        for c, (k0, kn) in enumerate(((0, 1024), (1024, 512))):
                            s, w, r = RA.get()
                            for u in range(kn // 512):
                                m = pe(lambda e, s=s, h=h, t=t, u=u, k0=k0: e.matmul(
                                    s[:, 512 * u:512 * u + 512], QT[i][0:65, h, 128 * t:128 * t + 128],
                                    KT[i][0:65, h, k0 + 512 * u:k0 + 512 * u + 512], start=True, stop=True),
                                    *gtok[n], *w)
                            o = dve(lambda e, s=s, h=h, t=t, c=c, kn=kn: e.tensor_reduce(
                                MXC[:, 4 * h + t, c:c + 1], s[:, 0:kn], AX.X, ALU.max), m, *mrel)
                            RA.done(r, o)
                o = dve(lambda e: e.tensor_reduce(NM[i], MXC, AX.X, ALU.max, negate=True), o, *grel[i])
                mrel = [o]
                negm[n] = (o, m)

            def shift(n):
                i = n % 2
                t0, mlast = negm[n]
                for h in range(4):
                    s, w, r = RB.get()
                    for t in range(4):
                        m = pe(lambda e, s=s, h=h, t=t: e.matmul(
                            s[64:65, 128 * t:128 * t + 128], NM[i][:, 4 * h + t:4 * h + t + 1], ID,
                            start=True, stop=True), t0, t_id, *w)
                    o = act(lambda e, s=s, h=h: e.activation(QT[i][64:65, h, :], s[64:65, :], ACT.Copy), m, mlast)
                    RB.done(r, o)
                gtok[n] = gtok[n] + [o]

            def attend(n):
                hg, b = steps[n]
                i = n % 2
                if own:
                    shift(n)
                ot, otw = OT[i], otrel[i]
                work = [(h, kp) for h in range(4) for kp in range(nk // 2)]
                pend = []
                heads = {}
                ott = []

                def values():
                    h, kp, pt, tp, pr = pend.pop(0)
                    if kp == 0:
                        heads[h] = RB.get()
                    s, w, r = heads[h]
                    for a in range(2):
                        kt = 2 * kp + a
                        m = pe(lambda e, s=s, pt=pt, a=a, kt=kt, h=h: e.matmul(
                            s, VA[i][:, kt, h // 2, 64 * (h % 2):64 * (h % 2) + 128], pt[:, a, :],
                            start=(kt == 0), stop=(kt == nk - 1)), tp, *w)
                    PT.done(pr, m)
                    if kp == nk // 2 - 1:
                        lo, hi = 64 * (h % 2), 64 - 64 * (h % 2)
                        tm, tw, tr = TR.get()
                        o = dve(lambda e, s=s, tm=tm, lo=lo, hi=hi: e.reciprocal(
                            tm[lo:lo + 64, 0, :], s[hi:hi + 64, :]), m, *tw)
                        o = dve(lambda e, s=s, tm=tm, lo=lo, h=h: e.tensor_tensor(
                            ot[lo:lo + 64, h // 2, :], s[lo:lo + 64, :], tm[lo:lo + 64, 0, :], ALU.mult), o, *otw)
                        RB.done(r, o)
                        TR.done(tr, o)
                        ott.append(o)
                    return m

                for h, kp in work:
                    s, w, r = RA.get()
                    for a in range(2):
                        kt = 2 * kp + a
                        m = pe(lambda e, s=s, a=a, kt=kt, h=h: e.matmul(
                            s[:, 512 * a:512 * a + 512], KT[i][0:65, h, 128 * kt:128 * kt + 128],
                            QT[i][0:65, h, :], start=True, stop=True), *gtok[n], *w)
                    pt, pw, pr = PT.get()
                    tp = act(lambda e, s=s, pt=pt: e.activation(
                        pt.rearrange("p a n -> p (a n)"), s, ACT.Exp, scale=0.125), m, *pw)
                    RA.done(r, tp)
                    if not own:
                        tp = dve(lambda e, pt=pt: e.tensor_scalar(pt, pt, CLIP_LO, CLIP_HI, ALU.max, ALU.min), tp)
                    pend.append((h, kp, pt, tp, pr))
                    if len(pend) > 2:
                        values()
                while pend:
                    mv = values()
                if own:
                    z = pool(lambda e: e.memset(QT[i][64:65, :, :], 0.0), m)
                    grel[i] = [mv, z]
                else:
                    grel[i] = [mv]
                wo = W[hg % 2][:, 2048:2560].rearrange("p (q n) -> p q n", q=2)
                for t in range(4):
                    s, w, r = RB.get()
                    for p in range(2):
                        m = pe(lambda e, s=s, t=t, p=p: e.matmul(
                            s[:, 0:256], ot[:, p, 128 * t:128 * t + 128], wo[:, p, :],
                            start=(p == 0), stop=(p == 1)), w_t[hg], *ott, *w)
                    o = dve(lambda e, s=s, t=t, b=b: e.tensor_tensor(
                        X[:, 4 * b + t, :], X[:, 4 * b + t, :], s[:, 0:256], ALU.add), m, xt[4 * b + t])
                    xt[4 * b + t] = o
                    RB.done(r, o)
                otrel[i] = [m]
                if b == 1:
                    w_rel[hg] = [m]
                    if hg + 2 < nhg:
                        wload(hg + 2)
                return m

            for n in range(len(steps) + 1):
                if n < len(steps):
                    proj(n)
                    if own:
                        rowmax(n)
                if n >= 1:
                    last = attend(n - 1)
            return [last, xt[0], xt[7]] + grel[0] + grel[1]

        NMX = view(6144 + 1024 - 64, 64)
        assert at[0] <= 7104

        def attention16(layer, lat_t, lat_free, CT, ctx_t, free):
            causal = layer == 2
            S = 512 if causal else 1024
            nk = S // P
            o0 = 11264
            KT = view(o0, 4096, "p (q n) -> p q n", q=4)
            QB = view(o0 + 4096, 2048, "p (q n) -> p q n", q=4)
            QP = view(o0 + 6144, 8192, "p (h n) -> p h n", h=16)
            VA = view(o0 + 14336, 4096, "p (t h c) -> p t h c", h=16, c=32)
            PT = Ring([view(o0 + 18432 + 1024 * i, 1024) for i in range(4)])
            OT = view(o0 + 22528, 2048, "p (q n) -> p q n", q=4)
            OU = view(o0 + 24576, 1024, "p (u n) -> p u n", u=2)
            NMT = view(o0 + 25600, 2048, "p (t c) -> p t c", t=4)
            COS, SIN = view(o0 + 27648, 1024), view(o0 + 28672, 1024)
            W = view(o0 + 29696, 5632)
            wq, wqr, wk, wkr = [W[:, 1024 * j:1024 * j + 1024].rearrange("p (k n) -> p k n", k=2) for j in range(4)]
            wv = W[:, 4096:4608].rearrange("p (k n) -> p k n", k=2)
            wo = W[:, 4608:5632].rearrange("p (q n) -> p q n", q=4)
            BV = view(o0 + 35328, 256)
            TRI = view(o0 + 35584, 128)
            SEL = view(o0 + 35712, 128)
            MXC = view(o0 + 35840, 16, "p (t h) -> p t h", t=4)
            TR = Ring([view(2048 + 1024 * i, 1024, "p (h n) -> p h n", h=2) for i in range(2)])
            for i in range(2):
                TR.done(i, *lat_free)
            wt = load("w16", W, T[f"l{layer}_w"], *free)
            tt = load("tab", view(o0 + 27648, 2048), T["l3_tab"], *free)
            bt = load("bv", BV, T["bc"][:, 512:768], *free)
            st = load("sel", SEL, T["sel"], *free)
            z1 = pool(lambda e: e.memset(QP, 0.0), *free)
            z2 = pool(lambda e: e.memset(VA, 0.0), *free)
            z2 = pool(lambda e: e.memset(VA[:, :, :, 16:17], 1.0), z2)
            z3 = pool(lambda e: e.memset(NMT, 0.0), *free)
            z4 = pool(lambda e: e.memset(TRI, 0.0), *free)
            z4 = pool(lambda e: e.affine_select(out=TRI, in_=TRI, compare_op=ALU.is_ge, fill=NEG, base=0,
                                                pattern=[[-1, P]], channel_multiplier=1), z4)
            brel = list(free)
            orel = list(free)

            for b in range(B):
                for g in range(4):
                    for c in range(S // 512):
                        s, w, r = RA.get()
                        for j in range(1 if causal else 2):
                            for k in range(2):
                                m = pe(lambda e, s=s, g=g, c=c, j=j, k=k, b=b: e.matmul(
                                    s[:, 512 * j:512 * j + 512], (wk, wkr)[j][:, k, 128 * g:128 * g + 128],
                                    CT[:, k, 1024 * b + 512 * c:1024 * b + 512 * c + 512],
                                    start=(k == 0), stop=(k == 1)), wt, *ctx_t, *w)
                        dst = KT[:, g, 512 * c:512 * c + 512]
                        if causal:
                            ko = dve(lambda e, s=s, dst=dst, g=g: e.tensor_scalar(
                                dst, s[:, 0:512], BK[:, g:g + 1], None, ALU.add), m, t_vec, *brel)
                            RA.done(r, ko)
                        else:
                            tm, tw, tr = TR.get()
                            a1 = dve(lambda e, s=s, tm=tm, c=c: e.tensor_tensor(
                                tm[:, 0, :], s[:, 0:512], COS[:, 512 * c:512 * c + 512], ALU.mult), m, tt, *tw)
                            a2 = dve(lambda e, s=s, tm=tm, c=c: e.tensor_tensor(
                                tm[:, 1, :], s[:, 512:1024], SIN[:, 512 * c:512 * c + 512], ALU.mult), m)
                            RA.done(r, a2)
                            ko = dve(lambda e, tm=tm, dst=dst: e.scalar_tensor_tensor(
                                out=dst, in0=tm[:, 0, :], scalar=ONE16, in1=tm[:, 1, :], op0=ALU.add,
                                op1=ALU.add), a2, t_vec, *brel)
                            TR.done(tr, ko)
                for g in range(4):
                    s, w, r = RA.get()
                    for j in range(1 if causal else 2):
                        for k in range(2):
                            m = pe(lambda e, s=s, g=g, j=j, k=k, b=b: e.matmul(
                                s[:, 512 * j:512 * j + 512], (wq, wqr)[j][:, k, 128 * g:128 * g + 128],
                                XNT[:, k, 512 * b:512 * b + 512], start=(k == 0), stop=(k == 1)), wt, *lat_t, *w)
                    if causal:
                        qo = dve(lambda e, s=s, g=g: e.tensor_scalar(
                            QB[:, g, :], s[:, 0:512], BQ[:, g:g + 1], None, ALU.add), m, t_vec, *brel)
                        RA.done(r, qo)
                    else:
                        tm, tw, tr = TR.get()
                        a1 = dve(lambda e, s=s, tm=tm: e.tensor_tensor(
                            tm[:, 0, :], s[:, 0:512], COS[:, 0:512], ALU.mult), m, tt, *tw)
                        a2 = dve(lambda e, s=s, tm=tm: e.tensor_tensor(
                            tm[:, 1, :], s[:, 512:1024], SIN[:, 0:512], ALU.mult), m)
                        RA.done(r, a2)
                        qo = dve(lambda e, tm=tm, g=g: e.tensor_tensor(
                            QB[:, g, :], tm[:, 0, :], tm[:, 1, :], ALU.add), a2, *brel)
                        TR.done(tr, qo)
                    for j in range(4):
                        qp = pool(lambda e, g=g, j=j: e.tensor_copy(
                            QP[32 * j:32 * j + 32, 4 * g + j, :], QB[32 * j:32 * j + 32, g, :]), qo, z1, *brel)
                for t in range(nk):
                    s, w, r = RB.get()
                    for k in range(2):
                        m = pe(lambda e, s=s, t=t, k=k, b=b: e.matmul(
                            s[:, 0:256], CT[:, k, 1024 * b + 128 * t:1024 * b + 128 * t + 128], wv[:, k, :],
                            start=(k == 0), stop=(k == 1)), wt, *w)
                    dst = VA[:, t, :, 0:16]
                    src = s[:, 0:256].rearrange("p (h c) -> p h c", c=16)
                    if causal:
                        vo = dve(lambda e, dst=dst, src=src: e.tensor_tensor(
                            dst, src, BV.rearrange("p (h c) -> p h c", c=16), ALU.add), m, bt, z2, *brel)
                    else:
                        vo = act(lambda e, dst=dst, src=src: e.activation(dst, src, ACT.Copy), m, z2, *brel)
                    RB.done(r, vo)

                ready = {}

                def rowmax(g):
                    nonlocal mrel
                    for j in range(4):
                        h = 4 * g + j
                        for t in range(4):
                            kn = 128 * (t + 1) if causal else 1024
                            s, w, r = RA.get()
                            for u in range(0, kn, 512):
                                n = min(512, kn - u)
                                m = pe(lambda e, s=s, h=h, g=g, t=t, u=u, n=n: e.matmul(
                                    s[:, u:u + n], QP[:, h, 128 * t:128 * t + 128], KT[:, g, u:u + n],
                                    start=True, stop=True), qp, ko, *w)
                            if causal:
                                o = dve(lambda e, s=s, t=t: e.tensor_tensor(
                                    s[:, 128 * t:128 * t + 128], s[:, 128 * t:128 * t + 128], TRI, ALU.add), m, z4)
                                o = dve(lambda e, s=s, t=t, j=j, g=g, kn=kn: e.tensor_reduce(
                                    NMT[:, t, 128 * g + 32 * j + 16:128 * g + 32 * j + 17], s[:, 0:kn], AX.X,
                                    ALU.max, negate=True), o, z3, *brel)
                            else:
                                o = dve(lambda e, s=s, t=t, j=j, g=g, kn=kn: e.tensor_reduce(
                                    NMT[:, t, 128 * g + 32 * j + 16:128 * g + 32 * j + 17], s[:, 0:kn], AX.X,
                                    ALU.max, negate=True), m, z3, *brel)
                            RA.done(r, o)
                    ready[g] = (o, m)

                def shift(g):
                    o, mlast = ready[g]
                    s, w, r = RB.get()
                    for t in range(4):
                        m = pe(lambda e, s=s, g=g, t=t: e.matmul(
                            s[:, 128 * t:128 * t + 128], NMT[:, t, 128 * g:128 * g + 128], ID,
                            start=True, stop=True), o, t_id, *w)
                    for j in range(4):
                        o = dve(lambda e, s=s, g=g, j=j: e.tensor_tensor(
                            QP[32 * j:32 * j + 32, 4 * g + j, :], s[32 * j:32 * j + 32, :],
                            QB[32 * j:32 * j + 32, g, :], ALU.add), m, mlast)
                    RB.done(r, o)
                    ready[g] = o

                mrel = []
                oto = []

                def attend(g):
                    nonlocal orel
                    qs = ready[g]
                    so, sw, sr = RB.get()
                    pend = []

                    def values():
                        j, kts, pt, tp, pr = pend.pop(0)
                        for a, kt in enumerate(kts):
                            q0 = 128 * kt if causal else 0
                            m = pe(lambda e, j=j, kt=kt, a=a, pt=pt, q0=q0: e.matmul(
                                so[32 * j:32 * j + 32, q0:512], VA[:, kt, 4 * g + j, :],
                                pt[:, 512 * a + q0:512 * a + 512], start=(kt == 0), stop=(kt == nk - 1),
                                skip_group_check=True), tp, vo, *sw)
                        PT.done(pr, m)
                        return m

                    for j in range(4):
                        for kp in range(nk // 2):
                            kts = (2 * kp, 2 * kp + 1)
                            s, w, r = RA.get()
                            for a, kt in enumerate(kts):
                                q0 = 128 * kt if causal else 0
                                m = pe(lambda e, s=s, a=a, kt=kt, j=j, q0=q0: e.matmul(
                                    s[:, 512 * a + q0:512 * a + 512], KT[:, g, 128 * kt:128 * kt + 128],
                                    QP[:, 4 * g + j, q0:512], start=True, stop=True), qs, *w)
                            pt, pw, pr = PT.get()
                            if causal:
                                for a, kt in enumerate(kts):
                                    lo, hi = 512 * a + 128 * kt, 512 * a + 512
                                    tp = act(lambda e, s=s, pt=pt, lo=lo, hi=hi: e.activation(
                                        pt[:, lo:hi], s[:, lo:hi], ACT.Exp, scale=0.25), m, *pw)
                                RA.done(r, tp)
                                for a, kt in enumerate(kts):
                                    lo = 512 * a + 128 * kt
                                    d = pt[:, lo:lo + 128]
                                    tg = pool(lambda e, d=d: e.affine_select(
                                        out=d, in_=d, compare_op=ALU.is_ge, fill=0.0, base=0,
                                        pattern=[[1, P]], channel_multiplier=-1), tp)
                                tp = tg
                            else:
                                tp = act(lambda e, s=s, pt=pt: e.activation(pt, s, ACT.Exp, scale=0.25), m, *pw)
                                RA.done(r, tp)
                            pend.append((j, kts, pt, tp, pr))
                            if len(pend) > 2:
                                values()
                    while pend:
                        m = values()
                    ou = OU[:, 0, :]
                    c1 = act(lambda e: e.activation(ou, so, ACT.Copy), m, *orel)
                    RB.done(sr, c1)
                    s, w, r = RB.get()
                    m2 = pe(lambda e, s=s: e.matmul(s, SEL, ou, start=True, stop=True), c1, st, *w)
                    o = dve(lambda e, s=s: e.reciprocal(OU[:, 1, :], s), m2, *orel)
                    RB.done(r, o)
                    o = dve(lambda e, g=g: e.tensor_tensor(OT[:, g, :], ou, OU[:, 1, :], ALU.mult), o, c1, *brel)
                    orel = [m2, o]
                    oto.append(o)
                    return m

                rowmax(0)
                for g in range(4):
                    if g + 1 < 4:
                        rowmax(g + 1)
                    shift(g)
                    m = attend(g)
                for t in range(4):
                    s, w, r = RB.get()
                    for g in range(4):
                        m = pe(lambda e, s=s, t=t, g=g: e.matmul(
                            s[:, 0:256], OT[:, g, 128 * t:128 * t + 128], wo[:, g, :],
                            start=(g == 0), stop=(g == 3)), wt, *oto, *w)
                    i = 4 * b + t
                    o = dve(lambda e, s=s, i=i: e.tensor_tensor(
                        X[:, i, :], X[:, i, :], s[:, 0:256], ALU.add), m, xt[i])
                    xt[i] = o
                    RB.done(r, o)
                brel = [m, o]
            return [m, o]

        def bc(ap):
            return ap.unsqueeze(2).to_broadcast([P, NT, 8])

        def logits(src, wt_ap, wt, src_t, bias=None, bias_t=None):
            s, w, r = RB.get()
            for i in range(NT):
                for k in range(2):
                    m = pe(lambda e, s=s, i=i, k=k: e.matmul(
                        s[:, 8 * i:8 * i + 8], src[:, k, 128 * i:128 * i + 128], wt_ap[:, k, :],
                        start=(k == 0), stop=(k == 1)), wt, *src_t, *w)
            sv = s[:, 0:64].rearrange("p (t e) -> p t e", e=8)
            o = dve(lambda e: e.tensor_copy(LG, sv), m, *rel_lg)
            o2 = o
            if bias is not None:
                o2 = dve(lambda e: e.tensor_tensor(LB, LG, bias, ALU.add), o, bias_t)
            RB.done(r, o)
            return o, o2

        rel_lg = []

        def top(src, oh, mx, tk):
            o = dve(lambda e: e.tensor_reduce(mx, src, AX.X, ALU.max), tk)
            o = dve(lambda e: e.tensor_tensor(oh, src, bc(mx), ALU.is_equal), o)
            o = dve(lambda e: e.tensor_tensor(oh, oh, REV, ALU.mult), o, t_rev)
            o = dve(lambda e: e.tensor_reduce(RT[:, 7, :], oh, AX.X, ALU.max), o)
            return dve(lambda e: e.tensor_tensor(oh, oh, bc(RT[:, 7, :]), ALU.is_equal), o)

        def second(src, tk):
            o = dve(lambda e: e.scalar_tensor_tensor(
                out=LB.rearrange("p t e -> p (t e)"), in0=OH1.rearrange("p t e -> p (t e)"), scalar=NEG,
                in1=src.rearrange("p t e -> p (t e)"), op0=ALU.mult, op1=ALU.add), tk)
            return top(LB, OH2, RT[:, 1, :], o)

        def pair_gates(tk):
            o = dve(lambda e: e.tensor_tensor(RT[:, 2, :], RT[:, 1, :], RT[:, 0, :], ALU.subtract), tk)
            o = act(lambda e: e.activation(RT[:, 3, :], RT[:, 2, :], ACT.Exp), o)
            o2 = act(lambda e: e.activation(RT[:, 4, :], RT[:, 2, :], ACT.Exp, scale=-1.0), o)
            o = dve(lambda e: e.tensor_scalar(RT[:, 3:5, :], RT[:, 3:5, :], 1.0, None, ALU.add), o2)
            o = dve(lambda e: e.reciprocal(RT[:, 5:7, :], RT[:, 3:5, :]), o)
            o1 = dve(lambda e: e.tensor_tensor(OH1, OH1, bc(RT[:, 5, :]), ALU.mult), o)
            o2 = dve(lambda e: e.tensor_tensor(OH2, OH2, bc(RT[:, 6, :]), ALU.mult), o)
            return dve(lambda e: e.tensor_tensor(GATE, OH1, OH2, ALU.add), o2)

        FW = [view(11264 + 6144 * i, 6144) for i in range(2)]
        HT = [view(23552 + 4096 * i, 4096, "p (f n) -> p f n", n=512) for i in range(2)]
        SR_OFF = 31744
        EX = 34304

        def experts(layer, F, jobs, free, gate_t, consume):
            nf = F // P
            glu = layer != 2
            up_n = (2 if glu else 1) * 2 * F
            SRG = Ring([view(SR_OFF + 512 * i, 512) for i in range(4)])
            for i in range(4):
                SRG.done(i, *free)
            wrel = [list(free), list(free)]
            hrel = [list(free), list(free)]
            wt = {}
            units = [(j, c) for j in range(len(jobs)) for c in range(2)]

            def wload(j):
                src = jobs[j][0]
                wt[j] = load(f"fw{j % 2}", FW[j % 2][:, 0:src.shape[1]], src, *wrel[j % 2])

            def up(u):
                j, c = units[u]
                _, src, st = jobs[j]
                W = FW[j % 2]
                ht = HT[u % 2]
                wa = W[:, 0:2 * F].rearrange("p (k n) -> p k n", k=2)
                wg = W[:, 2 * F:4 * F].rearrange("p (k n) -> p k n", k=2)
                toks = []
                for f in range(nf if glu else nf // 2):
                    s, w, r = RA.get()
                    for z in range(2):
                        ww = (wa, wg)[z] if glu else wa
                        ff = f if glu else 2 * f + z
                        for k in range(2):
                            m = pe(lambda e, s=s, z=z, ww=ww, ff=ff, k=k: e.matmul(
                                s[:, 512 * z:512 * z + 512], ww[:, k, 128 * ff:128 * ff + 128],
                                src[:, k, 512 * c:512 * c + 512], start=(k == 0), stop=(k == 1)),
                                wt[j], *st, *w)
                    if glu:
                        sg, gw, gr = SRG.get()
                        a = act(lambda e, s=s, sg=sg: e.activation(sg, s[:, 0:512], ACT.Silu), m, *gw)
                        o = dve(lambda e, s=s, sg=sg, ht=ht, f=f: e.tensor_tensor(
                            ht[:, f, :], sg, s[:, 512:1024], ALU.mult), a, *hrel[u % 2])
                        SRG.done(gr, o)
                    else:
                        dst = ht[:, 2 * f:2 * f + 2, :].rearrange("p f n -> p (f n)")
                        if f % 2 == 0:
                            o = act(lambda e, s=s, dst=dst: e.activation(dst, s, ACT.Relu), m, *hrel[u % 2])
                        else:
                            o = dve(lambda e, s=s, dst=dst: e.tensor_scalar(dst, s, 0.0, None, ALU.max), m,
                                    *hrel[u % 2])
                    RA.done(r, o)
                    toks.append(o)
                return toks

            def down(u, toks):
                j, c = units[u]
                wd = FW[j % 2][:, up_n:up_n + nf * 256].rearrange("p (f n) -> p f n", n=256)
                ht = HT[u % 2]
                for t in range(4):
                    s, w, r = RB.get()
                    for f in range(nf):
                        m = pe(lambda e, s=s, t=t, f=f: e.matmul(
                            s[:, 0:256], ht[:, f, 128 * t:128 * t + 128], wd[:, f, :],
                            start=(f == 0), stop=(f == nf - 1)), *toks, *w)
                    consume(j, 4 * c + t, s[:, 0:256], m, r)
                hrel[u % 2] = [m]
                if c == 1:
                    wrel[j % 2] = [m]
                    if j + 2 < len(jobs):
                        wload(j + 2)
                return m

            wload(0)
            wload(1)
            prev = None
            for u in range(len(units)):
                cur = up(u)
                if prev is not None:
                    down(u - 1, prev)
                prev = cur
            return down(len(units) - 1, prev)

        def add_gated(gate, gate_t):
            def consume(j, t, s, m, r):
                g = gate(j, t)
                if g is None:
                    o = dve(lambda e, s=s, t=t: e.tensor_tensor(X[:, t, :], X[:, t, :], s, ALU.add), m, xt[t])
                else:
                    o = dve(lambda e, s=s, t=t, g=g: e.scalar_tensor_tensor(
                        out=X[:, t, :], in0=s, scalar=g, in1=X[:, t, :], op0=ALU.mult, op1=ALU.add),
                        m, xt[t], gate_t)
                xt[t] = o
                RB.done(r, o)
            return consume

        RW = view(51200, 16, "p (k e) -> p k e", k=2)
        BCR = view(51216, 64, "p (t e) -> p t e", e=8)
        BIAS = view(51300, 256)

        def finish(free):
            o = OUT.rearrange("b (t p) d -> p (b t) d", p=P)
            f = q.dma("out", lambda e: e.dma_start(o, X), list(xt) + list(free))
            q.add("sync", lambda e: e.nop(), [f])
            q.emit()

        def add_bias(col, n_t, free):
            t = load("bias", BIAS, T["bc"][:, col:col + 256], *free)
            for i in range(NT):
                xt[i] = pool(lambda e, i=i: e.tensor_tensor(X[:, i, :], X[:, i, :], BIAS, ALU.add),
                             t, n_t[i], xt[i])
            return [xt[NT - 1]]

        nt = norm(X, XN, NT, EPS, xt, [])
        bias_free = add_bias(0, nt, [])
        nt2 = norm(XN, XN, NT, EPS, nt, [nt[-1]])
        lat, lpe = turn(XN, XNT, NT, nt2, [], (vec(V_LATG), vec(V_LATB)))
        CTN = view(25000, 4096, "p (t d) -> p t d", d=D)
        c_t = []
        for hb in range(2):
            c_t += norm(CTX[:, 8 * hb:8 * hb + 8, :], CTN[:, 8 * hb:8 * hb + 8, :], 8, EPS, [t_ctx] * 8,
                        [nt2[-1]] + c_t[-1:])
        hat, hpe = turn(CTN, HAT, 16, c_t, [])
        CT0 = view(29696, 4096, "p (k n) -> p k n", k=2)
        ct = []
        for k in range(2):
            ct.append(act(lambda e, k=k: e.activation(CT0[:, k, :], HAT[:, k, :], ACT.Identity,
                                                      bias=vec(V_CTXB)[:, k:k + 1],
                                                      scale=vec(V_CTXG)[:, k:k + 1]), *hat, hpe, t_vec))
        TB = view(TAB_OFF, 2048)
        tab = load("tab", TB, T["l0_tab"])
        tab = dve(lambda e: e.tensor_scalar(TB[:, 1024:2048], TB[:, 1024:2048], SGN, None, ALU.mult), tab, t_vec)
        fr = attention64(0, lat, [lpe], ct, CT0, [tab], [], [hpe, c_t[-1]])
        if stop == 1:
            finish(fr)
            return

        def pre_ffn(fr, rw, twice=False):
            nt = norm(X, XN, NT, EPS, xt, fr)
            lat, lpe = turn(XN, XNT, NT, nt, fr)
            w = load("rw", RW, rw, *fr)
            return nt, lat, lpe, w

        nt, lat, lpe, w = pre_ffn(fr, T["l0_rw"])
        bt = load("rb", BCR, T["bc"][:, 1536:1600].rearrange("p (t e) -> p t e", e=8))
        o, o2 = logits(XNT, RW, w, lat, BCR, bt)
        o = top(LB, OH1, RT[:, 0, :], o2)
        o = dve(lambda e: e.tensor_tensor(LB, LB, bc(RT[:, 0, :]), ALU.subtract), o)
        o = act(lambda e: e.activation(LB, LB, ACT.Exp), o)
        o = dve(lambda e: e.tensor_reduce(RT[:, 1, :], LB, AX.X, ALU.add), o)
        o = dve(lambda e: e.reciprocal(RT[:, 2, :], RT[:, 1, :]), o)
        gt = dve(lambda e: e.tensor_tensor(GATE, OH1, bc(RT[:, 2, :]), ALU.mult), o)
        m = experts(0, 1024, [(T["l0_ffn"][e], XNT, lat) for e in range(8)], fr,
                    gt, add_gated(lambda j, t: GATE[:, t, j:j + 1], gt))
        fr = [m] + xt
        if stop == 2:
            finish(fr)
            return

        nt = norm(X, XN, NT, EPS, xt, fr)
        nt2 = norm(XN, XN, NT, EPS, nt, [nt[-1]])
        lat, lpe = turn(XN, XNT, NT, nt2, fr, (vec(V_GL), vec(V_BL)))
        ct = []
        for k in range(2):
            ct.append(act(lambda e, k=k: e.activation(HAT[:, k, :], HAT[:, k, :], ACT.Identity,
                                                      bias=vec(V_BX)[:, k:k + 1],
                                                      scale=vec(V_GX)[:, k:k + 1]), *ct))
        tab = load("tab", TB, T["l1_tab"], *fr)
        fr = attention64(1, lat, [lpe], ct, HAT, [tab], fr, fr)
        if stop == 3:
            finish(fr)
            return

        nt, lat, lpe, w = pre_ffn(fr, T["l1_rw"])
        o, _ = logits(XNT, RW, w, lat)
        o = top(LG, OH1, RT[:, 0, :], o)
        o = act(lambda e: e.activation(RT[:, 1, :], RT[:, 0, :], ACT.Exp, scale=-1.0), o)
        o = dve(lambda e: e.tensor_scalar(RT[:, 1, :], RT[:, 1, :], 1.0, None, ALU.add), o)
        o = dve(lambda e: e.reciprocal(RT[:, 2, :], RT[:, 1, :]), o)
        ns = [dve(lambda e, i=i: e.tensor_scalar(XN[:, i, :], XN[:, i, :], RT[:, 2, i:i + 1], None, ALU.mult), o, lpe)
              for i in range(NT)]
        XST = view(EX, 2048, "p (k n) -> p k n", k=2)
        lats, lpe = turn(XN, XST, NT, ns, fr)
        m = experts(1, 512, [(T["l1_shared"], XNT, lat)] + [(T["l1_ffn"][e], XST, lats) for e in range(8)], fr,
                    o, add_gated(lambda j, t: OH1[:, t, j - 1:j] if j else None, o))
        fr = [m] + xt
        if stop == 4:
            finish(fr)
            return

        CT = view(7168, 4096, "p (k n) -> p k n", k=2)
        ctr = load("ctxT", CT, T["ctxT"].rearrange("p (k n) -> p k n", k=2), *fr)
        nt = norm(X, XN, NT, EPS, xt, fr)
        add_bias(256, nt, fr)
        lat, lpe = turn(XN, XNT, NT, nt, fr)
        fr = attention16(2, lat, [lpe], CT, [ctr], fr)
        if stop == 5:
            finish(fr)
            return

        fr = fr + [xt[3], xt[7]]
        nt, lat, lpe, w = pre_ffn(fr, T["l2_rw"])
        o, _ = logits(XNT, RW, w, lat)
        o = top(LG, OH1, RT[:, 0, :], o)
        o = second(LG, o)
        gt = pair_gates(o)
        m = experts(2, 1024, [(T["l2_ffn"][e], XNT, lat) for e in range(8)], fr,
                    gt, add_gated(lambda j, t: GATE[:, t, j:j + 1], gt))
        fr = [m] + xt
        if stop == 6:
            finish(fr)
            return

        nt = norm(X, XN, NT, EPS, xt, fr)
        add_bias(768, nt, fr)
        lat, lpe = turn(XN, XNT, NT, nt, fr)
        fr = attention16(3, lat, [lpe], CT, [ctr], fr)
        fr = fr + [xt[3], xt[7]]
        if stop == 7:
            finish(fr)
            return

        nt = norm(X, XN, NT, EPS, xt, fr)
        lat, lpe = turn(XN, XNT, NT, nt, fr)
        WIO = view(EX, 1024, "p (a k n) -> p a k n", a=2, k=2)
        NW = view(EX + 1024, 512, "p (a n) -> p a n", a=2)
        EN = view(EX + 1536, 2048, "p (e n) -> p e n", n=256)
        ACC = view(EX + 3584, 2048, "p (t n) -> p t n", n=256)
        JK = [view(EX + 5632 + 256 * i, 256) for i in range(2)]
        TM = Ring([view(EX + 6144 + 256 * i, 256) for i in range(4)])
        wio = load("wio", WIO.rearrange("p a k n -> p (a k n)"), T["l3_wio"], *fr)
        nwt = load("nw", NW.rearrange("p a n -> p (a n)"), T["bc"][:, 1024:1536], *fr)
        ent = load("en", EN.rearrange("p e n -> p (e n)"), T["bc"][:, 1664:3712], *fr)
        w = load("rw", RW, T["l3_rw"], *fr)
        bt = load("rb", BCR, T["bc"][:, 1600:1664].rearrange("p (t e) -> p t e", e=8), *fr)

        def rms(src, i, col, tk, rel):
            return act(lambda e: e.activation(JK[i % 2], src, ACT.Square, accum_out=col), tk, *rel)

        def rsq(dst, src, tk):
            o = pool(lambda e: e.tensor_scalar(src, src, 1.0 / D, EPS3, ALU.mult, ALU.add), *tk)
            return pool(lambda e: e.tensor_tensor(dst, src, MHALF[:, 0:src.shape[1]], ALU.pow), o)

        ht_, jrel, pss = [], [[], []], []
        for i in range(NT):
            s, w_, r = RB.get()
            for k in range(2):
                m = pe(lambda e, s=s, i=i, k=k: e.matmul(s[:, 0:256], XNT[:, k, 128 * i:128 * i + 128],
                                                         WIO[:, 0, k, :], start=(k == 0), stop=(k == 1)),
                       wio, *lat, *w_)
            a = dve(lambda e, s=s, i=i: e.tensor_copy(XN[:, i, :], s[:, 0:256]), m, lpe)
            RB.done(r, a)
            o = rms(XN[:, i, :], i, VE[:, i:i + 1], a, jrel[i % 2])
            jrel[i % 2] = [o]
        o = rsq(RS[:, 0:8], VE[:, 0:8], [o])
        hn = [dve(lambda e, i=i: e.scalar_tensor_tensor(out=XN[:, i, :], in0=XN[:, i, :], scalar=RS[:, i:i + 1],
                                                        in1=NW[:, 0, :], op0=ALU.mult, op1=ALU.mult), o, nwt)
              for i in range(NT)]
        lat, lpe = turn(XN, XNT, NT, hn, [m])
        o, o2 = logits(XNT, RW, w, lat, BCR, bt)
        o = top(LB, OH1, RT[:, 0, :], o2)
        o = second(LB, o)
        for n, oh in enumerate((OH1, OH2)):
            o = dve(lambda e, oh=oh: e.tensor_tensor(LB, oh, LG, ALU.mult), o)
            o = dve(lambda e, n=n: e.tensor_reduce(RT[:, n, :], LB, AX.X, ALU.add), o)
        gt = pair_gates(o)
        hold = []
        msrel = [[], []]
        acct = [None] * NT

        def consume(j, t, s, m, r):
            hold.append((t, s, m, r))
            if len(hold) < 4:
                return
            u = (2 * j + t // 4) % 2
            ms, grr = MS[:, u, :], GR[:, u, :]
            for n, (t_, s_, m_, r_) in enumerate(hold):
                o = rms(s_, n, ms[:, n:n + 1], m_, jrel[n % 2] + msrel[u])
                jrel[n % 2] = [o]
            o = rsq(grr, ms, [o] + msrel[u])
            t0 = hold[0][0]
            o = pool(lambda e: e.tensor_tensor(grr, grr, GATE[:, t0:t0 + 4, j], ALU.mult), o, gt)
            for n, (t_, s_, m_, r_) in enumerate(hold):
                if j == 0:
                    d = dve(lambda e, s_=s_, n=n, t_=t_: e.scalar_tensor_tensor(
                        out=ACC[:, t_, :], in0=s_, scalar=grr[:, n:n + 1], in1=EN[:, j, :], op0=ALU.mult,
                        op1=ALU.mult), o, ent)
                    acct[t_] = d
                else:
                    tm, tw, tr = TM.get()
                    d = dve(lambda e, s_=s_, n=n, tm=tm: e.scalar_tensor_tensor(
                        out=tm, in0=s_, scalar=grr[:, n:n + 1], in1=EN[:, j, :], op0=ALU.mult, op1=ALU.mult),
                        o, ent, *tw)
                    acct[t_] = pool(lambda e, t_=t_, tm=tm: e.tensor_tensor(
                        ACC[:, t_, :], ACC[:, t_, :], tm, ALU.add), d, acct[t_])
                    TM.done(tr, acct[t_])
                RB.done(r_, d)
            msrel[u] = [d]
            hold.clear()

        m = experts(3, 1024, [(T["l3_ffn"][e], XNT, lat) for e in range(8)], fr, gt, consume)
        for i in range(NT):
            o = rms(ACC[:, i, :], i, VE[:, i:i + 1], acct[i], jrel[i % 2])
            jrel[i % 2] = [o]
        o = rsq(RS[:, 0:8], VE[:, 0:8], [o])
        hn = [dve(lambda e, i=i: e.scalar_tensor_tensor(out=XN[:, i, :], in0=ACC[:, i, :], scalar=RS[:, i:i + 1],
                                                        in1=NW[:, 1, :], op0=ALU.mult, op1=ALU.mult), o, lpe)
              for i in range(NT)]
        lat, lpe = turn(XN, XNT, NT, hn, [m])
        for i in range(NT):
            s, w_, r = RB.get()
            for k in range(2):
                m = pe(lambda e, s=s, i=i, k=k: e.matmul(s[:, 0:256], XNT[:, k, 128 * i:128 * i + 128],
                                                         WIO[:, 1, k, :], start=(k == 0), stop=(k == 1)), *lat, *w_)
            xt[i] = dve(lambda e, s=s, i=i: e.tensor_tensor(X[:, i, :], X[:, i, :], s[:, 0:256], ALU.add), m, xt[i])
            RB.done(r, xt[i])
        finish([])


def rope_table(n, d, slot, copies):
    inv = (np.float32(1.0) / np.float32(10000.0) ** (np.arange(0, d, 2, dtype=np.float32) / np.float32(d)))
    ang = (np.arange(n, dtype=np.float32)[:, None] * inv.astype(np.float32)[None, :]).astype(np.float32)
    c, s = np.cos(ang).astype(np.float32).T, np.sin(ang).astype(np.float32).T
    cos, sin = np.zeros((copies, slot, n), np.float32), np.zeros((copies, slot, n), np.float32)
    h = d // 2
    cos[:, 0:h], cos[:, h:d], sin[:, 0:h], sin[:, h:d] = c, c, -s, s
    return np.concatenate([cos.reshape(-1, n), sin.reshape(-1, n)], axis=1)


def layout(a):
    def f(n):
        return np.asarray(a[n])

    def rows(w):
        k = w.shape[0] // P
        return w.reshape(k, P, -1).transpose(1, 0, 2).reshape(P, -1)

    def swap(w, d):
        v = w.reshape(w.shape[0], -1, 2, d // 2)
        return np.concatenate([v[:, :, 1], v[:, :, 0]], axis=2).reshape(w.shape)

    def slots(w):
        o = np.zeros((w.shape[0], 16, 32), np.float32)
        o[:, :, 0:16] = w.reshape(w.shape[0], 16, 16)
        return o.reshape(w.shape[0], 512)

    T = {"x": f("x"), "ctx": f("ctx_1024")}
    v = np.zeros((P, 26), np.float32)
    for i, n in enumerate(("L0_xattn_ln_lat_g", "L0_xattn_ln_lat_b", "L0_xattn_ln_ctx_g", "L0_xattn_ln_ctx_b",
                           "L1_xattn_gamma_x", "L1_xattn_beta_x", "L1_xattn_gamma_l", "L1_xattn_beta_l")):
        v[:, 2 * i:2 * i + 2] = f(n).reshape(2, P).T
    bkv = f("L2_xattn_bkv")
    v[:, 16:20] = slots(f("L2_xattn_bq")[None]).reshape(4, P).T
    v[:, 20:24] = slots(bkv[None, 0:256]).reshape(4, P).T
    v[16::32, 20:24] = 1.0
    v[:, 24] = np.where(np.arange(P) % 64 < 32, -1.0, 1.0)
    v[16::32, 25] = 1.0
    T["vec"] = v
    T["rev"] = np.broadcast_to(np.tile(np.arange(8, 0, -1, dtype=np.float32), 8), (P, 64))
    row = np.concatenate([f("L0_xattn_bo"), f("L2_xattn_bp"), bkv[256:512], f("L3_xattn_bo"),
                          f("L3_ffn_in_norm_w"), f("L3_ffn_out_norm_w"), np.tile(f("L0_ffn_router_b"), 8),
                          np.tile(f("L3_ffn_expert_bias"), 8), f("L3_ffn_enorm_w").reshape(-1)])
    T["bc"] = np.broadcast_to(row, (P, row.size))
    sel = np.zeros((P, P), np.float32)
    for j in range(4):
        sel[32 * j + 16, 32 * j:32 * j + 32] = 1.0
    T["sel"] = sel
    T["ctxT"] = rows(f("ctx_1024").reshape(2048, D).T)
    cs = [np.concatenate([f(n).T] * 4) for n in ("L0_xattn_cos", "L0_xattn_sin")]
    T["l0_tab"] = np.concatenate(cs, axis=1)
    T["l1_tab"] = rope_table(1024, 64, 64, 2)
    T["l3_tab"] = rope_table(1024, 16, 32, 4)

    for L, inner in ((0, 1024), (1, 512)):
        wq, wkv, wo = f(f"L{L}_xattn_Wq"), f(f"L{L}_xattn_Wkv"), f(f"L{L}_xattn_Wo")
        wk, wv = wkv[:, 0:inner], wkv[:, inner:]
        wr = swap(wk, 64)
        T[f"l{L}_w"] = np.stack([np.concatenate(
            [rows(w[:, 256 * g:256 * g + 256]) for w in (wq, wk, wr, wv)] + [rows(wo[256 * g:256 * g + 256])],
            axis=1) for g in range(inner // 256)])

    def wo_slots(w):
        o = np.zeros((16, 32, D), np.float32)
        o[:, 0:16] = w.reshape(16, 16, D)
        return rows(o.reshape(512, D))

    for L, wo in ((2, "L2_xattn_Wp"), (3, "L3_xattn_Wo")):
        wq, wkv = f(f"L{L}_xattn_Wq"), f(f"L{L}_xattn_Wkv")
        wk, wv = wkv[:, 0:256], wkv[:, 256:512]
        T[f"l{L}_w"] = np.concatenate([rows(slots(wq)), rows(slots(swap(wq, 16))), rows(slots(wk)),
                                       rows(slots(swap(wk, 16))), rows(wv), wo_slots(f(wo))], axis=1)
    w1, w2 = f("L0_ffn_w1"), f("L0_ffn_w2")
    T["l0_ffn"] = np.stack([np.concatenate([rows(w1[e][:, 0:1024]), rows(w1[e][:, 1024:]), rows(w2[e])], axis=1)
                            for e in range(8)])
    g, u, d = f("L1_ffn_expert_gate"), f("L1_ffn_expert_up"), f("L1_ffn_expert_down")
    T["l1_ffn"] = np.stack([np.concatenate([rows(g[e]), rows(u[e]), rows(d[e])], axis=1) for e in range(8)])
    T["l1_shared"] = np.concatenate([rows(f("L1_ffn_shared_gate")), rows(f("L1_ffn_shared_up")),
                                     rows(f("L1_ffn_shared_down"))], axis=1)
    w1, w2 = f("L2_ffn_w1"), f("L2_ffn_w2")
    T["l2_ffn"] = np.stack([np.concatenate([rows(w1[e].T), rows(w2[e].T)], axis=1) for e in range(8)])
    g, u, d = f("L3_ffn_Wg"), f("L3_ffn_Wu"), f("L3_ffn_Wd")
    T["l3_ffn"] = np.stack([np.concatenate([rows(g[e].T), rows(u[e].T), rows(d[e].T)], axis=1) for e in range(8)])
    T["l3_wio"] = np.concatenate([rows(f("L3_ffn_W_in").T), rows(f("L3_ffn_W_out").T)], axis=1)

    def rw(w):
        return rows(w).reshape(P, 2, 8)

    T["l0_rw"] = rw(f("L0_ffn_router_w"))
    T["l1_rw"] = rw(f("L1_ffn_router_w").T)
    T["l2_rw"] = rw(f("L2_ffn_gate_w").T)
    T["l3_rw"] = rw(f("L3_ffn_Wr").T)
    return {n: np.ascontiguousarray(x) for n, x in T.items()}


def kernel(**inputs):
    import concourse.bacc as _bacc
    from concourse.bass_utils import run_bass_kernel_spmd as _run

    nc = _bacc.Bacc("TRN2", target_bir_lowering=False, num_devices=1)
    arrays = layout(inputs)
    T = {n: nc.dram_tensor(f"in_{n}", x.shape, F32, kind="ExternalInput").ap() for n, x in arrays.items()}
    out = nc.dram_tensor("out_x", (2, 512, 256), F32, kind="ExternalOutput").ap()
    build(nc, T, out)
    r = _run(nc, [{f"in_{n}": x for n, x in arrays.items()}], core_ids=[0])
    return r.results[0]["out_x"]
```

```python
from contextlib import ExitStack

import numpy as np

import concourse.bass as bass
from concourse import mybir

F32 = mybir.dt.float32
F32R = mybir.dt.float32r
ALU = mybir.AluOpType
ACT = mybir.ActivationFunctionType
AX = mybir.AxisListType

P = 128
D = 256
NT = 8
B = 2
EPS = 1e-5
EPS3 = float(np.finfo(np.float32).eps)
CLIP_LO = float(np.exp(np.float64(-11.0)))
CLIP_HI = float(np.exp(np.float64(11.0)))
NEG = -1e30
NF = 20300
NR = 32800


class Tok:

    __slots__ = ("key", "n", "used")

    def __init__(self, key, n):
        self.key, self.n, self.used = key, n, False


class Queues:

    ENGINES = ("tensor", "vector", "scalar", "gpsimd", "sync")

    def __init__(self, nc, ctx):
        self.nc, self.ctx = nc, ctx
        self.ops = {e: [] for e in self.ENGINES}
        self.sems, self.counts = {}, {}

    def add(self, eng, fn, waits):
        t = Tok(eng, len(self.ops[eng]))
        flat = [w for w in waits if w is not None]
        for w in flat:
            w.used = True
        self.ops[eng].append((fn, flat, t, None))
        return t

    def dma(self, name, fn, waits, eng="sync"):
        self.counts[name] = self.counts.get(name, 0) + 16
        t = Tok("d_" + name, self.counts[name])
        flat = [w for w in waits if w is not None]
        for w in flat:
            w.used = True
        self.ops[eng].append((fn, flat, None, "d_" + name))
        return t

    def sem(self, key):
        if key not in self.sems:
            self.sems[key] = self.ctx.enter_context(self.nc.semaphore("s_" + key))
        return self.sems[key]

    def emit(self):
        for e in self.ENGINES:
            n = 0
            for _, _, t, d in self.ops[e]:
                if t is not None and t.used:
                    n += 1
                    t.n = n
            self.sem(e)
            for _, _, _, d in self.ops[e]:
                if d:
                    self.sem(d)
        block = self.ctx.enter_context(self.nc.Block())
        for e in self.ENGINES:
            into = {"tensor": block.tensor, "vector": block.vector, "scalar": block.scalar,
                            "gpsimd": block.gpsimd, "sync": block.sync}[e]
            into(self.body(e))

    def body(self, e):
        def run(eng):
            known = {}
            for fn, waits, t, d in self.ops[e]:
                need = {}
                for w in waits:
                    need[w.key] = max(need.get(w.key, 0), w.n)
                for key, v in need.items():
                    if known.get(key, 0) < v:
                        eng.wait_ge(self.sem(key), v)
                        known[key] = v
                ins = fn(eng)
                if d:
                    ins.then_inc(self.sem(d), 16)
                elif t.used:
                    ins.then_inc(self.sem(e), 1)
        return run


class Ring:

    def __init__(self, bufs):
        self.bufs, self.rel, self.n = bufs, [[] for _ in bufs], 0

    def get(self):
        i = self.n % len(self.bufs)
        self.n += 1
        rel, self.rel[i] = self.rel[i], None
        assert rel is not None, "a buffer's last use isn't queued yet"
        return self.bufs[i], rel, i

    def done(self, i, *toks):
        self.rel[i] = list(toks)


class Work:

    def __init__(self, parts, total):
        self.parts, self.total, self.sum = parts, total, 0.0

    def upto(self, share):
        while self.sum < share * self.total - 1e-6:
            w = next(self.parts, None)
            if w is None:
                return
            self.sum += w

    def rest(self):
        for w in self.parts:
            self.sum += w
        return self.sum


def build(nc, T, OUT, stop=99):
    ctx = ExitStack()
    with ctx:
        q = Queues(nc, ctx)
        AF = ctx.enter_context(nc.sbuf_tensor("plain", [P, NF], F32))
        AR = ctx.enter_context(nc.sbuf_tensor("split", [P, NR], F32R))
        PS = ctx.enter_context(nc.psum_tensor("psum", [P, 4096], F32))

        def pe(fn, *w):
            return q.add("tensor", fn, w)

        def dve(fn, *w):
            return q.add("vector", fn, w)

        def act(fn, *w):
            return q.add("scalar", fn, w)

        pool_last = [None]

        def pool(fn, *w):
            pool_last[0] = q.add("gpsimd", fn, (pool_last[0],) + w)
            return pool_last[0]

        def load(name, dst, src, *w):
            return q.dma(name, lambda e: e.dma_start(dst, src), w)

        def view(off, cnt, pat=None, **kw):
            v = AF[:, off:off + cnt]
            return v.rearrange(pat, **kw) if pat else v

        def rview(off, cnt, pat=None, **kw):
            v = AR[:, off:off + cnt]
            return v.rearrange(pat, **kw) if pat else v

        def pairview(off, cnt, pat=None, **kw):
            return rview(off, cnt, pat, **kw), rview(off + cnt, cnt, pat, **kw)

        def f32(ap):
            return ap.bitcast(F32)

        def mm3(out, lhs, rhs, first, last, waits, skip=False):
            for n, (x, y) in enumerate(((0, 0), (0, 1), (1, 0))):
                m = pe(lambda e, x=x, y=y, n=n: e.matmul(out, lhs[x], rhs[y], start=(first and n == 0),
                                                         stop=(last and n == 2), skip_group_check=skip), *waits)
            return m

        def bank(i, n=512):
            return PS[:, 512 * i:512 * i + n]

        RA = Ring([PS[:, 0:1024], PS[:, 1024:2048]])
        RB = RB4 = Ring([bank(i) for i in range(4, 8)])

        X = view(0, 2048, "p (t d) -> p t d", d=D)
        XN = view(2048, 2048, "p (t d) -> p t d", d=D)
        XNT = pairview(0, 2048, "p (k n) -> p k n", k=2)
        ID = view(4096, 128)
        at = [4224]

        def small(cnt, pat=None, **kw):
            at[0] += cnt
            assert at[0] <= 5120
            return view(at[0] - cnt, cnt, pat, **kw)

        VEC = small(T["vec"].shape[1])
        ST = small(96, "p (t s) -> p t s", s=6)
        MV = small(32, "p (t s) -> p t s", s=2)
        VE = small(16)
        RS = small(16)
        MHALF = small(16)
        LG = small(64, "p (t e) -> p t e", e=8)
        LB = small(64, "p (t e) -> p t e", e=8)
        OH1 = small(64, "p (t e) -> p t e", e=8)
        OH2 = small(64, "p (t e) -> p t e", e=8)
        GATE = small(64, "p (t e) -> p t e", e=8)
        REV = small(64, "p (t e) -> p t e", e=8)
        RT = small(64, "p (s t) -> p s t", t=8)
        MS = small(16, "p (r t) -> p r t", t=4)
        GR = small(16, "p (r t) -> p r t", t=4)
        xin = T["x"].rearrange("b (t p) d -> p (b t) d", p=P)
        t_x = load("x", X, xin)
        t_vec = load("vec", VEC, T["vec"])
        t_rev = load("rev", REV.rearrange("p t e -> p (t e)"), T["rev"])
        t = pool(lambda e: e.memset(ID, 0.0))
        t_id = pool(lambda e: e.affine_select(out=ID, in_=ID, compare_op=ALU.not_equal, fill=1.0, base=0,
                                              pattern=[[-1, P]], channel_multiplier=1), t)
        t_mh = pool(lambda e: e.memset(MHALF, -0.5))

        xt = [t_x] * NT

        def norm(src, dst, n, eps, src_t, free):
            for i in range(n):
                a = dve(lambda e, i=i: e.bn_stats(ST[:, i, :], src[:, i, :]), src_t[i], *free)
            for i in range(n):
                a = dve(lambda e, i=i: e.bn_aggr(MV[:, i, :], ST[:, i, :]), a if i == 0 else None)
            b = pool(lambda e: e.tensor_scalar(VE[:, 0:n], MV[:, 0:n, 1], eps, None, ALU.add), a)
            b = pool(lambda e: e.tensor_tensor(RS[:, 0:n], VE[:, 0:n], MHALF[:, 0:n], ALU.pow), b, t_mh)
            out = []
            for i in range(n):
                out.append(dve(lambda e, i=i: e.tensor_scalar(dst[:, i, :], src[:, i, :], MV[:, i, 0:1],
                                                              RS[:, i:i + 1], ALU.subtract, ALU.mult), a, b))
            return out

        def split(dst, src, tk, free, lo_eng=None):
            h = act(lambda e: e.activation(dst[0], src, ACT.Copy), *tk, *free)
            o = (lo_eng or dve)(lambda e: e.tensor_tensor(dst[1], src, f32(dst[0]), ALU.subtract), h, *tk, *free)
            return h, o

        def turn(src, dst, n, src_t, free, gain=None, tmp=None):
            out = []
            for c in range(n // 4):
                for k in range(2):
                    s, w, r = RB.get()
                    for j in range(4):
                        i = 4 * c + j
                        m = pe(lambda e, s=s, i=i, j=j, k=k: e.transpose(
                            s[:, 128 * j:128 * j + 128], src[:, i, 128 * k:128 * k + 128], ID),
                            src_t[i], t_id, *w)
                    d = [x[:, k, 512 * c:512 * c + 512] for x in dst]
                    if gain:
                        tb, tw, tr = tmp.get()
                        a = dve(lambda e, tb=tb, s=s, k=k: e.tensor_scalar(
                            tb, s, gain[0][:, k:k + 1], gain[1][:, k:k + 1], ALU.mult, ALU.add), m, t_vec, *tw)
                        RB.done(r, a)
                        h, o = split(d, tb, [a], free)
                        tmp.done(tr, h, o)
                    else:
                        h, o = split(d, s, [m], free)
                        RB.done(r, h, o)
                    out += [h, o]
            return out, m

        def vec(i):
            return VEC[:, 2 * i:2 * i + 2]

        V_LATG, V_LATB, V_CTXG, V_CTXB, V_GX, V_BX, V_GL, V_BL = range(8)
        BQ = VEC[:, 16:20]
        BK = VEC[:, 20:24]
        SGN = VEC[:, 24:25]
        ONE16 = VEC[:, 25:26]

        C64 = pairview(4096, 4096, "p (k n) -> p k n", k=2)
        TB = view(12288, 2048)
        ONES = view(18944, 64)
        t_one = dve(lambda e: e.memset(ONES, 1.0))
        ONESR = rview(NR - 128, 128)
        t_oner = dve(lambda e: e.memset(f32(ONESR), 1.0))
        NMX = view(20288, 12)
        K32 = Ring([view(19008 + 512 * i, 512) for i in range(2)])

        def attention64(layer, lat_t, lat_free, ctx_t, tab_t, free):
            own = layer == 1
            S = 1536 if own else 1024
            nk = S // P
            KT = [rview(14336 + 3072 * i, 2 * S, "p (h n) -> p h n", h=2) for i in range(2)]
            QA = [rview(20480 + 2048 * i, 1024, "p (h n) -> p h n", h=2) for i in range(2)]
            QB = [rview(21504 + 2048 * i, 1024, "p (h n) -> p h n", h=2) for i in range(2)]
            DG = [rview(24576 + 1024 * i, 1024, "p (h n) -> p h n", h=2) for i in range(2)]
            PT = Ring([view(5120 + 1024 * i, 1024, "p (h n) -> p h n", h=2) for i in range(3)])
            VA = [view(8192 + 1536 * i, nk * 128, "p (t c) -> p t c", c=128) for i in range(2)]
            OT = [view(11264 + 512 * i, 512) for i in range(2)]
            COS, SIN = TB[:, 0:1024], TB[:, 1024:2048]
            WR = [view(14336 + 1280 * i, 1280) for i in range(2)]
            W = [pairview(12288, 1024), pairview(26624, 1024)]
            SA = [view(16896 + 1024 * i, 1024, "p (h n) -> p h n", h=2) for i in range(2)]
            TR = Ring([view(2048 + 1024 * i, 1024, "p (h n) -> p h n", h=2) for i in range(2)])
            for i in range(2):
                TR.done(i, *lat_free)
            npair = 4 if own else 8
            steps = [(p, b) for p in range(npair) for b in range(B)]
            init = []
            for i in range(2):
                for h in range(2):
                    lo = 64 - 64 * h
                    init.append(pool(lambda e, i=i, h=h, lo=lo: e.memset(f32(QB[i][lo:lo + 64, h, :]), 0.0), *free))
            w_raw, w_t = {}, {}
            raw_rel = [list(free), list(free)]
            w_rel = [list(free), list(free)]
            grel = [list(free), list(free)]
            orel = [list(free), list(free)]
            gtok, vtok, negm = {}, {}, {}

            def wload(p):
                w_raw[p] = load(f"wa{p % 2}", WR[p % 2], T[f"l{layer}_w"][p], *raw_rel[p % 2])

            wload(0)
            wload(1)

            def wsplit(p):
                if p < npair:
                    w_t[p] = split(W[p % 2], WR[p % 2][:, 0:1024], [w_raw[p]], w_rel[p % 2])

            wsplit(0)

            def proj(n):
                p, b = steps[n]
                i = n % 2
                toks = list(init)
                wt = w_t[p]

                def wsl(j):
                    return [x[:, 256 * j:256 * j + 256].rearrange("p (k n) -> p k n", k=2) for x in W[p % 2]]

                x0 = 512 * b

                def project(out, j, src, c0, cn, waits):
                    ww = wsl(j)
                    for k in range(2):
                        m = mm3(out, [x[:, k, :] for x in ww], [x[:, k, c0:c0 + cn] for x in src],
                                k == 0, k == 1, [*wt, *waits])
                    return m

                def place(src, tk, c0, cn):
                    out = []
                    for h in range(2):
                        hi, lo = 64 * h, 64 - 64 * h
                        a = act(lambda e, h=h, hi=hi: e.activation(
                            KT[i][hi:hi + 64, h, c0:c0 + cn], src[hi:hi + 64, :], ACT.Copy), tk, *grel[i])
                        out += [a, dve(lambda e, h=h, hi=hi, lo=lo: e.tensor_tensor(
                            KT[i][lo:lo + 64, h, c0:c0 + cn], src[hi:hi + 64, :],
                            f32(KT[i][hi:hi + 64, h, c0:c0 + cn]), ALU.subtract), a, *grel[i])]
                    return out

                s, w, r = RB.get()
                m = project(s, 0, XNT, x0, 512, [*lat_t, *w])
                for h in range(2):
                    hi, lo = 64 * h, 64 - 64 * h
                    a = act(lambda e, s=s, h=h, hi=hi: e.activation(
                        QA[i][hi:hi + 64, h, :], s[hi:hi + 64, :], ACT.Copy), m, *grel[i])
                    a2 = act(lambda e, s=s, h=h, hi=hi, lo=lo: e.activation(
                        QA[i][lo:lo + 64, h, :], s[hi:hi + 64, :], ACT.Copy), m, *grel[i])
                    o = dve(lambda e, s=s, h=h, hi=hi: e.tensor_tensor(
                        QB[i][hi:hi + 64, h, :], s[hi:hi + 64, :], f32(QA[i][hi:hi + 64, h, :]), ALU.subtract),
                        a, a2, *grel[i])
                RB.done(r, a2, o)
                toks += [a2, o]
                yield 1.3
                for c in range(2):
                    tm, tw, tr = TR.get()
                    for j, tb in enumerate((COS, SIN)):
                        s, w, r = RB.get()
                        m = project(s, 1 + j, C64, 1024 * b + 512 * c, 512, [*ctx_t, *w])
                        a2 = dve(lambda e, s=s, tm=tm, c=c, j=j, tb=tb: e.tensor_tensor(
                            tm[:, j, :], s, tb[:, 512 * c:512 * c + 512], ALU.mult), m, *tab_t, *tw)
                        RB.done(r, a2)
                        if j == 0:
                            yield 1.3
                    kb, kw, kr = K32.get()
                    a = pool(lambda e, kb=kb, tm=tm: e.tensor_tensor(kb, tm[:, 0, :], tm[:, 1, :], ALU.add), a2, *kw)
                    TR.done(tr, a)
                    pl = place(kb, a, 512 * c, 512)
                    K32.done(kr, *pl)
                    toks += pl
                    yield 1.3
                if own:
                    s, w, r = RB.get()
                    m = project(s, 1, XNT, x0, 512, w)
                    pl = place(s, m, 1024, 512)
                    RB.done(r, *pl)
                    toks += pl
                    yield 1.3
                ww = wsl(3)
                for t0 in range(0, nk, 4):
                    s, w, r = RB.get()
                    src = C64 if t0 < 8 else XNT
                    for t in range(4):
                        c0 = 1024 * b + 128 * (t0 + t) if t0 < 8 else x0 + 128 * t
                        for k in range(2):
                            m = mm3(s[:, 128 * t:128 * t + 128], [x[:, k, c0:c0 + 128] for x in src],
                                    [x[:, k, :] for x in ww], k == 0, k == 1, [*wt, *w])
                    o = act(lambda e, s=s, t0=t0: e.activation(
                        VA[i][:, t0:t0 + 4, :].rearrange("p t c -> p (t c)"), s, ACT.Copy), m, *grel[i])
                    RB.done(r, o)
                    yield 1.3
                if b == 1:
                    w_rel[p % 2] = [m]
                    wsplit(p + 1)
                gtok[n], vtok[n] = toks, o

            NM = NMX[:, 0:4]
            MXC = NMX[:, 4:12].rearrange("p (t c) -> p t c", c=2)

            def rowmax(n):
                i = n % 2
                nm = []
                prev = mxrel[0]
                for h in range(2):
                    for t in range(4):
                        for c, (k0, kn) in enumerate(((0, 1024), (1024, 512))):
                            s, w, r = RA.get()
                            for u in range(0, kn, 512):
                                m = pe(lambda e, s=s, h=h, t=t, u=u, k0=k0: e.matmul(
                                    s[:, u:u + 512], QA[i][:, h, 128 * t:128 * t + 128],
                                    KT[i][:, h, k0 + u:k0 + u + 512], start=True, stop=True), *gtok[n], *w)
                            o = dve(lambda e, s=s, t=t, c=c, kn=kn: e.tensor_reduce(
                                MXC[:, t, c:c + 1], s[:, 0:kn], AX.X, ALU.max), m, *prev)
                            RA.done(r, o)
                            yield kn / 800
                    o = dve(lambda e: e.tensor_reduce(NM, MXC, AX.X, ALU.max, negate=True), o, *prev)
                    for t in range(4):
                        a = act(lambda e, h=h, t=t: e.activation(
                            DG[i][:, h, 128 * t:128 * t + 128], ID, ACT.Copy, scale=NM[:, t:t + 1]),
                            o, t_id, *grel[i])
                    prev = [o, a]
                mxrel[0] = prev
                gtok[n] = gtok[n] + [a]
                yield 0.0

            def attend(n, work):
                i = n % 2
                out = []
                pend = []
                sacc = [None]

                def values():
                    kt, pt, tp, pr = pend.pop(0)
                    if kt == 0:
                        out.extend(RO.get())
                    so, sw, _ = out
                    for h in range(2):
                        m = pe(lambda e, pt=pt, kt=kt, h=h: e.matmul(
                            so[64 * h:64 * h + 64, :], VA[i][:, kt, 64 * h:64 * h + 64], pt[:, h, :],
                            start=(kt == 0), stop=(kt == nk - 1)), tp, vtok[n], *sw)
                    if kt == 0:
                        sacc[0] = [tp, m]
                        return m
                    sacc[0] = [(dve if kt % 4 == 3 else pool)(
                        lambda e, pt=pt: e.tensor_tensor(SA[i], SA[i], pt, ALU.add), tp, *sacc[0])]
                    PT.done(pr, m, *sacc[0])
                    return m

                for kt in range(nk):
                    s, w, r = RA.get()
                    for h in range(2):
                        d = s[:, 512 * h:512 * h + 512]
                        kk = KT[i][:, h, 128 * kt:128 * kt + 128]
                        pe(lambda e, d=d, kk=kk, h=h: e.matmul(d, kk, QA[i][:, h, :], start=True, stop=False),
                           *gtok[n], *w)
                        m = pe(lambda e, d=d, kk=kk, h=h: e.matmul(d, kk, QB[i][:, h, :], start=False,
                                                                   stop=not own))
                        if own:
                            m = pe(lambda e, d=d, h=h: e.matmul(d, ONESR, DG[i][:, h, :], start=False, stop=True),
                                   t_oner)
                    pt, pw, pr = PT.get() if kt else (SA[i], orel[i], None)
                    tp = act(lambda e, s=s, pt=pt: e.activation(
                        pt.rearrange("p h n -> p (h n)"), s, ACT.Exp, scale=0.125), m, *pw)
                    RA.done(r, tp)
                    if not own:
                        tp = dve(lambda e, pt=pt: e.tensor_scalar(pt, pt, CLIP_LO, CLIP_HI, ALU.max, ALU.min), tp)
                    pend.append((kt, pt, tp, pr))
                    if len(pend) > 2:
                        values()
                    work.upto((kt + 1) / nk)
                while pend:
                    mv = values()
                grel[i] = [mv]
                ends[n] = (out[0], out[2], mv, sacc[0][0])

            def divide(n):
                i = n % 2
                so, sr, mv, sacc = ends[n]
                s, w, r = RB.get()
                for h in range(2):
                    m = pe(lambda e, h=h: e.matmul(s[64 * h:64 * h + 64, :], ONES, SA[i][:, h, :],
                                                   start=True, stop=True), sacc, t_one, *w)
                rb, rw, rr = K32.get()
                o = dve(lambda e: e.reciprocal(rb, s), m, *rw)
                RB.done(r, o)
                o = dve(lambda e: e.tensor_tensor(OT[i], so, rb, ALU.mult), o, mv, *orel[i])
                RO.done(sr, o)
                K32.done(rr, o)
                ends[n] = o

            def output(n):
                p, b = steps[n]
                i = n % 2
                wo = WR[p % 2][:, 1024:1280]
                for t in range(4):
                    s, w, r = RB.get()
                    m = pe(lambda e, s=s, t=t: e.matmul(s[:, 0:256], OT[i][:, 128 * t:128 * t + 128], wo,
                                                        start=True, stop=True), w_raw[p], ends[n], *w)
                    xt[4 * b + t] = dve(lambda e, s=s, t=t: e.tensor_tensor(
                        X[:, 4 * b + t, :], X[:, 4 * b + t, :], s[:, 0:256], ALU.add), m, xt[4 * b + t])
                    RB.done(r, xt[4 * b + t])
                orel[i] = [m]
                if b == 1:
                    raw_rel[p % 2] = [m, *w_t[p]]
                    if p + 2 < npair:
                        wload(p + 2)
                return m

            RO = Ring(RB4.bufs[0:1])
            RB = Ring(RB4.bufs[1:4])
            RO.rel, RB.rel = RB4.rel[0:1], RB4.rel[1:4]
            ends = {}
            mxrel = [list(free)]

            def side(n):
                if n:
                    divide(n - 1)
                    yield 0.5
                g = prepare(n + 1)
                for x in range(2):
                    yield next(g, 0.0)
                if n:
                    output(n - 1)
                    yield 1.0
                yield from g

            def prepare(n):
                if n < len(steps):
                    yield from proj(n)
                    if own:
                        yield from rowmax(n)

            total = Work(prepare(0), 0.0).rest() + 1.5
            for n in range(len(steps)):
                work = Work(side(n), total)
                attend(n, work)
                work.rest()
            divide(n)
            last = output(n)
            RB4.rel = RO.rel + RB.rel
            return [last, xt[3], xt[7]]

        C16 = pairview(24448, 4096, "p (k n) -> p k n", k=2)

        def attention16(layer, lat_t, lat_free, ctx_t, free):
            causal = layer == 2
            S = 512 if causal else 1024
            nk = S // P
            KS = [rview(4096 + 4096 * i, 4096, "p (h n) -> p h n", h=4) for i in range(2)]
            QS = [rview(12288 + 2048 * i, 2048, "p (h n) -> p h n", h=4) for i in range(2)]
            KHL = pairview(16384, 1024)
            QHL = pairview(18432, 512)
            QM = rview(19456, 512)
            W = pairview(19968, 1024)
            WV = pairview(8192, 512, "p (k n) -> p k n", k=2)
            PT = Ring([view(5120 + 1024 * i, 1024, "p (h n) -> p h n", h=2) for i in range(4)])
            VA = view(9216, 4096, "p (t h c) -> p t h c", h=16, c=32)
            NMT = view(13312, 512, "p (t c) -> p t c", t=4)
            OU = view(13824, 512)
            QZ = rview(22016, 2048, "p (h n) -> p h n", h=4)
            RC = view(3584, 512)
            COS, SIN = view(16384, 1024), view(17408, 1024)
            WR = view(18432, 1024)
            WO = [view(19456 + 256 * i, 256) for i in range(2)]
            TM = view(2048, 1024, "p (h n) -> p h n", h=2)
            TRI, SEL, BV = view(3072, 128), view(3200, 128), view(3328, 256)
            tt = load("tab", view(16384, 2048), T["l3_tab"], *free)
            bt = load("bv", BV, T["bc"][:, 512:768], *free, *lat_free)
            st = load("sel", SEL, T["sel"], *free, *lat_free)
            z2 = pool(lambda e: e.memset(VA, 0.0), *free)
            z2 = pool(lambda e: e.memset(VA[:, :, :, 16:17], 1.0), z2)
            z3 = pool(lambda e: e.memset(NMT, 0.0), *free)
            z5 = pool(lambda e: e.memset(f32(QZ), 0.0), *free)
            z4 = pool(lambda e: e.memset(TRI, 0.0), *free, *lat_free)
            z4 = pool(lambda e: e.affine_select(out=TRI, in_=TRI, compare_op=ALU.is_ge, fill=NEG, base=0,
                                                pattern=[[-1, P]], channel_multiplier=1), z4)
            steps = [(b, g) for b in range(B) for g in range(4)]
            wrel, raw_rel = list(free), list(free)
            wo_rel = [list(free), list(free)]
            wo_t, kq_t, qm_t, staged, ends = {}, {}, {}, {}, {}
            srel = [list(free), list(free)]
            krel, qrel, tmrel = list(free), list(free), [*free, *lat_free]
            ourel, zrel = list(free), [z5]
            vt, mx, last_att = {}, {}, [None]
            vrel, rcrel = list(free), []

            def move(i, dst, src, src_t, name):
                for n, x in src:
                    for j in range(4):
                        t = q.dma(f"{name}{i}", lambda e, j=j, n=n, x=x: e.dma_start(
                            f32(dst[32 * n:32 * n + 32, j, :]), f32(x[32 * j:32 * j + 32, :])), src_t)
                return t

            def wload(n):
                if n < len(steps):
                    w_raw[n] = load("w16", WR, T[f"l{layer}_w"][steps[n][1]], *raw_rel)

            def wsplit(n):
                nonlocal raw_rel
                if n < len(steps):
                    w_t[n] = split(W, WR, [w_raw[n]], wrel, pool)
                    raw_rel = list(w_t[n])
                    wload(n + 1)

            w_raw, w_t = {}, {}

            def proj(n):
                nonlocal wrel, qrel, zrel
                b, g = steps[n]
                wt = w_t[n]

                def project(out, j, src, c0, waits):
                    for k in range(2):
                        m = mm3(out, [x[:, 256 * j + 128 * k:256 * j + 128 * k + 128] for x in W],
                                [x[:, k, c0:c0 + 512] for x in src], k == 0, k == 1, [*wt, *waits])
                    return m

                def rows(which, c0, src, src_t, cos0, bias, dst, rel):
                    nonlocal tmrel
                    s, w, r = RA.get()
                    for j in range(1 if causal else 2):
                        m = project(s[:, 512 * j:512 * j + 512], which + j, src, c0, [*src_t, *w])
                    if causal:
                        a = dve(lambda e: e.tensor_scalar(TM[:, 0, :], s[:, 0:512], bias, None, ALU.add),
                                m, t_vec, *tmrel)
                        RA.done(r, a)
                    else:
                        one = ONE16 if which == 2 else 0.0
                        dve(lambda e: e.scalar_tensor_tensor(
                            out=TM[:, 0, :], in0=s[:, 0:512], scalar=one, in1=COS[:, cos0:cos0 + 512],
                            op0=ALU.add, op1=ALU.mult), m, tt, t_vec, *tmrel)
                        a = dve(lambda e: e.tensor_tensor(
                            TM[:, 1, :], s[:, 512:1024], SIN[:, cos0:cos0 + 512], ALU.mult))
                        RA.done(r, a)
                        a = pool(lambda e: e.tensor_tensor(TM[:, 0, :], TM[:, 0, :], TM[:, 1, :], ALU.add), a)
                    h, o = split(dst, TM[:, 0, :], [a], rel, pool)
                    tmrel = [h, o]
                    return m, [h, o]

                kt = []
                for c in range(S // 512):
                    m, o = rows(2, 1024 * b + 512 * c, C16, ctx_t, 512 * c, BK[:, g:g + 1],
                                [x[:, 512 * c:512 * c + 512] for x in KHL], krel)
                    kt += o
                    yield 1.3
                m, qt = rows(0, 512 * b, XNT, lat_t, 0, BQ[:, g:g + 1], QHL, qrel)
                for j in range(4):
                    z = dve(lambda e, j=j: e.tensor_copy(
                        QZ[32 * j:32 * j + 32, j, :], QHL[0][32 * j:32 * j + 32, :]), *qt, *zrel)
                wrel, qrel = [m], [z]
                staged[n] = (kt, qt, z)
                yield 1.3

            def load_out(n):
                if n < len(steps):
                    wo_t[n] = load(f"wo{n % 2}", WO[n % 2], T[f"l{layer}_wo"][steps[n][1]], *wo_rel[n % 2])

            def place(n):
                nonlocal krel, qrel
                i = n % 2
                kt, qt, _ = staged[n]
                k = [x[:, 0:S] for x in KHL]
                t1 = move(i, KS[i][:, :, 0:S], enumerate((k[0], k[1], k[0])), [*kt, *srel[i]], "mk")
                t2 = move(i, QS[i], ((1, QHL[0]), (2, QHL[1])), [*qt, *srel[i]], "mq")
                krel, qrel = [t1], [*qrel, t2]
                kq_t[n] = [t1, t2]

            wv_t = {}

            def values_weight(b, *free_t):
                wv_t[b] = load("wv", RC, T[f"l{layer}_wv"], *free_t)

            def project_values(b):
                nonlocal rcrel
                wvt = split([x.rearrange("p k n -> p (k n)") for x in WV], RC, [wv_t[b]], srel[1])
                rcrel = list(wvt)
                for t in range(nk):
                    s, w, r = RB.get()
                    for k in range(2):
                        c0 = 1024 * b + 128 * t
                        m = mm3(s[:, 0:256], [x[:, k, c0:c0 + 128] for x in C16], [x[:, k, :] for x in WV],
                                k == 0, k == 1, [*wvt, *ctx_t, *w])
                    dst = VA[:, t, :, 0:16]
                    src = s[:, 0:256].rearrange("p (h c) -> p h c", c=16)
                    if causal:
                        o = dve(lambda e, dst=dst, src=src: e.tensor_tensor(
                            dst, src, BV.rearrange("p (h c) -> p h c", c=16), ALU.add), m, bt, z2, *vrel)
                    else:
                        o = act(lambda e, dst=dst, src=src: e.activation(dst, src, ACT.Copy), m, z2, *vrel)
                    RB.done(r, o)
                srel[1] = [m]
                vt[b] = o

            mtrel = [z3]

            def rowmax(n):
                nonlocal krel, zrel
                kt, qt, z = staged[n]
                for j in range(4):
                    for t in range(4):
                        kn = 128 * (t + 1) if causal else 1024
                        s, w, r = RA.get()
                        for u in range(0, kn, 512):
                            c = min(512, kn - u)
                            m = pe(lambda e, s=s, j=j, t=t, u=u, c=c: e.matmul(
                                s[:, u:u + c], QZ[:, j, 128 * t:128 * t + 128], KHL[0][:, u:u + c],
                                start=True, stop=True), *kt, z, *w)
                        o = m
                        if causal:
                            o = dve(lambda e, s=s, t=t: e.tensor_tensor(
                                s[:, 128 * t:128 * t + 128], s[:, 128 * t:128 * t + 128], TRI, ALU.add), m, z4)
                        o = dve(lambda e, s=s, t=t, j=j, kn=kn: e.tensor_reduce(
                            NMT[:, t, 32 * j + 16:32 * j + 17], s[:, 0:kn], AX.X, ALU.max, negate=True),
                            o, *mtrel)
                        RA.done(r, o)
                        yield kn / 900
                krel, zrel = [*krel, m], [m]
                mx[n] = o

            def shift(n):
                nonlocal qrel, mtrel
                i = n % 2
                s, w, r = RB.get()
                for t in range(4):
                    m = pe(lambda e, s=s, t=t: e.matmul(
                        s[:, 128 * t:128 * t + 128], NMT[:, t, :], ID, start=True, stop=True), mx[n], t_id, *w)
                mtrel = [m]
                o = dve(lambda e, s=s: e.tensor_tensor(QM, f32(QHL[0]), s, ALU.add), m, *qmrel[0])
                RB.done(r, o)
                t = move(i, QS[i], ((0, QM),), [o, *srel[i]], "mm")
                qmrel[0] = [t]
                qrel = [*qrel, o]
                qm_t[n] = [t, *kq_t[n]]

            qmrel = [list(free)]

            def attend(n, work):
                b, g = steps[n]
                i = n % 2
                so, sw, sr = RO.get()
                pend = []

                def values():
                    kt, pts = pend.pop(0)
                    q0 = 128 * kt if causal else 0
                    for j in range(4):
                        pt, tp, pr = pts[j // 2]
                        m = pe(lambda e, j=j, pt=pt: e.matmul(
                            so[32 * j:32 * j + 32, q0:512], VA[:, kt, 4 * g + j, :], pt[:, j % 2, q0:512],
                            start=(kt == 0), stop=(kt == nk - 1), skip_group_check=True), tp, vt[b], *sw)
                    for pt, tp, pr in pts:
                        PT.done(pr, m)
                    return m

                for kt in range(nk):
                    q0 = 128 * kt if causal else 0
                    pts = []
                    for jj in range(2):
                        s, w, r = RA.get()
                        for h in range(2):
                            j = 2 * jj + h
                            m = pe(lambda e, s=s, j=j, h=h, kt=kt, q0=q0: e.matmul(
                                s[:, 512 * h + q0:512 * h + 512], KS[i][0:96, j, 128 * kt:128 * kt + 128],
                                QS[i][0:96, j, q0:512], start=True, stop=True), *qm_t[n], *w)
                        pt, pw, pr = PT.get()
                        sv = s.rearrange("p (h n) -> p h n", h=2)
                        tp = act(lambda e, sv=sv, pt=pt, q0=q0: e.activation(
                            pt[:, :, q0:512], sv[:, :, q0:512], ACT.Exp, scale=0.25), m, *pw)
                        RA.done(r, tp)
                        if causal:
                            d = pt[:, :, q0:q0 + 128]
                            tp = pool(lambda e, d=d: e.affine_select(
                                out=d, in_=d, compare_op=ALU.is_ge, fill=0.0, base=0,
                                pattern=[[0, 2], [1, P]], channel_multiplier=-1), tp)
                        pts.append((pt, tp, pr))
                        work.upto((2 * kt + jj + 1) / (2 * nk - 1))
                    pend.append((kt, pts))
                    if len(pend) > 1:
                        values()
                m = values()
                srel[i] = [m]
                last_att[0] = m
                c1 = act(lambda e: e.activation(OU, so, ACT.Copy), m, *ourel)
                RO.done(sr, c1)
                ends[n] = c1

            def divide(n):
                s, w, r = RB.get()
                m = pe(lambda e: e.matmul(s, SEL, OU, start=True, stop=True), ends[n], st, *w)
                o = dve(lambda e: e.reciprocal(RC, s), m, *rcrel)
                RB.done(r, o)
                ends[n] = dve(lambda e: e.tensor_tensor(OU, OU, RC, ALU.mult), o)

            def output(n):
                nonlocal ourel
                b, g = steps[n]
                i = n % 2
                for t in range(4):
                    s, w, r = RB.get()
                    m = pe(lambda e, s=s, t=t: e.matmul(s[:, 0:256], OU[:, 128 * t:128 * t + 128], WO[i],
                                                        start=True, stop=True), wo_t[n], ends[n], *w)
                    x = 4 * b + t
                    xt[x] = dve(lambda e, s=s, x=x: e.tensor_tensor(X[:, x, :], X[:, x, :], s[:, 0:256], ALU.add),
                                m, xt[x])
                    RB.done(r, xt[x])
                ourel = [m]
                wo_rel[i] = [m]
                return m

            def side(n):
                if n + 1 < len(steps):
                    place(n + 1)
                    wsplit(n + 2)
                yield 1.0
                if n:
                    divide(n - 1)
                    yield 1.0
                if n + 1 < len(steps):
                    if steps[n + 1][0] != steps[n][0]:
                        values_weight(steps[n + 1][0], ends[n - 1])
                    for x, w in enumerate(rowmax(n + 1)):
                        yield w
                        if n and x == 1:
                            output(n - 1)
                            load_out(n + 1)
                            yield 0.5
                    shift(n + 1)
                    yield 0.5
                    if n + 2 < len(steps):
                        yield from proj(n + 2)
                elif n:
                    output(n - 1)

            RO = Ring(RB4.bufs[0:1])
            RB = Ring(RB4.bufs[1:4])
            RO.rel, RB.rel = RB4.rel[0:1], RB4.rel[1:4]
            wload(0)
            wsplit(0)
            load_out(0)
            load_out(1)
            total = 2.5 + Work(proj(0), 0.0).rest()
            place(0)
            values_weight(0, *free, *lat_free)
            project_values(0)
            total += Work(rowmax(0), 0.0).rest()
            shift(0)
            wsplit(1)
            Work(proj(1), 0.0).rest()
            for n in range(len(steps)):
                b = steps[n][0]
                if b != steps[max(n - 1, 0)][0]:
                    vrel = [last_att[0]]
                    project_values(b)
                work = Work(side(n), total)
                attend(n, work)
                work.rest()
            divide(n)
            m = output(n)
            RB4.rel = RO.rel + RB.rel
            return [m, xt[3], xt[7]]

        def bc(ap):
            return ap.unsqueeze(2).to_broadcast([P, NT, 8])

        def logits(src, raw, src_t, free, bias=None, bias_t=None):
            wt = split([x.rearrange("p k e -> p (k e)") for x in RWS], RW, [raw], free)
            s, w, r = RB.get()
            for i in range(NT):
                for k in range(2):
                    m = mm3(s[:, 8 * i:8 * i + 8], [x[:, k, 128 * i:128 * i + 128] for x in src],
                            [x[:, k, :] for x in RWS], k == 0, k == 1, [*wt, *src_t, *w])
            sv = s[:, 0:64].rearrange("p (t e) -> p t e", e=8)
            o = dve(lambda e: e.tensor_copy(LG, sv), m)
            o2 = o
            if bias is not None:
                o2 = dve(lambda e: e.tensor_tensor(LB, LG, bias, ALU.add), o, bias_t)
            RB.done(r, o)
            return o, o2

        def top(src, oh, mx, tk):
            o = dve(lambda e: e.tensor_reduce(mx, src, AX.X, ALU.max), tk)
            o = dve(lambda e: e.tensor_tensor(oh, src, bc(mx), ALU.is_equal), o)
            o = dve(lambda e: e.tensor_tensor(oh, oh, REV, ALU.mult), o, t_rev)
            o = dve(lambda e: e.tensor_reduce(RT[:, 7, :], oh, AX.X, ALU.max), o)
            return dve(lambda e: e.tensor_tensor(oh, oh, bc(RT[:, 7, :]), ALU.is_equal), o)

        def second(src, tk):
            o = dve(lambda e: e.scalar_tensor_tensor(
                out=LB.rearrange("p t e -> p (t e)"), in0=OH1.rearrange("p t e -> p (t e)"), scalar=NEG,
                in1=src.rearrange("p t e -> p (t e)"), op0=ALU.mult, op1=ALU.add), tk)
            return top(LB, OH2, RT[:, 1, :], o)

        def pair_gates(tk):
            o = dve(lambda e: e.tensor_tensor(RT[:, 2, :], RT[:, 1, :], RT[:, 0, :], ALU.subtract), tk)
            o = act(lambda e: e.activation(RT[:, 3, :], RT[:, 2, :], ACT.Exp), o)
            o2 = act(lambda e: e.activation(RT[:, 4, :], RT[:, 2, :], ACT.Exp, scale=-1.0), o)
            o = dve(lambda e: e.tensor_scalar(RT[:, 3:5, :], RT[:, 3:5, :], 1.0, None, ALU.add), o2)
            o = dve(lambda e: e.reciprocal(RT[:, 5:7, :], RT[:, 3:5, :]), o)
            o1 = dve(lambda e: e.tensor_tensor(OH1, OH1, bc(RT[:, 5, :]), ALU.mult), o)
            o2 = dve(lambda e: e.tensor_tensor(OH2, OH2, bc(RT[:, 6, :]), ALU.mult), o)
            return dve(lambda e: e.tensor_tensor(GATE, OH1, OH2, ALU.add), o2)

        EX = 11264

        def experts(layer, nf, jobs, free, consume):
            glu = layer != 2
            up_n = 512 if glu else 256
            cn = up_n + 256
            RAW = Ring([view(5120 + 768 * i, cn) for i in range(4)])
            WS = Ring([pairview(8192 + 1536 * i, cn) for i in range(4)])
            HS = Ring([pairview(14336 + 1024 * i, 512) for i in range(4)])
            H32 = Ring([view(8192 + 512 * i, 512) for i in range(3)])
            SG = Ring([view(9728 + 512 * i, 512) for i in range(3)])
            for ring in (RAW, WS, HS, H32, SG):
                for i in range(len(ring.bufs)):
                    ring.done(i, *free)
            yrel = [list(x) for x in RB.rel]
            units = [(j, f) for j in range(len(jobs)) for f in range(nf)]
            pieces = {}
            held = []

            def fetch(u):
                j, f = units[u]
                raw, w, r = RAW.get()
                t = load(f"fw{r}", raw, jobs[j][0](f), *w)
                ws, w, rs = WS.get()
                wt = split(ws, raw, [t], w, pool)
                RAW.done(r, *wt)
                pieces[u] = (ws, wt, rs)

            def hidden(src, tk):
                hs, w, r = HS.get()
                return hs, split(hs, src, tk, w), r

            def up(u, c):
                j, f = units[u]
                _, src, st = jobs[j]
                ws, wt, _ = pieces[u]
                s, w, r = RA.get()
                for z in range(2 if glu else 1):
                    for k in range(2):
                        o0 = 256 * z + 128 * k
                        m = mm3(s[:, 512 * z:512 * z + 512], [x[:, o0:o0 + 128] for x in ws],
                                [x[:, k, 512 * c:512 * c + 512] for x in src], k == 0, k == 1, [*wt, *st, *w])
                h, hw, hr = H32.get()
                if glu:
                    sg, gw, gr = SG.get()
                    a = act(lambda e: e.activation(sg, s[:, 0:512], ACT.Silu), m, *gw)
                    o = dve(lambda e: e.tensor_tensor(h, sg, s[:, 512:1024], ALU.mult), a, *hw)
                    SG.done(gr, o)
                else:
                    o = dve(lambda e: e.tensor_scalar(h, s[:, 0:512], 0.0, None, ALU.max), m, *hw)
                RA.done(r, o)
                hs, ht, hsr = hidden(h, [o])
                H32.done(hr, *ht)
                return u, c, hs, ht, hsr

            def down(u, c, hs, ht, hsr):
                j, f = units[u]
                ws, wt, rs = pieces[u]
                wd = [x[:, up_n:cn] for x in ws]
                for t in range(4):
                    bk = 2 * c + t // 2
                    y = PS[:, 2048 + 512 * bk + 256 * (t % 2):2048 + 512 * bk + 256 * (t % 2) + 256]
                    m = mm3(y, [x[:, 128 * t:128 * t + 128] for x in hs], wd, f == 0 and t % 2 == 0, f == nf - 1,
                            [*ht, *(yrel[bk] if f == 0 else ())], skip=True)
                    held.append((4 * c + t, y))
                    if t % 2:
                        for t_, y_ in held:
                            if f == nf - 1:
                                consume(j, t_, y_, m, yrel)
                        held.clear()
                HS.done(hsr, m)
                if c == 1:
                    WS.done(rs, m)
                return m

            for u in range(min(3, len(units))):
                fetch(u)
            prev = None
            for u in range(len(units)):
                for c in range(2):
                    cur = up(u, c)
                    if prev is not None:
                        m = down(*prev)
                    prev = cur
                if u + 3 < len(units):
                    fetch(u + 3)
            m = down(*prev)
            for i in range(4):
                RB.done(i, *yrel[i])
            return m

        def add_gated(gate, gate_t):
            def consume(j, t, s, m, yrel):
                g = gate(j, t)
                if g is None:
                    o = dve(lambda e: e.tensor_tensor(X[:, t, :], X[:, t, :], s, ALU.add), m, xt[t])
                else:
                    o = dve(lambda e: e.scalar_tensor_tensor(
                        out=X[:, t, :], in0=s, scalar=g, in1=X[:, t, :], op0=ALU.mult, op1=ALU.add),
                        m, xt[t], gate_t)
                xt[t] = o
                yrel[t // 2] = [o]
            return consume

        RW = small(16)
        BCR = small(64, "p (t e) -> p t e", e=8)
        RWS = pairview(20480, 16, "p (k e) -> p k e", k=2)
        BIAS = view(20032, 256)

        def finish(free):
            o = OUT.rearrange("b (t p) d -> p (b t) d", p=P)
            f = q.dma("out", lambda e: e.dma_start(o, X), list(xt) + list(free))
            q.add("sync", lambda e: e.nop(), [f])
            q.emit()

        def add_bias(col, n_t, free):
            t = load("bias", BIAS, T["bc"][:, col:col + 256], *free)
            for i in range(NT):
                xt[i] = pool(lambda e, i=i: e.tensor_tensor(X[:, i, :], X[:, i, :], BIAS, ALU.add),
                             t, n_t[i], xt[i])
            return [xt[NT - 1]]

        def context(gain, free):
            out = []
            for hb in range(B):
                a = view(5120 + 2048 * hb, 2048, "p (t d) -> p t d", d=D)
                ld = load(f"ctx{hb}", a, T["ctx"][hb].rearrange("(t p) d -> p t d", p=P), *free)
                nt = norm(a, a, 8, EPS, [ld] * 8, [*free, *out[-2:]])
                o, m = turn(a, [x[:, :, 1024 * hb:1024 * hb + 1024] for x in C64], 8, nt, free, gain, K32)
                out += o
            return out, m

        nt = norm(X, XN, NT, EPS, xt, [])
        add_bias(0, nt, [])
        nt2 = norm(XN, XN, NT, EPS, nt, [nt[-1]])
        lat, lpe = turn(XN, XNT, NT, nt2, [], (vec(V_LATG), vec(V_LATB)), K32)
        ct, hpe = context((vec(V_CTXG), vec(V_CTXB)), [nt2[-1]])
        tab = load("tab", TB, T["l0_tab"])
        tab = dve(lambda e: e.tensor_scalar(TB[:, 1024:2048], TB[:, 1024:2048], SGN, None, ALU.mult), tab, t_vec)
        fr = attention64(0, lat, [lpe], ct, [tab], [hpe])
        if stop == 1:
            finish(fr)
            return

        def pre_ffn(fr, rw):
            nt = norm(X, XN, NT, EPS, xt, fr)
            lat, lpe = turn(XN, XNT, NT, nt, fr)
            w = load("rw", RW, rw, *fr)
            return lat, lpe, w

        lat, lpe, w = pre_ffn(fr, T["l0_rw"])
        bt = load("rb", BCR, T["bc"][:, 1536:1600].rearrange("p (t e) -> p t e", e=8))
        o, o2 = logits(XNT, w, lat, fr, BCR, bt)
        o = top(LB, OH1, RT[:, 0, :], o2)
        o = dve(lambda e: e.tensor_tensor(LB, LB, bc(RT[:, 0, :]), ALU.subtract), o)
        o = act(lambda e: e.activation(LB, LB, ACT.Exp), o)
        o = dve(lambda e: e.tensor_reduce(RT[:, 1, :], LB, AX.X, ALU.add), o)
        o = dve(lambda e: e.reciprocal(RT[:, 2, :], RT[:, 1, :]), o)
        gt = dve(lambda e: e.tensor_tensor(GATE, OH1, bc(RT[:, 2, :]), ALU.mult), o)
        m = experts(0, 8, [(lambda f, x=x: T["l0_ffn"][x, f], XNT, lat) for x in range(8)], fr,
                    add_gated(lambda j, t: GATE[:, t, j:j + 1], gt))
        fr = [m] + xt
        if stop == 2:
            finish(fr)
            return

        nt = norm(X, XN, NT, EPS, xt, fr)
        nt2 = norm(XN, XN, NT, EPS, nt, [nt[-1]])
        lat, lpe = turn(XN, XNT, NT, nt2, fr, (vec(V_GL), vec(V_BL)), K32)
        ct, hpe = context((vec(V_GX), vec(V_BX)), [*fr, nt2[-1]])
        tab = load("tab", TB, T["l1_tab"], *fr)
        fr = attention64(1, lat, [lpe], ct, [tab], [*fr, hpe])
        if stop == 3:
            finish(fr)
            return

        lat, lpe, w = pre_ffn(fr, T["l1_rw"])
        o, _ = logits(XNT, w, lat, fr)
        o = top(LG, OH1, RT[:, 0, :], o)
        o = act(lambda e: e.activation(RT[:, 1, :], RT[:, 0, :], ACT.Exp, scale=-1.0), o)
        o = dve(lambda e: e.tensor_scalar(RT[:, 1, :], RT[:, 1, :], 1.0, None, ALU.add), o)
        o = dve(lambda e: e.reciprocal(RT[:, 2, :], RT[:, 1, :]), o)
        ns = [dve(lambda e, i=i: e.tensor_scalar(XN[:, i, :], XN[:, i, :], RT[:, 2, i:i + 1], None, ALU.mult), o, lpe)
              for i in range(NT)]
        XST = pairview(4096, 2048, "p (k n) -> p k n", k=2)
        lats, lpe = turn(XN, XST, NT, ns, fr)
        m = experts(1, 4, [(lambda f: T["l1_shared"][f], XNT, lat)] +
                    [(lambda f, x=x: T["l1_ffn"][x, f], XST, lats) for x in range(8)], fr,
                    add_gated(lambda j, t: OH1[:, t, j - 1:j] if j else None, o))
        fr = [m] + xt
        if stop == 4:
            finish(fr)
            return

        ctr, rel = [], fr
        for hb in range(B):
            a = view(5120, 2048)
            ld = load("ctxT", a, T["ctxT"][hb], *rel)
            rel = split([x[:, :, 1024 * hb:1024 * hb + 1024] for x in C16],
                        a.rearrange("p (k n) -> p k n", k=2), [ld], fr)
            ctr += rel
        nt = norm(X, XN, NT, EPS, xt, fr)
        add_bias(256, nt, fr)
        lat, lpe = turn(XN, XNT, NT, nt, fr)
        fr = attention16(2, lat, [lpe], ctr, [*fr, *ctr])
        if stop == 5:
            finish(fr)
            return

        lat, lpe, w = pre_ffn(fr, T["l2_rw"])
        o, _ = logits(XNT, w, lat, fr)
        o = top(LG, OH1, RT[:, 0, :], o)
        o = second(LG, o)
        gt = pair_gates(o)
        m = experts(2, 8, [(lambda f, x=x: T["l2_ffn"][x, f], XNT, lat) for x in range(8)], fr,
                    add_gated(lambda j, t: GATE[:, t, j:j + 1], gt))
        fr = [m] + xt
        if stop == 6:
            finish(fr)
            return

        nt = norm(X, XN, NT, EPS, xt, fr)
        add_bias(768, nt, fr)
        lat, lpe = turn(XN, XNT, NT, nt, fr)
        fr = attention16(3, lat, [lpe], ctr, fr)
        if stop == 7:
            finish(fr)
            return

        nt = norm(X, XN, NT, EPS, xt, fr)
        lat, lpe = turn(XN, XNT, NT, nt, fr)
        WIO = view(EX, 1024)
        WIOS = pairview(18432, 1024, "p (a k n) -> p a k n", a=2, k=2)
        NW = view(EX + 1024, 512, "p (a n) -> p a n", a=2)
        EN = view(EX + 1536, 2048, "p (e n) -> p e n", n=256)
        ACC = view(EX + 3584, 2048, "p (t n) -> p t n", n=256)
        JK = [view(EX + 5632 + 256 * i, 256) for i in range(2)]
        TM = Ring([view(EX + 6144 + 256 * i, 256) for i in range(4)])
        wio = load("wio", WIO, T["l3_wio"], *fr)
        wios = split([x.rearrange("p a k n -> p (a k n)") for x in WIOS], WIO, [wio], fr)
        nwt = load("nw", NW.rearrange("p a n -> p (a n)"), T["bc"][:, 1024:1536], *fr)
        ent = load("en", EN.rearrange("p e n -> p (e n)"), T["bc"][:, 1664:3712], *fr)
        w = load("rw", RW, T["l3_rw"], *fr)
        bt = load("rb", BCR, T["bc"][:, 1600:1664].rearrange("p (t e) -> p t e", e=8), *fr)

        def tokens(out, i, src, ww, waits):
            for k in range(2):
                m = mm3(out, [x[:, k, 128 * i:128 * i + 128] for x in src], [x[:, ww, k, :] for x in WIOS],
                        k == 0, k == 1, waits)
            return m

        def rms(src, i, col, tk, rel):
            return act(lambda e: e.activation(JK[i % 2], src, ACT.Square, accum_out=col), tk, *rel)

        def rsq(dst, src, tk):
            o = pool(lambda e: e.tensor_scalar(src, src, 1.0 / D, EPS3, ALU.mult, ALU.add), *tk)
            return pool(lambda e: e.tensor_tensor(dst, src, MHALF[:, 0:src.shape[1]], ALU.pow), o)

        ht_, jrel, pss = [], [[], []], []
        for i in range(NT):
            s, w_, r = RB.get()
            m = tokens(s[:, 0:256], i, XNT, 0, [*wios, *lat, *w_])
            a = dve(lambda e, s=s, i=i: e.tensor_copy(XN[:, i, :], s[:, 0:256]), m, lpe)
            RB.done(r, a)
            o = rms(XN[:, i, :], i, VE[:, i:i + 1], a, jrel[i % 2])
            jrel[i % 2] = [o]
        o = rsq(RS[:, 0:8], VE[:, 0:8], [o])
        hn = [dve(lambda e, i=i: e.scalar_tensor_tensor(out=XN[:, i, :], in0=XN[:, i, :], scalar=RS[:, i:i + 1],
                                                        in1=NW[:, 0, :], op0=ALU.mult, op1=ALU.mult), o, nwt)
              for i in range(NT)]
        lat, lpe = turn(XN, XNT, NT, hn, [m])
        o, o2 = logits(XNT, w, lat, fr, BCR, bt)
        o = top(LB, OH1, RT[:, 0, :], o2)
        o = second(LB, o)
        for n, oh in enumerate((OH1, OH2)):
            o = dve(lambda e, oh=oh: e.tensor_tensor(LB, oh, LG, ALU.mult), o)
            o = dve(lambda e, n=n: e.tensor_reduce(RT[:, n, :], LB, AX.X, ALU.add), o)
        gt = pair_gates(o)
        hold = []
        msrel = [[], []]
        acct = [None] * NT

        def consume(j, t, s, m, yrel):
            hold.append((t, s, m, t // 2))
            if len(hold) < 4:
                return
            u = (2 * j + t // 4) % 2
            ms, grr = MS[:, u, :], GR[:, u, :]
            for n, (t_, s_, m_, r_) in enumerate(hold):
                o = rms(s_, n, ms[:, n:n + 1], m_, jrel[n % 2] + msrel[u])
                jrel[n % 2] = [o]
            o = rsq(grr, ms, [o] + msrel[u])
            t0 = hold[0][0]
            o = pool(lambda e: e.tensor_tensor(grr, grr, GATE[:, t0:t0 + 4, j], ALU.mult), o, gt)
            for n, (t_, s_, m_, r_) in enumerate(hold):
                if j == 0:
                    d = dve(lambda e, s_=s_, n=n, t_=t_: e.scalar_tensor_tensor(
                        out=ACC[:, t_, :], in0=s_, scalar=grr[:, n:n + 1], in1=EN[:, j, :], op0=ALU.mult,
                        op1=ALU.mult), o, ent)
                    acct[t_] = d
                else:
                    tm, tw, tr = TM.get()
                    d = dve(lambda e, s_=s_, n=n, tm=tm: e.scalar_tensor_tensor(
                        out=tm, in0=s_, scalar=grr[:, n:n + 1], in1=EN[:, j, :], op0=ALU.mult, op1=ALU.mult),
                        o, ent, *tw)
                    acct[t_] = pool(lambda e, t_=t_, tm=tm: e.tensor_tensor(
                        ACC[:, t_, :], ACC[:, t_, :], tm, ALU.add), d, acct[t_])
                    TM.done(tr, acct[t_])
                yrel[r_] = [d]
            msrel[u] = [d]
            hold.clear()

        m = experts(3, 8, [(lambda f, x=x: T["l3_ffn"][x, f], XNT, lat) for x in range(8)], fr, consume)
        for i in range(NT):
            o = rms(ACC[:, i, :], i, VE[:, i:i + 1], acct[i], jrel[i % 2])
            jrel[i % 2] = [o]
        o = rsq(RS[:, 0:8], VE[:, 0:8], [o])
        hn = [dve(lambda e, i=i: e.scalar_tensor_tensor(out=XN[:, i, :], in0=ACC[:, i, :], scalar=RS[:, i:i + 1],
                                                        in1=NW[:, 1, :], op0=ALU.mult, op1=ALU.mult), o, lpe)
              for i in range(NT)]
        lat, lpe = turn(XN, XNT, NT, hn, [m])
        for i in range(NT):
            s, w_, r = RB.get()
            m = tokens(s[:, 0:256], i, XNT, 1, [*lat, *w_])
            xt[i] = dve(lambda e, s=s, i=i: e.tensor_tensor(X[:, i, :], X[:, i, :], s[:, 0:256], ALU.add), m, xt[i])
            RB.done(r, xt[i])
        finish([])


def rope_table(n, d, slot, copies):
    inv = (np.float32(1.0) / np.float32(10000.0) ** (np.arange(0, d, 2, dtype=np.float32) / np.float32(d)))
    ang = (np.arange(n, dtype=np.float32)[:, None] * inv.astype(np.float32)[None, :]).astype(np.float32)
    c, s = np.cos(ang).astype(np.float32).T, np.sin(ang).astype(np.float32).T
    cos, sin = np.zeros((copies, slot, n), np.float32), np.zeros((copies, slot, n), np.float32)
    h = d // 2
    cos[:, d:] = 1.0
    cos[:, 0:h], cos[:, h:d], sin[:, 0:h], sin[:, h:d] = c, c, -s, s
    return np.concatenate([cos.reshape(-1, n), sin.reshape(-1, n)], axis=1)


def layout(a):
    def f(n):
        return np.asarray(a[n])

    def rows(w):
        k = w.shape[0] // P
        return w.reshape(k, P, -1).transpose(1, 0, 2).reshape(P, -1)

    def swap(w, d):
        v = w.reshape(w.shape[0], -1, 2, d // 2)
        return np.concatenate([v[:, :, 1], v[:, :, 0]], axis=2).reshape(w.shape)

    def slots(w):
        o = np.zeros((w.shape[0], 16, 32), np.float32)
        o[:, :, 0:16] = w.reshape(w.shape[0], 16, 16)
        return o.reshape(w.shape[0], 512)

    T = {"x": f("x"), "ctx": f("ctx_1024")}
    v = np.zeros((P, 26), np.float32)
    for i, n in enumerate(("L0_xattn_ln_lat_g", "L0_xattn_ln_lat_b", "L0_xattn_ln_ctx_g", "L0_xattn_ln_ctx_b",
                           "L1_xattn_gamma_x", "L1_xattn_beta_x", "L1_xattn_gamma_l", "L1_xattn_beta_l")):
        v[:, 2 * i:2 * i + 2] = f(n).reshape(2, P).T
    bkv = f("L2_xattn_bkv")
    v[:, 16:20] = slots(f("L2_xattn_bq")[None]).reshape(4, P).T
    v[:, 20:24] = slots(bkv[None, 0:256]).reshape(4, P).T
    v[16::32, 20:24] = 1.0
    v[:, 24] = np.where(np.arange(P) % 64 < 32, -1.0, 1.0)
    v[16::32, 25] = 1.0
    T["vec"] = v
    T["rev"] = np.broadcast_to(np.tile(np.arange(8, 0, -1, dtype=np.float32), 8), (P, 64))
    row = np.concatenate([f("L0_xattn_bo"), f("L2_xattn_bp"), bkv[256:512], f("L3_xattn_bo"),
                          f("L3_ffn_in_norm_w"), f("L3_ffn_out_norm_w"), np.tile(f("L0_ffn_router_b"), 8),
                          np.tile(f("L3_ffn_expert_bias"), 8), f("L3_ffn_enorm_w").reshape(-1)])
    T["bc"] = np.broadcast_to(row, (P, row.size))
    sel = np.zeros((P, P), np.float32)
    for j in range(4):
        sel[32 * j + 16, 32 * j:32 * j + 32] = 1.0
    T["sel"] = sel
    T["ctxT"] = np.stack([rows(f("ctx_1024")[b].T) for b in range(2)])
    cs = [np.concatenate([f(n).T] * 4) for n in ("L0_xattn_cos", "L0_xattn_sin")]
    T["l0_tab"] = np.concatenate(cs, axis=1)
    T["l1_tab"] = rope_table(1024, 64, 64, 2)
    T["l3_tab"] = rope_table(1024, 16, 32, 4)

    for L, inner in ((0, 1024), (1, 512)):
        wq, wkv, wo = f(f"L{L}_xattn_Wq"), f(f"L{L}_xattn_Wkv"), f(f"L{L}_xattn_Wo")
        wk, wv = wkv[:, 0:inner], wkv[:, inner:]
        wr = swap(wk, 64)
        T[f"l{L}_w"] = np.stack([np.concatenate(
            [rows(w[:, 128 * g:128 * g + 128]) for w in (wq, wk, wr, wv)] + [wo[128 * g:128 * g + 128]],
            axis=1) for g in range(inner // 128)])

    for L, wo in ((2, "L2_xattn_Wp"), (3, "L3_xattn_Wo")):
        wq, wkv = f(f"L{L}_xattn_Wq"), f(f"L{L}_xattn_Wkv")
        wk, wv = wkv[:, 0:256], wkv[:, 256:512]
        parts = [slots(w) for w in (wq, swap(wq, 16), wk, swap(wk, 16))]
        T[f"l{L}_w"] = np.stack([np.concatenate([rows(w[:, 128 * g:128 * g + 128]) for w in parts], axis=1)
                                 for g in range(4)])
        T[f"l{L}_wv"] = rows(wv)
        o = np.zeros((16, 32, D), np.float32)
        o[:, 0:16] = f(wo).reshape(16, 16, D)
        T[f"l{L}_wo"] = o.reshape(4, P, D)

    def pieces(ups, dn):
        n = dn.shape[0] // P
        return np.stack([np.concatenate([rows(w[:, P * i:P * i + P]) for w in ups] + [dn[P * i:P * i + P]], axis=1)
                         for i in range(n)])

    w1, w2 = f("L0_ffn_w1"), f("L0_ffn_w2")
    T["l0_ffn"] = np.stack([pieces((w1[e][:, 0:1024], w1[e][:, 1024:]), w2[e]) for e in range(8)])
    g, u, d = f("L1_ffn_expert_gate"), f("L1_ffn_expert_up"), f("L1_ffn_expert_down")
    T["l1_ffn"] = np.stack([pieces((g[e], u[e]), d[e]) for e in range(8)])
    T["l1_shared"] = pieces((f("L1_ffn_shared_gate"), f("L1_ffn_shared_up")), f("L1_ffn_shared_down"))
    w1, w2 = f("L2_ffn_w1"), f("L2_ffn_w2")
    T["l2_ffn"] = np.stack([pieces((w1[e].T,), w2[e].T) for e in range(8)])
    g, u, d = f("L3_ffn_Wg"), f("L3_ffn_Wu"), f("L3_ffn_Wd")
    T["l3_ffn"] = np.stack([pieces((g[e].T, u[e].T), d[e].T) for e in range(8)])
    T["l3_wio"] = np.concatenate([rows(f("L3_ffn_W_in").T), rows(f("L3_ffn_W_out").T)], axis=1)

    def rw(w):
        return rows(w)

    T["l0_rw"] = rw(f("L0_ffn_router_w"))
    T["l1_rw"] = rw(f("L1_ffn_router_w").T)
    T["l2_rw"] = rw(f("L2_ffn_gate_w").T)
    T["l3_rw"] = rw(f("L3_ffn_Wr").T)
    return {n: np.ascontiguousarray(x) for n, x in T.items()}


def kernel(**inputs):
    import concourse.bacc as _bacc
    from concourse.bass_utils import run_bass_kernel_spmd as _run

    nc = _bacc.Bacc("TRN2", target_bir_lowering=False, num_devices=1)
    arrays = layout(inputs)
    T = {n: nc.dram_tensor(f"in_{n}", x.shape, F32, kind="ExternalInput").ap() for n, x in arrays.items()}
    out = nc.dram_tensor("out_x", (2, 512, 256), F32, kind="ExternalOutput").ap()
    build(nc, T, out)
    r = _run(nc, [{f"in_{n}": x for n, x in arrays.items()}], core_ids=[0])
    return r.results[0]["out_x"]
```

```python
from contextlib import ExitStack

import numpy as np

import concourse.bass as bass
from concourse import mybir

F32 = mybir.dt.float32
F32R = mybir.dt.float32r
I32 = mybir.dt.int32
ALU = mybir.AluOpType
ACT = mybir.ActivationFunctionType
AX = mybir.AxisListType

P = 128
D = 256
NT = 8
B = 2
EPS = 1e-5
EPS3 = float(np.finfo(np.float32).eps)
CLIP_LO = float(np.exp(np.float64(-11.0)))
CLIP_HI = float(np.exp(np.float64(11.0)))
NEG = -1e30
TILE = 256
NF = 20700
NR = 32384


class Tok:

    __slots__ = ("key", "n", "used")

    def __init__(self, key, n):
        self.key, self.n, self.used = key, n, False


class Queues:

    ENGINES = ("tensor", "vector", "scalar", "gpsimd", "sync")

    def __init__(self, nc, ctx):
        self.nc, self.ctx = nc, ctx
        self.ops = {e: [] for e in self.ENGINES}
        self.sems, self.counts = {}, {}

    def add(self, eng, fn, waits):
        t = Tok(eng, len(self.ops[eng]))
        flat = [w for w in waits if w is not None]
        for w in flat:
            w.used = True
        self.ops[eng].append((fn, flat, t, None))
        return t

    def dma(self, name, fn, waits, eng="sync"):
        self.counts[name] = self.counts.get(name, 0) + 16
        t = Tok("d_" + name, self.counts[name])
        flat = [w for w in waits if w is not None]
        for w in flat:
            w.used = True
        self.ops[eng].append((fn, flat, None, "d_" + name))
        return t

    def sem(self, key):
        if key not in self.sems:
            self.sems[key] = self.ctx.enter_context(self.nc.semaphore("s_" + key))
        return self.sems[key]

    def emit(self):
        for e in self.ENGINES:
            n = 0
            for _, _, t, d in self.ops[e]:
                if t is not None and t.used:
                    n += 1
                    t.n = n
            self.sem(e)
            for _, _, _, d in self.ops[e]:
                if d:
                    self.sem(d)
        block = self.ctx.enter_context(self.nc.Block())
        for e in self.ENGINES:
            into = {"tensor": block.tensor, "vector": block.vector, "scalar": block.scalar,
                            "gpsimd": block.gpsimd, "sync": block.sync}[e]
            into(self.body(e))

    def body(self, e):
        def run(eng):
            known = {}
            for fn, waits, t, d in self.ops[e]:
                need = {}
                for w in waits:
                    need[w.key] = max(need.get(w.key, 0), w.n)
                for key, v in need.items():
                    if known.get(key, 0) < v:
                        eng.wait_ge(self.sem(key), v)
                        known[key] = v
                ins = fn(eng)
                if d:
                    ins.then_inc(self.sem(d), 16)
                elif t.used:
                    ins.then_inc(self.sem(e), 1)
        return run


class Ring:

    def __init__(self, bufs):
        self.bufs, self.rel, self.n = bufs, [[] for _ in bufs], 0

    def get(self):
        i = self.n % len(self.bufs)
        self.n += 1
        rel, self.rel[i] = self.rel[i], None
        assert rel is not None, "a buffer's last use isn't queued yet"
        return self.bufs[i], rel, i

    def done(self, i, *toks):
        self.rel[i] = list(toks)


class Work:

    def __init__(self, parts, total):
        self.parts, self.total, self.sum = parts, total, 0.0

    def upto(self, share):
        while self.sum < share * self.total - 1e-6:
            w = next(self.parts, None)
            if w is None:
                return
            self.sum += w

    def rest(self):
        for w in self.parts:
            self.sum += w
        return self.sum


def build(nc, T, OUT, stop=99):
    ctx = ExitStack()
    with ctx:
        q = Queues(nc, ctx)
        AF = ctx.enter_context(nc.sbuf_tensor("plain", [P, NF], F32))
        AR = ctx.enter_context(nc.sbuf_tensor("split", [P, NR], F32R))
        PS = ctx.enter_context(nc.psum_tensor("psum", [P, 4096], F32))

        def pe(fn, *w):
            return q.add("tensor", fn, w)

        def dve(fn, *w):
            return q.add("vector", fn, w)

        def act(fn, *w):
            return q.add("scalar", fn, w)

        pool_last = [None]

        def pool(fn, *w):
            pool_last[0] = q.add("gpsimd", fn, (pool_last[0],) + w)
            return pool_last[0]

        def load(name, dst, src, *w):
            return q.dma(name, lambda e: e.dma_start(dst, src), w)

        def view(off, cnt, pat=None, **kw):
            v = AF[:, off:off + cnt]
            return v.rearrange(pat, **kw) if pat else v

        def rview(off, cnt, pat=None, **kw):
            v = AR[:, off:off + cnt]
            return v.rearrange(pat, **kw) if pat else v

        def pairview(off, cnt, pat=None, **kw):
            return rview(off, cnt, pat, **kw), rview(off + cnt, cnt, pat, **kw)

        def f32(ap):
            return ap.bitcast(F32)

        def mm3(out, lhs, rhs, first, last, waits, skip=False):
            for n, (x, y) in enumerate(((0, 0), (0, 1), (1, 0))):
                m = pe(lambda e, x=x, y=y, n=n: e.matmul(out, lhs[x], rhs[y], start=(first and n == 0),
                                                         stop=(last and n == 2), skip_group_check=skip), *waits)
            return m

        def bank(i, n=512):
            return PS[:, 512 * i:512 * i + n]

        RA = Ring([PS[:, 0:1024], PS[:, 1024:2048]])

        def singles():
            ring = Ring([bank(i) for i in range(4)])
            ring.rel = [list(RA.rel[i // 2]) for i in range(4)]
            return ring

        def pairs(ring):
            RA.rel = [ring.rel[2 * i] + ring.rel[2 * i + 1] for i in range(2)]

        RB = RB4 = Ring([bank(i) for i in range(4, 8)])

        X = view(0, 2048, "p (t d) -> p t d", d=D)
        XN = view(2048, 2048, "p (t d) -> p t d", d=D)
        XNT = pairview(0, 2048, "p (k n) -> p k n", k=2)
        ID = view(4096, 128)
        at = [4224]

        def small(cnt, pat=None, **kw):
            at[0] += cnt
            assert at[0] <= 5120
            return view(at[0] - cnt, cnt, pat, **kw)

        VEC = small(T["vec"].shape[1])
        ST = small(48, "p (t s) -> p t s", s=6)
        MV = small(16, "p (t s) -> p t s", s=2)
        VE = small(8)
        RS = small(8)
        MHALF = small(8)
        LG = small(64, "p (t e) -> p t e", e=8)
        LB = small(64, "p (t e) -> p t e", e=8)
        OH12 = small(128)
        OH1, OH2 = (OH12[:, 64 * i:64 * i + 64].rearrange("p (t e) -> p t e", e=8) for i in range(2))
        REV = small(64, "p (t e) -> p t e", e=8)
        RT = small(64, "p (s t) -> p s t", t=8)
        MS = small(8, "p (r t) -> p r t", t=2)
        GR = small(8, "p (r t) -> p r t", t=2)
        CST = small(88)
        JJ, BASE, FULL, UPTO = CST[:, 0:16], CST[:, 16:20], CST[:, 20:24], CST[:, 24:88]
        NTL = small(8)
        END = small(8)
        EJ = small(16)
        IDXS = small(16).bitcast(I32)
        IDX = [IDXS[:, 8 * i:8 * i + 8] for i in range(2)]
        WIX = small(64).bitcast(I32).rearrange("p (j u) -> p j u", u=4)
        EIX = small(16).bitcast(I32)
        xin = T["x"].rearrange("b (t p) d -> p (b t) d", p=P)
        t_vec = load("vec", VEC, T["vec"])
        t_rev = load("rev", REV.rearrange("p t e -> p (t e)"), T["rev"])
        t_cst = load("cst", CST, T["cst"])
        t = pool(lambda e: e.memset(ID, 0.0))
        t_id = pool(lambda e: e.affine_select(out=ID, in_=ID, compare_op=ALU.not_equal, fill=1.0, base=0,
                                              pattern=[[-1, P]], channel_multiplier=1), t)
        t_mh = pool(lambda e: e.memset(MHALF, -0.5))
        XS = nc.dram_tensor("sorted_x", (TILE * 15, D), F32, kind="Internal").ap()
        YS = nc.dram_tensor("sorted_y", (TILE * 15, D), F32, kind="Internal").ap()
        xt = []

        def stats(src, lo, hi, src_t, free):
            for i in range(lo, hi):
                a = dve(lambda e, i=i: e.bn_stats(ST[:, i, :], src[:, i, :]), src_t[i], *free)
            for i in range(lo, hi):
                a = dve(lambda e, i=i: e.bn_aggr(MV[:, i, :], ST[:, i, :]), a if i == lo else None)
            b = pool(lambda e: e.tensor_scalar(VE[:, lo:hi], MV[:, lo:hi, 1], EPS, None, ALU.add), a)
            b = pool(lambda e: e.tensor_tensor(RS[:, lo:hi], VE[:, lo:hi], MHALF[:, lo:hi], ALU.pow), b, t_mh)
            return a, b

        def scaled(src, dst, lo, hi, tk):
            return {i: dve(lambda e, i=i: e.tensor_scalar(dst[:, i, :], src[:, i, :], MV[:, i, 0:1],
                                                          RS[:, i:i + 1], ALU.subtract, ALU.mult), *tk)
                    for i in range(lo, hi)}

        def norm(src, dst, lo, hi, src_t, free):
            return scaled(src, dst, lo, hi, stats(src, lo, hi, src_t, free))

        def split(dst, src, tk, free, lo_eng=None):
            h = act(lambda e: e.activation(dst[0], src, ACT.Copy), *tk, *free)
            o = (lo_eng or dve)(lambda e: e.tensor_tensor(dst[1], src, f32(dst[0]), ALU.subtract), h, *tk, *free)
            return h, o

        def turn(src, dst, blocks, src_t, free, gain=None, tmp=None, ring=None):
            out = []
            ring = ring or RB4
            for c in blocks:
                for k in range(2):
                    s, w, r = ring.get()
                    for j in range(4):
                        i = 4 * c + j
                        m = pe(lambda e, s=s, i=i, j=j, k=k: e.transpose(
                            s[:, 128 * j:128 * j + 128], src[:, i, 128 * k:128 * k + 128], ID),
                            src_t[i], t_id, *w)
                    d = [x[:, k, 512 * c:512 * c + 512] for x in dst]
                    if gain:
                        tb, tw, tr = tmp.get()
                        a = act(lambda e, tb=tb, s=s, k=k: e.activation(
                            tb, s, ACT.Identity, bias=gain[1][:, k:k + 1], scale=gain[0][:, k:k + 1]), m, t_vec, *tw)
                        ring.done(r, a)
                        h, o = split(d, tb, [a], free)
                        tmp.done(tr, h, o)
                    else:
                        h, o = split(d, s, [m], free)
                        ring.done(r, h, o)
                    out += [h, o]
            return out, m

        def vec(i):
            return VEC[:, 2 * i:2 * i + 2]

        V_LATG, V_LATB, V_CTXG, V_CTXB, V_GX, V_BX, V_GL, V_BL = range(8)
        BQ = VEC[:, 16:20]
        BK = VEC[:, 20:24]
        SGN = VEC[:, 24:25]
        ONE16 = VEC[:, 25:26]

        C64 = C16 = pairview(24064, 4096, "p (k n) -> p k n", k=2)
        BIAS = view(20400, 256)
        TB = view(12288, 2048)
        ONES = view(18960, 64)
        t_one = dve(lambda e: e.memset(ONES, 1.0))
        ONESR = rview(NR - 128, 128)
        t_oner = dve(lambda e: e.memset(f32(ONESR), 1.0))
        NMX = view(20304, 16)
        K32 = Ring([view(17664 + 512 * i, 512) for i in range(2)])
        WR64 = [view(19024, 1280), view(14336, 1280)]

        def attention64(layer, late, ctx_t, tab_t, w0, free, tail, after0=None, sums=()):
            own = layer == 1
            S = 1536 if own else 1024
            nk = S // P
            KT = [rview(6144 + 3072 * i, 2 * S, "p (h n) -> p h n", h=2) for i in range(2)]
            QA = [rview(12288 + 2048 * i, 1024, "p (h n) -> p h n", h=2) for i in range(2)]
            QB = [rview(13312 + 2048 * i, 1024, "p (h n) -> p h n", h=2) for i in range(2)]
            DG = [rview(16384 + 1024 * i, 1024, "p (h n) -> p h n", h=2) for i in range(2)]
            PT = Ring([view(5120 + 1024 * i, 1024, "p (h n) -> p h n", h=2) for i in range(3)])
            VA = [view(8192 + 1536 * i, nk * 128, "p (t c) -> p t c", c=128) for i in range(2)]
            OT, VT = view(11264, 512), view(11776, 512)
            vtrel, vlast = [list(free)], [None, None]
            COS, SIN = TB[:, 0:1024], TB[:, 1024:2048]
            WR = WR64
            W = [pairview(4096, 1024), pairview(18432, 1024)]
            SA = [view(15616 + 1024 * i, 1024, "p (h n) -> p h n", h=2) for i in range(2)]
            TR = Ring([view(2048 + 1024 * i, 1024, "p (h n) -> p h n", h=2) for i in range(2)])
            for i in range(2):
                TR.done(i, *free)
            npair = 4 if own else 8
            steps = [(p, b) for p in range(npair) for b in range(B)]
            init = []
            for i in range(2):
                for h in range(2):
                    lo = 64 - 64 * h
                    init.append(pool(lambda e, i=i, h=h, lo=lo: e.memset(f32(QB[i][lo:lo + 64, h, :]), 0.0), *free))
            w_raw, w_t = {}, {}
            raw_rel = [list(free), list(free)]
            w_rel = [list(free), list(free)]
            grel = [list(free), list(free)]
            orel = [[*free, *sums], [*free, *sums]]
            gtok, vtok, negm = {}, {}, {}

            def wload(p):
                w_raw[p] = load(f"wa{p % 2}", WR[p % 2], T[f"l{layer}_w"][p], *raw_rel[p % 2])

            w_raw[0] = w0
            wload(1)
            lat_t = []

            def wsplit(p):
                if p < npair:
                    w_t[p] = split(W[p % 2], WR[p % 2][:, 0:1024], [w_raw[p]], w_rel[p % 2])

            wsplit(0)

            def proj(n):
                p, b = steps[n]
                i = n % 2
                toks = list(init)
                wt = w_t[p]

                def wsl(j):
                    return [x[:, 256 * j:256 * j + 256].rearrange("p (k n) -> p k n", k=2) for x in W[p % 2]]

                x0 = 512 * b

                def project(out, j, src, c0, cn, waits):
                    ww = wsl(j)
                    for k in range(2):
                        m = mm3(out, [x[:, k, :] for x in ww], [x[:, k, c0:c0 + cn] for x in src],
                                k == 0, k == 1, [*wt, *waits])
                    return m

                def place(src, tk, c0, cn):
                    out = []
                    for h in range(2):
                        hi, lo = 64 * h, 64 - 64 * h
                        a = act(lambda e, h=h, hi=hi: e.activation(
                            KT[i][hi:hi + 64, h, c0:c0 + cn], src[hi:hi + 64, :], ACT.Copy), tk, *grel[i])
                        out += [a, dve(lambda e, h=h, hi=hi, lo=lo: e.tensor_tensor(
                            KT[i][lo:lo + 64, h, c0:c0 + cn], src[hi:hi + 64, :],
                            f32(KT[i][hi:hi + 64, h, c0:c0 + cn]), ALU.subtract), a, *grel[i])]
                    return out

                for c in range(2):
                    tm, tw, tr = TR.get()
                    for j, tb in enumerate((COS, SIN)):
                        s, w, r = RB.get()
                        m = project(s, 1 + j, C64, 1024 * b + 512 * c, 512, [*ctx_t[b], *w])
                        a2 = dve(lambda e, s=s, tm=tm, c=c, j=j, tb=tb: e.tensor_tensor(
                            tm[:, j, :], s, tb[:, 512 * c:512 * c + 512], ALU.mult), m, *tab_t, *tw)
                        RB.done(r, a2)
                        if j == 0:
                            yield 1.3
                    kb, kw, kr = K32.get()
                    a = (pool if n else dve)(lambda e, kb=kb, tm=tm: e.tensor_tensor(kb, tm[:, 0, :], tm[:, 1, :], ALU.add), a2, *kw)
                    TR.done(tr, a)
                    yield 1.3
                    pl = place(kb, a, 512 * c, 512)
                    K32.done(kr, *pl)
                    toks += pl
                def values(t0):
                    s, w, r = RB.get()
                    m = project(s, 3, C64 if t0 < 8 else XNT, 1024 * b + 128 * t0 if t0 < 8 else x0, 512,
                                [*lat_t, *w] if t0 == 8 else [*ctx_t[b], *w])
                    o = act(lambda e, s=s: e.activation(VT, s, ACT.Copy), m, *vtrel[0])
                    RB.done(r, o)
                    yield 1.3
                    s, w, r = RB.get()
                    for t in range(4):
                        tm_ = pe(lambda e, s=s, t=t: e.transpose(
                            s[:, 128 * t:128 * t + 128], VT[:, 128 * t:128 * t + 128], ID), o, t_id, *w)
                    vtrel[0] = [tm_]
                    vlast[0] = act(lambda e, s=s, t0=t0: e.activation(
                        VA[i][:, t0:t0 + 4, :].rearrange("p t c -> p (t c)"), s, ACT.Copy), tm_, *grel[i])
                    RB.done(r, vlast[0])
                    vlast[1] = m
                    yield 0.4

                for t0 in range(0, 8, 4):
                    yield from values(t0)
                if n == 0:
                    toks0, lpe = late(RB, [x for i2 in range(2) for x in TR.rel[i2]])
                    lat_t.extend(toks0)
                    for i2 in range(2):
                        TR.done(i2, lpe)
                s, w, r = RB.get()
                m = tail_m = project(s, 0, XNT, x0, 512, [*lat_t, *w])
                for h in range(2):
                    hi, lo = 64 * h, 64 - 64 * h
                    a = act(lambda e, s=s, h=h, hi=hi: e.activation(
                        QA[i][hi:hi + 64, h, :], s[hi:hi + 64, :], ACT.Copy), m, *grel[i])
                    a2 = act(lambda e, s=s, h=h, hi=hi, lo=lo: e.activation(
                        QA[i][lo:lo + 64, h, :], s[hi:hi + 64, :], ACT.Copy), m, *grel[i])
                    o = dve(lambda e, s=s, h=h, hi=hi: e.tensor_tensor(
                        QB[i][hi:hi + 64, h, :], s[hi:hi + 64, :], f32(QA[i][hi:hi + 64, h, :]), ALU.subtract),
                        a, a2, *grel[i])
                RB.done(r, a2, o)
                toks += [a2, o]
                yield 1.3
                if own:
                    s, w, r = RB.get()
                    m = project(s, 1, XNT, x0, 512, [*lat_t, *w])
                    pl = place(s, m, 1024, 512)
                    RB.done(r, *pl)
                    toks += pl
                    yield 1.3
                if own:
                    yield from values(8)
                o = vlast[0]
                if b == 1:
                    w_rel[p % 2] = [vlast[1] if own else tail_m]
                    wsplit(p + 1)
                gtok[n], vtok[n] = toks, o

            NM = NMX[:, 0:4]
            MXC = NMX[:, 4:16].rearrange("p (t c) -> p t c", c=3)

            def rowmax(n):
                i = n % 2
                prev = mxrel[0]
                for h in range(2):
                    for t in range(4):
                        for c in range(3):
                            s, w, r = RS1.get()
                            m = pe(lambda e, s=s, h=h, t=t, c=c: e.matmul(
                                s, QA[i][:, h, 128 * t:128 * t + 128],
                                KT[i][:, h, 512 * c:512 * c + 512], start=True, stop=True), *gtok[n], *w)
                            o = dve(lambda e, s=s, t=t, c=c: e.tensor_reduce(
                                MXC[:, t, c:c + 1], s, AX.X, ALU.max), m, *prev)
                            RS1.done(r, o)
                            yield 0.85
                    o = dve(lambda e: e.tensor_reduce(NM, MXC, AX.X, ALU.max, negate=True), o, *prev)
                    for t in range(4):
                        a = act(lambda e, h=h, t=t: e.activation(
                            DG[i][:, h, 128 * t:128 * t + 128], ID, ACT.Copy, scale=NM[:, t:t + 1]),
                            o, t_id, *grel[i])
                    prev = [o, a]
                mxrel[0] = prev
                gtok[n] = gtok[n] + [a]
                yield 0.0

            def attend(n, work):
                i = n % 2
                out = []
                pend = []
                sacc = [None]

                def values():
                    kt, pt, tp, pr = pend.pop(0)
                    if kt == 0:
                        out.extend(RO.get())
                    so, sw, _ = out
                    for h in range(2):
                        m = pe(lambda e, pt=pt, kt=kt, h=h: e.matmul(
                            so[64 * h:64 * h + 64, :], VA[i][:, kt, 64 * h:64 * h + 64], pt[:, h, :],
                            start=(kt == 0), stop=(kt == nk - 1)), tp, vtok[n], *sw)
                    if kt == 0:
                        sacc[0] = [tp, m]
                        return m
                    sacc[0] = [(dve if kt % 4 == 3 else pool)(
                        lambda e, pt=pt: e.tensor_tensor(SA[i], SA[i], pt, ALU.add), tp, *sacc[0])]
                    PT.done(pr, m, *sacc[0])
                    return m

                for kt in range(nk):
                    pt, pw, pr = PT.get() if kt else (SA[i], orel[i], None)
                    for h in range(2):
                        d, w, r = RS1.get()
                        kk = KT[i][:, h, 128 * kt:128 * kt + 128]
                        pe(lambda e, d=d, kk=kk, h=h: e.matmul(d, kk, QA[i][:, h, :], start=True, stop=False),
                           *gtok[n], *w)
                        m = pe(lambda e, d=d, kk=kk, h=h: e.matmul(d, kk, QB[i][:, h, :], start=False,
                                                                   stop=not own))
                        if own:
                            m = pe(lambda e, d=d, h=h: e.matmul(d, ONESR, DG[i][:, h, :], start=False, stop=True),
                                   t_oner)
                        tp = act(lambda e, d=d, pt=pt, h=h: e.activation(pt[:, h, :], d, ACT.Exp, scale=0.125),
                                 m, *pw)
                        RS1.done(r, tp)
                    if not own:
                        tp = dve(lambda e, pt=pt: e.tensor_scalar(pt, pt, CLIP_LO, CLIP_HI, ALU.max, ALU.min), tp)
                    pend.append((kt, pt, tp, pr))
                    if len(pend) > 2:
                        values()
                    work.upto((kt + 1) / nk)
                while pend:
                    mv = values()
                grel[i] = [mv]
                ends[n] = (out[0], out[2], mv, sacc[0][0])

            def divide(n):
                i = n % 2
                so, sr, mv, sacc = ends[n]
                s, w, r = RB.get()
                for h in range(2):
                    m = pe(lambda e, h=h: e.matmul(s[64 * h:64 * h + 64, :], ONES, SA[i][:, h, :],
                                                   start=True, stop=True), sacc, t_one, *w)
                rb, rw, rr = K32.get()
                o = dve(lambda e: e.reciprocal(rb, s), m, *rw)
                RB.done(r, o)
                o = dve(lambda e: e.tensor_tensor(OT, so, rb, ALU.mult), o, mv, *orel[0], *orel[1])
                RO.done(sr, o)
                K32.done(rr, o)
                ends[n] = o

            def output(n):
                p, b = steps[n]
                i = n % 2
                wo = WR[p % 2][:, 1024:1280]
                for t in range(4):
                    s, w, r = RB.get()
                    m = pe(lambda e, s=s, t=t: e.matmul(s[:, 0:256], OT[:, 128 * t:128 * t + 128], wo,
                                                        start=True, stop=True), w_raw[p], ends[n], *w)
                    xt[4 * b + t] = dve(lambda e, s=s, t=t: e.tensor_tensor(
                        X[:, 4 * b + t, :], X[:, 4 * b + t, :], s[:, 0:256], ALU.add), m, xt[4 * b + t])
                    RB.done(r, xt[4 * b + t])
                orel[i] = [m]
                if b == 1:
                    raw_rel[p % 2] = [m, *w_t[p]]
                    if p + 2 < npair:
                        wload(p + 2)
                return m

            RO = Ring(RB4.bufs[0:1])
            RB = Ring(RB4.bufs[1:4])
            RO.rel, RB.rel = RB4.rel[0:1], RB4.rel[1:4]
            RS1 = singles()
            ends = {}
            mxrel = [list(free)]

            def side(n):
                if n:
                    divide(n - 1)
                    yield 0.5
                g = prepare(n + 1)
                for x in range(2):
                    yield next(g, 0.0)
                if n:
                    output(n - 1)
                    yield 1.0
                yield from g
                if n == len(steps) - 1:
                    tail(RB, [*w_rel[(npair - 1) % 2], *TR.rel[0], *TR.rel[1]])

            def prepare(n):
                if n < len(steps):
                    yield from proj(n)
                    if own:
                        yield from rowmax(n)

            total = Work(prepare(0), 0.0).rest() + 1.5
            if after0:
                after0(RB)
            for n in range(len(steps)):
                work = Work(side(n), total)
                attend(n, work)
                work.rest()
            divide(n)
            last = output(n)
            RB4.rel = RO.rel + RB.rel
            pairs(RS1)
            return [last, xt[3], xt[7]]

        WR16 = view(18448, 1024)
        WO16 = [view(19472 + 256 * i, 256) for i in range(2)]

        def first_weights(layer, free):
            return (load("w16", WR16, T[f"l{layer}_w"][0], *free), load("wo0", WO16[0], T[f"l{layer}_wo"][0], *free),
                    load("wo1", WO16[1], T[f"l{layer}_wo"][1], *free))


        def attention16(layer, late, ctx_t, w0, free, tail):
            causal = layer == 2
            S = 512 if causal else 1024
            nk = S // P
            KS = [rview(4096 + 4096 * i, 4096, "p (h n) -> p h n", h=4) for i in range(2)]
            QS = [rview(12288 + 2048 * i, 2048, "p (h n) -> p h n", h=4) for i in range(2)]
            KHL = pairview(16384, 1024)
            QHL = pairview(18432, 512)
            QM = rview(19456, 512)
            W = pairview(19968, 1024)
            WV = pairview(8192, 512, "p (k n) -> p k n", k=2)
            PT = Ring([view(5120 + 1024 * i, 1024, "p (h n) -> p h n", h=2) for i in range(4)])
            VA = view(9216, 4096, "p (t h c) -> p t h c", h=16, c=32)
            NMT = view(13312, 512, "p (t c) -> p t c", t=4)
            MXC = NMX[:, 0:8].rearrange("p (t c) -> p t c", c=2)
            OU = view(13824, 512)
            QZ = rview(22016, 2048, "p (h n) -> p h n", h=4)
            RC = view(14336, 512)
            COS, SIN = view(16384, 1024), view(17408, 1024)
            WR, WO = WR16, WO16
            TM = Ring([view(x, 1024, "p (h n) -> p h n", h=2) for x in (15360, 2048)])
            for i in range(2):
                TM.done(i, *free)
            BV, SEL, TRI = view(14848, 256), view(15104, 128), view(15232, 128)
            if causal:
                tt, bt = None, load("bv", BV, T["bc"][:, 512:768], *free)
            else:
                tt, bt = load("tab", view(16384, 2048), T["l3_tab"], *free), None
            st = load("sel", SEL, T["sel"], *free)
            z4 = pool(lambda e: e.memset(TRI, 0.0), *free)
            z4 = pool(lambda e: e.affine_select(out=TRI, in_=TRI, compare_op=ALU.is_ge, fill=NEG, base=0,
                                                pattern=[[-1, P]], channel_multiplier=1), z4)
            steps = [(b, g) for b in range(B) for g in range(4)]
            wrel, raw_rel = free[:1], list(free)
            wo_rel = [list(free), list(free)]
            wo_t, kq_t, qm_t, staged, ends = {}, {}, {}, {}, {}
            srel = [list(free), list(free)]
            krel, qrel = list(free), list(free)
            ourel, zrel, z2 = list(free), [], None
            vt, mx, last_att = {}, {}, [None]
            vrel, rcrel = list(free), []

            def move(i, dst, src, src_t, name):
                for n, x in src:
                    for j in range(4):
                        t = q.dma(f"{name}{i}", lambda e, j=j, n=n, x=x: e.dma_start(
                            f32(dst[32 * n:32 * n + 32, j, :]), f32(x[32 * j:32 * j + 32, :])), src_t)
                return t

            def wload(n):
                if n < len(steps):
                    w_raw[n] = load("w16", WR, T[f"l{layer}_w"][steps[n][1]], *raw_rel)

            def wsplit(n):
                nonlocal raw_rel
                if n < len(steps):
                    w_t[n] = split(W, WR, [w_raw[n]], wrel, pool if n else dve)
                    raw_rel = list(w_t[n])
                    wload(n + 1)

            w_raw, w_t = {0: w0[0]}, {}
            wo_t[0], wo_t[1] = w0[1:]
            lat_t = []

            def proj(n):
                nonlocal wrel, qrel, zrel
                b, g = steps[n]
                wt = w_t[n]

                def project(out, j, src, c0, waits):
                    for k in range(2):
                        m = mm3(out, [x[:, 256 * j + 128 * k:256 * j + 128 * k + 128] for x in W],
                                [x[:, k, c0:c0 + 512] for x in src], k == 0, k == 1, [*wt, *waits])
                    return m

                def rows(which, c0, src, src_t, cos0, bias, dst, rel):
                    tm, tw, tr = TM.get()
                    if causal:
                        s, w, r = RS1.get()
                        m = project(s, which, src, c0, [*src_t, *w])
                        a = dve(lambda e: e.tensor_scalar(tm[:, 0, :], s, bias, None, ALU.add), m, t_vec, *tw)
                        RS1.done(r, a)
                    else:
                        one = ONE16 if which == 2 else 0.0
                        for j, tb in enumerate((COS, SIN)):
                            s, w, r = RS1.get()
                            m = project(s, which + j, src, c0, [*src_t, *w])
                            a = dve(lambda e, s=s, j=j, tb=tb, one=(0.0 if j else one): e.scalar_tensor_tensor(
                                out=tm[:, j, :], in0=s, scalar=one, in1=tb[:, cos0:cos0 + 512],
                                op0=ALU.add, op1=ALU.mult), m, tt, t_vec, *tw)
                            RS1.done(r, a)
                        a = dve(lambda e: e.tensor_tensor(tm[:, 0, :], tm[:, 0, :], tm[:, 1, :], ALU.add), a)
                    h, o = split(dst, tm[:, 0, :], [a], rel, dve)
                    TM.done(tr, h, o)
                    return m, [h, o]

                kt = []
                for c in range(S // 512):
                    m, o = rows(2, 1024 * b + 512 * c, C16, ctx_t, 512 * c, BK[:, g:g + 1],
                                [x[:, 512 * c:512 * c + 512] for x in KHL], krel)
                    kt += o
                    yield 1.3
                if n == 0:
                    project_values(0)
                    lat0, lpe = late(RB, [*TM.rel[0], *TM.rel[1]])
                    lat_t.extend(lat0)
                    TM.done(1, lpe)
                m, qt = rows(0, 512 * b, XNT, lat_t, 0, BQ[:, g:g + 1], QHL, qrel)
                for j in range(4):
                    z = dve(lambda e, j=j: e.tensor_copy(
                        QZ[32 * j:32 * j + 32, j, :], QHL[0][32 * j:32 * j + 32, :]), *qt, *zrel)
                wrel, qrel = [m], [z]
                staged[n] = (kt, qt, z)
                yield 1.3

            def load_out(n):
                if n < len(steps):
                    wo_t[n] = load(f"wo{n % 2}", WO[n % 2], T[f"l{layer}_wo"][steps[n][1]], *wo_rel[n % 2])

            def place(n):
                nonlocal krel, qrel
                i = n % 2
                kt, qt, _ = staged[n]
                k = [x[:, 0:S] for x in KHL]
                t1 = move(i, KS[i][:, :, 0:S], enumerate((k[0], k[1], k[0])), [*kt, *srel[i]], "mk")
                t2 = move(i, QS[i], ((1, QHL[0]), (2, QHL[1])), [*qt, *srel[i]], "mq")
                krel, qrel = [t1], [*qrel, t2]
                kq_t[n] = [t1, t2]

            wv_t = {}

            def values_weight(b, *free_t):
                wv_t[b] = load("wv", RC, T[f"l{layer}_wv"], *free_t)

            def zeros(ap, n):
                return act(lambda e: e.activation(ap, ID.unsqueeze(1).to_broadcast([P, n, P]), ACT.Copy, scale=0.0),
                           t_id, *free)

            def clear():
                nonlocal z2, zrel, mtrel
                z2 = zeros(view(9216, 4096, "p (a n) -> p a n", n=P), 32)
                z2 = dve(lambda e: e.memset(VA[:, :, :, 16:17], 1.0), z2)
                zrel = [zeros(rview(22016, 2048, "p (a n) -> p a n", n=P), 16)]
                mtrel = [dve(lambda e: e.memset(NMT, 0.0), *free)]

            def project_values(b):
                nonlocal rcrel
                wvt = split([x.rearrange("p k n -> p (k n)") for x in WV], RC, [wv_t[b]], srel[1])
                rcrel = list(wvt)
                if z2 is None:
                    clear()
                for t in range(nk):
                    s, w, r = RB.get()
                    for k in range(2):
                        c0 = 1024 * b + 128 * t
                        m = mm3(s[:, 0:256], [x[:, k, c0:c0 + 128] for x in C16], [x[:, k, :] for x in WV],
                                k == 0, k == 1, [*wvt, *ctx_t, *w])
                    dst = VA[:, t, :, 0:16]
                    src = s[:, 0:256].rearrange("p (h c) -> p h c", c=16)
                    if causal:
                        o = dve(lambda e, dst=dst, src=src: e.tensor_tensor(
                            dst, src, BV.rearrange("p (h c) -> p h c", c=16), ALU.add), m, bt, z2, *vrel)
                    else:
                        o = act(lambda e, dst=dst, src=src: e.activation(dst, src, ACT.Copy), m, z2, *vrel)
                    RB.done(r, o)
                srel[1] = [m]
                vt[b] = o

            mtrel = []

            def rowmax(n):
                nonlocal krel, zrel
                kt, qt, z = staged[n]
                mxl = None
                for j in range(4):
                    for t in range(4):
                        for u in range(0, 128 * (t + 1) if causal else 1024, 512):
                            kn = min(512, 128 * (t + 1)) if causal else 512
                            s, w, r = RB.get()
                            m = pe(lambda e, s=s, j=j, t=t, u=u, kn=kn: e.matmul(
                                s[:, 0:kn], QZ[:, j, 128 * t:128 * t + 128], KHL[0][:, u:u + kn],
                                start=True, stop=True), *kt, z, *w)
                            o = m
                            if causal:
                                o = dve(lambda e, s=s, t=t: e.tensor_tensor(
                                    s[:, 128 * t:128 * t + 128], s[:, 128 * t:128 * t + 128], TRI, ALU.add), m, z4)
                                o = dve(lambda e, s=s, t=t, j=j, kn=kn: e.tensor_reduce(
                                    NMT[:, t, 32 * j + 16:32 * j + 17], s[:, 0:kn], AX.X, ALU.max, negate=True),
                                    o, *mtrel)
                            else:
                                o = dve(lambda e, s=s, t=t, u=u: e.tensor_reduce(
                                    MXC[:, t, u // 512:u // 512 + 1], s, AX.X, ALU.max), m, mxl)
                            RB.done(r, o)
                            yield kn / 900
                    if not causal:
                        o = mxl = dve(lambda e, j=j: e.tensor_reduce(
                            NMT[:, :, 32 * j + 16], MXC, AX.X, ALU.max, negate=True), o, *mtrel)
                krel, zrel = [*krel, m], [m]
                mx[n] = o

            def shift(n):
                nonlocal qrel, mtrel
                i = n % 2
                s, w, r = RB.get()
                for t in range(4):
                    m = pe(lambda e, s=s, t=t: e.matmul(
                        s[:, 128 * t:128 * t + 128], NMT[:, t, :], ID, start=True, stop=True), mx[n], t_id, *w)
                mtrel = [m]
                o = dve(lambda e, s=s: e.tensor_tensor(QM, f32(QHL[0]), s, ALU.add), m, *qmrel[0])
                RB.done(r, o)
                t = move(i, QS[i], ((0, QM),), [o, *srel[i]], "mm")
                qmrel[0] = [t]
                qrel = [*qrel, o]
                qm_t[n] = [t, *kq_t[n]]

            qmrel = [list(free)]

            def attend(n, work):
                b, g = steps[n]
                i = n % 2
                so, sw, sr = RO.get()
                pend = []

                def values():
                    kt, pts = pend.pop(0)
                    q0 = 128 * kt if causal else 0
                    for j in range(4):
                        pt, tp, pr = pts[j // 2]
                        m = pe(lambda e, j=j, pt=pt: e.matmul(
                            so[32 * j:32 * j + 32, q0:512], VA[:, kt, 4 * g + j, :], pt[:, j % 2, q0:512],
                            start=(kt == 0), stop=(kt == nk - 1), skip_group_check=True), tp, vt[b], *sw)
                    for pt, tp, pr in pts:
                        PT.done(pr, m)
                    return m

                for kt in range(nk):
                    q0 = 128 * kt if causal else 0
                    pts = []
                    for jj in range(2):
                        pt, pw, pr = PT.get()
                        for h in range(2):
                            j = 2 * jj + h
                            s, w, r = RS1.get()
                            m = pe(lambda e, s=s, j=j, kt=kt, q0=q0: e.matmul(
                                s[:, q0:512], KS[i][0:96, j, 128 * kt:128 * kt + 128],
                                QS[i][0:96, j, q0:512], start=True, stop=True), *qm_t[n], *w)
                            tp = act(lambda e, s=s, pt=pt, h=h, q0=q0: e.activation(
                                pt[:, h, q0:512], s[:, q0:512], ACT.Exp, scale=0.25), m, *pw)
                            RS1.done(r, tp)
                        if causal:
                            d = pt[:, :, q0:q0 + 128]
                            tp = pool(lambda e, d=d: e.affine_select(
                                out=d, in_=d, compare_op=ALU.is_ge, fill=0.0, base=0,
                                pattern=[[0, 2], [1, P]], channel_multiplier=-1), tp)
                        pts.append((pt, tp, pr))
                        work.upto((2 * kt + jj + 1) / (2 * nk - 1))
                    pend.append((kt, pts))
                    if len(pend) > 1:
                        values()
                m = values()
                srel[i] = [m]
                last_att[0] = m
                c1 = act(lambda e: e.activation(OU, so, ACT.Copy), m, *ourel)
                RO.done(sr, c1)
                ends[n] = c1

            def divide(n):
                s, w, r = RB.get()
                m = pe(lambda e: e.matmul(s, SEL, OU, start=True, stop=True), ends[n], st, *w)
                o = dve(lambda e: e.reciprocal(RC, s), m, *rcrel)
                RB.done(r, o)
                ends[n] = dve(lambda e: e.tensor_tensor(OU, OU, RC, ALU.mult), o)

            def output(n):
                nonlocal ourel
                b, g = steps[n]
                i = n % 2
                for t in range(4):
                    s, w, r = RB.get()
                    m = pe(lambda e, s=s, t=t: e.matmul(s[:, 0:256], OU[:, 128 * t:128 * t + 128], WO[i],
                                                        start=True, stop=True), wo_t[n], ends[n], *w)
                    x = 4 * b + t
                    xt[x] = dve(lambda e, s=s, x=x: e.tensor_tensor(X[:, x, :], X[:, x, :], s[:, 0:256], ALU.add),
                                m, xt[x])
                    RB.done(r, xt[x])
                ourel = [m]
                wo_rel[i] = [m]
                return m

            def side(n):
                if n + 1 < len(steps):
                    place(n + 1)
                    wsplit(n + 2)
                yield 1.0
                if n:
                    divide(n - 1)
                    yield 1.0
                if n + 1 < len(steps):
                    if steps[n + 1][0] != steps[n][0]:
                        values_weight(steps[n + 1][0], ends[n - 1])
                    for x, w in enumerate(rowmax(n + 1)):
                        yield w
                        if n and x == 7:
                            output(n - 1)
                            load_out(n + 1)
                            yield 0.5
                    shift(n + 1)
                    yield 0.5
                    if n + 2 < len(steps):
                        yield from proj(n + 2)
                elif n:
                    output(n - 1)
                    tail(RB, [*wrel, *TM.rel[0], *TM.rel[1]])

            RO = Ring(RB4.bufs[0:1])
            RB = Ring(RB4.bufs[1:4])
            RO.rel, RB.rel = RB4.rel[0:1], RB4.rel[1:4]
            RS1 = singles()
            wsplit(0)
            values_weight(0, *free)
            total = 2.5 + Work(proj(0), 0.0).rest()
            place(0)
            total += Work(rowmax(0), 0.0).rest()
            shift(0)
            wsplit(1)
            Work(proj(1), 0.0).rest()
            for n in range(len(steps)):
                b = steps[n][0]
                if b != steps[max(n - 1, 0)][0]:
                    vrel = [last_att[0]]
                    project_values(b)
                work = Work(side(n), total)
                attend(n, work)
                work.rest()
            divide(n)
            m = output(n)
            RB4.rel = RO.rel + RB.rel
            pairs(RS1)
            return [m, xt[3], xt[7]]

        def bc(ap):
            return ap.unsqueeze(2).to_broadcast([P, NT, 8])

        def logits(src, raw, src_t, free, bias=None, bias_t=None):
            wt = split([x.rearrange("p k e -> p (k e)") for x in RWS], RW, [raw], free)
            sv, w2, r2 = RB.get()
            for c in range(2):
                s, w, r = RB.get()
                for k in range(2):
                    m = mm3(s, [x[:, k, :] for x in RWS], [x[:, k, 512 * c:512 * c + 512] for x in src],
                            k == 0, k == 1, [*wt, *src_t, *w])
                o = dve(lambda e, s=s, c=c: e.tensor_copy(LT[:, 512 * c:512 * c + 512], s[0:8, :]), m, *free)
                RB.done(r, o)
                for t in range(4 * c, 4 * c + 4):
                    m = pe(lambda e, t=t: e.transpose(sv[:, 8 * t:8 * t + 8], LT[:, P * t:P * t + P], ID[0:8, 0:8]),
                           o, t_id, *w2)
            sv3 = sv[:, 0:64].rearrange("p (t e) -> p t e", e=8)
            o = dve(lambda e: e.tensor_copy(LG, sv3), m)
            o2 = o
            if bias is not None:
                o2 = dve(lambda e: e.tensor_tensor(LB, LG, bias, ALU.add), o, bias_t)
            RB.done(r2, o)
            return o, o2

        def top(src, oh, mx, tk):
            o = dve(lambda e: e.tensor_reduce(mx, src, AX.X, ALU.max), tk)
            o = dve(lambda e: e.tensor_tensor(oh, src, bc(mx), ALU.is_equal), o)
            o = dve(lambda e: e.tensor_tensor(oh, oh, REV, ALU.mult), o, t_rev)
            o = dve(lambda e: e.tensor_reduce(RT[:, 7, :], oh, AX.X, ALU.max), o)
            return dve(lambda e: e.tensor_tensor(oh, oh, bc(RT[:, 7, :]), ALU.is_equal), o)

        def second(src, tk):
            o = dve(lambda e: e.scalar_tensor_tensor(
                out=LB.rearrange("p t e -> p (t e)"), in0=OH1.rearrange("p t e -> p (t e)"), scalar=NEG,
                in1=src.rearrange("p t e -> p (t e)"), op0=ALU.mult, op1=ALU.add), tk)
            return top(LB, OH2, RT[:, 1, :], o)

        def pair_gates(tk):
            o = dve(lambda e: e.tensor_tensor(RT[:, 2, :], RT[:, 1, :], RT[:, 0, :], ALU.max), tk)
            for i in range(2):
                o = dve(lambda e, i=i: e.tensor_tensor(RT[:, 3 + i, :], RT[:, i, :], RT[:, 2, :], ALU.subtract), o)
            o = act(lambda e: e.activation(RT[:, 3:5, :], RT[:, 3:5, :], ACT.Exp), o)
            o = dve(lambda e: e.tensor_tensor(RT[:, 2, :], RT[:, 3, :], RT[:, 4, :], ALU.add), o)
            o = dve(lambda e: e.reciprocal(RT[:, 2, :], RT[:, 2, :]), o)
            for i in range(2):
                o = dve(lambda e, i=i: e.tensor_tensor(RT[:, 5 + i, :], RT[:, 3 + i, :], RT[:, 2, :], ALU.mult), o)
            return o

        def route(ohs, ntile, units, src_t, free):
            PF = view(16896, 72, "p (t e) -> p t e", e=8)
            FX = view(16968, 16)
            TMP = view(16984, 128)
            MK = TMP[:, 0:64].rearrange("p (t e) -> p t e", e=8)
            TRIU, ALL1 = view(17112, 128), view(17240, 128)
            c1 = pool(lambda e: e.memset(view(17112, 256), 1.0), *free)
            c2 = pool(lambda e: e.affine_select(out=TRIU, in_=TRIU, compare_op=ALU.is_gt, fill=0.0, base=0,
                                                pattern=[[1, P]], channel_multiplier=-1), c1)
            mk = ohs[0]
            o = src_t
            if len(ohs) == 2:
                mk = MK
                o = dve(lambda e: e.tensor_tensor(MK, ohs[0], ohs[1], ALU.add), o, *free)
            s, w, r = RB.get()
            sv = s[:, 0:72].rearrange("p (t e) -> p t e", e=8)
            pe(lambda e: e.matmul(sv[:, 0:8, :], TRIU, mk, start=True, stop=False, skip_group_check=True), o, c2, *w)
            for t in range(NT):
                m = pe(lambda e, t=t: e.matmul(sv[:, t + 1:NT + 1, :], ALL1,
                                               mk[:, t, :].unsqueeze(1).to_broadcast([P, NT - t, 8]), start=False,
                                               stop=(t == NT - 1), skip_group_check=True))
            o = dve(lambda e: e.tensor_copy(PF, sv), m)
            RB.done(r, o)

            def grid(n, k):
                return TMP[:, 0:n * k].rearrange("p (n k) -> p n k", k=k)

            def down_(ap, n, k):
                return ap.unsqueeze(2).to_broadcast([P, n, k])

            def over(ap, n, k):
                return ap.unsqueeze(1).to_broadcast([P, n, k])

            o = dve(lambda e: e.tensor_tensor(grid(8, 4), down_(PF[:, 8, :], 8, 4), over(FULL, 8, 4), ALU.is_gt), o, t_cst)
            o = dve(lambda e: e.tensor_reduce(NTL, grid(8, 4), AX.X, ALU.add), o)
            o = dve(lambda e: e.tensor_tensor(grid(8, 8), over(NTL, 8, 8), UPTO.rearrange("p (n k) -> p n k", k=8),
                                              ALU.mult), o)
            o = dve(lambda e: e.tensor_reduce(END, grid(8, 8), AX.X, ALU.add), o)
            st = dve(lambda e: e.tensor_tensor(NTL, END, NTL, ALU.subtract), o)
            wx = dve(lambda e: e.tensor_tensor(grid(16, 8), down_(JJ, 16, 8), over(END, 16, 8), ALU.is_ge), o)
            st = dve(lambda e: e.scalar_tensor_tensor(
                out=PF[:, 0:8, :], in0=over(NTL, 8, 8), scalar=float(TILE), in1=PF[:, 0:8, :], op0=ALU.mult,
                op1=ALU.add), st)
            wx = dve(lambda e: e.tensor_reduce(EJ, grid(16, 8), AX.X, ALU.add), wx)
            nc_ = len(ohs)
            oh = OH12[:, 0:64 * nc_].rearrange("p (c n) -> p c n", n=64)
            prod = TMP[:, 0:64 * nc_]
            st = dve(lambda e: e.tensor_tensor(
                prod.rearrange("p (c n) -> p c n", n=64), oh,
                PF[:, 0:8, :].rearrange("p t e -> p (t e)").unsqueeze(1).to_broadcast([P, nc_, 64]), ALU.mult), st, wx)
            wx = dve(lambda e: e.tensor_scalar(EJ, EJ, 7.0, None, ALU.min), wx)
            st = dve(lambda e: e.tensor_reduce(FX[:, 0:8 * nc_], prod.rearrange("p (n e) -> p n e", e=8), AX.X,
                                               ALU.add), st)
            wx = dve(lambda e: e.scalar_tensor_tensor(
                out=WIX[:, :, 0:units], in0=down_(EJ, 16, units), scalar=float(P * units),
                in1=over(BASE[:, 0:units], 16, units), op0=ALU.mult, op1=ALU.add), wx)
            st = dve(lambda e: e.tensor_copy(IDXS[:, 0:8 * nc_], FX[:, 0:8 * nc_]), st)
            wx = dve(lambda e: e.tensor_copy(EIX, EJ), wx)
            return [st] * nc_, wx

        def scatter(src, src_t, ix):
            out = []
            for c, o in enumerate(ix):
                for t in range(NT):
                    out.append(q.dma("sc", lambda e, c=c, t=t: e.indirect_dma_start(
                        XS, bass.IndirectOffsetOnAxis(IDX[c][:, t:t + 1], 0), src[:, t, :], None),
                        [o, t_xs, src_t[t]], "gpsimd"))
            return out

        def gather(layer, c, t, name, dst, waits):
            return q.dma(name, lambda e: e.indirect_dma_start(
                dst, None, YS[0:TILE * 11 if layer < 2 else TILE * 15, :], bass.IndirectOffsetOnAxis(IDX[c][:, t:t + 1], 0)), waits, "gpsimd")

        def experts(layer, units, ntile, placed, wx, free, finish_tile, shared=None, side=None):
            glu = layer != 2
            up_n = 512 if glu else 256
            cn = up_n + 256
            RAW = Ring([view(5120 + 1536 * i, 2 * cn, "p (f n) -> p f n", f=2) for i in range(4)])
            WS = Ring([pairview(4096 + 3072 * i, 2 * cn, "p (f n) -> p f n", f=2) for i in range(4)])
            HS = Ring([pairview(16384 + 1024 * i, 512, "p (f n) -> p f n", f=2) for i in range(4)])
            XP = Ring([pairview(20480 + 1024 * i, 512, "p (k n) -> p k n", k=2) for i in range(3)])
            H32 = Ring([view(11264 + 512 * i, 512) for i in range(3)])
            SG = Ring([view(12800 + 512 * i, 512) for i in range(3)])
            XR = Ring([view(14336 + 512 * i, 512, "p (u d) -> p u d", u=2) for i in range(2)])
            for ring in (RAW, WS, HS, XP, H32, SG, XR):
                for i in range(len(ring.bufs)):
                    ring.done(i, *free)
            ns = 4 if shared else 0
            tiles = ns + ntile
            todo = [(j, u) for j in range(tiles) for u in range(units)]
            raws, ws_, xs_, xr_, ys_ = {}, {}, {}, {}, {}
            W2 = T[f"l{layer}_ffn"]

            def fetch(i):
                if i >= len(todo):
                    return
                j, u = todo[i]
                raw, w, r = RAW.get()
                flat = raw.rearrange("p f n -> p (f n)")
                if j < ns:
                    t = load(f"fs{r}", flat, T[f"l{layer}_shared"][u], *w)
                else:
                    t = q.dma(f"fw{r}", lambda e: e.indirect_dma_start(
                        flat, None, W2, bass.IndirectOffsetOnAxis(WIX[:, j - ns, u:u + 1], 0)),
                        [wx, *w], "gpsimd")
                raws[i] = raw, t, r

            def weights(i):
                if i >= len(todo):
                    return
                raw, t, r = raws.pop(i)
                ws, w, rs = WS.get()
                tk = []
                for f in range(2):
                    tk += split([x[:, f, :] for x in ws], raw[:, f, :], [t], w, pool if f else dve)
                RAW.done(r, *tk)
                ws_[i] = ws, tk, rs

            def tile_load(j):
                if ns <= j < tiles:
                    xr, w, r = XR.get()
                    t = load(f"xs{r}", xr, XS[TILE * (j - ns):TILE * (j - ns) + TILE, :].rearrange(
                        "(u p) d -> p u d", p=P), *placed, *w)
                    xr_[j] = xr, t, r

            def tile_turn(j):
                if j >= tiles:
                    return
                if j < ns:
                    xs_[j] = [x[:, :, TILE * j:TILE * j + TILE] for x in XNT], shared, None
                    return
                xr, t, r = xr_.pop(j)
                s, w, rb = RB.get()
                for k in range(2):
                    for u in range(2):
                        m = pe(lambda e, k=k, u=u: e.transpose(
                            s[:, TILE * k + P * u:TILE * k + P * u + P], xr[:, u, P * k:P * k + P], ID), t, t_id, *w)
                XR.done(r, m)
                xp, w, rx = XP.get()
                tk = split([x.rearrange("p k n -> p (k n)") for x in xp], s, [m], w)
                RB.done(rb, *tk)
                xs_[j] = xp, tk, rx

            def up(i):
                j, u = todo[i]
                ws, wt, _ = ws_[i]
                xs, xt_, rx = xs_[j]
                s, w, r = RA.get()
                for f in range(2):
                    for z in range(2 if glu else 1):
                        for k in range(2):
                            c0 = 256 * z + 128 * k
                            d = s[:, 512 * z + TILE * f:512 * z + TILE * f + TILE]
                            for n, (a, b) in enumerate(((0, 0), (0, 1), (1, 0))):
                                m = pe(lambda e, d=d, a=a, b=b, c0=c0, k=k, f=f, n=n: e.matmul(
                                    d, ws[a][:, f, c0:c0 + 128], xs[b][:, k, :],
                                    start=(f == 0 and k == 0 and n == 0), stop=(f == 1 and k == 1 and n == 2),
                                    skip_group_check=True), *wt, *xt_, *w)
                if u == units - 1 and rx is not None:
                    XP.done(rx, m)
                h, hw, hr = H32.get()
                if glu:
                    sg, gw, gr = SG.get()
                    a = act(lambda e: e.activation(sg, s[:, 0:512], ACT.Silu), m, *gw)
                    o = dve(lambda e: e.tensor_tensor(h, sg, s[:, 512:1024], ALU.mult), a, *hw)
                    SG.done(gr, o)
                else:
                    o = dve(lambda e: e.tensor_scalar(h, s[:, 0:512], 0.0, None, ALU.max), m, *hw)
                RA.done(r, o)
                hs, w, hsr = HS.get()
                ht = split([x.rearrange("p f n -> p (f n)") for x in hs], h, [o], w)
                H32.done(hr, *ht)
                return i, hs, ht, hsr

            def down(i, hs, ht, hsr):
                j, u = todo[i]
                ws, wt, rs = ws_.pop(i)
                if u == 0:
                    ys_[j] = RB.get()
                y, yw, yr = ys_[j]
                for f in range(2):
                    for t in range(2):
                        for n, (a, b) in enumerate(((0, 0), (0, 1), (1, 0))):
                            m = pe(lambda e, f=f, t=t, a=a, b=b, n=n: e.matmul(
                                y[:, D * t:D * t + D], hs[a][:, f, P * t:P * t + P], ws[b][:, f, up_n:cn],
                                start=(u == 0 and f == 0 and t == 0 and n == 0),
                                stop=(u == units - 1 and f == 1 and n == 2), skip_group_check=True),
                                *ht, *yw)
                HS.done(hsr, m)
                WS.done(rs, m)
                if u == units - 1:
                    RB.done(yr, *finish_tile(j - ns, y.rearrange("p (u d) -> p u d", u=2), m))
                return m

            for i in range(3):
                fetch(i)
            tile_load(0)
            tile_load(1)
            weights(0)
            weights(1)
            tile_turn(0)
            prev = None
            for i, (j, u) in enumerate(todo):
                fetch(i + 3)
                weights(i + 2)
                cur = up(i)
                if u == 0:
                    tile_load(j + 1) if j + 1 not in xr_ else None
                if prev is not None:
                    m = down(*prev)
                if u == units - 2:
                    tile_turn(j + 1)
                if side and u % 2:
                    next(side, None)
                prev = cur
            for _ in side or ():
                pass
            return down(*prev)

        YB = Ring([view(15360 + 512 * i, 512, "p (u d) -> p u d", u=2) for i in range(2)])
        ys_t = []

        def put(j, yb, r, tk):
            t = load(f"ys{r}", YS[TILE * j:TILE * j + TILE, :].rearrange("(u p) d -> p u d", p=P), yb, *tk)
            YB.done(r, t)
            ys_t.append(t)

        def put_plain(j, y, m):
            if j < 0:
                for u in range(2):
                    t = 2 * (j + 4) + u
                    xt[t] = dve(lambda e, u=u, t=t: e.tensor_tensor(X[:, t, :], X[:, t, :], y[:, u, :], ALU.add),
                                m, xt[t])
                return xt[t - 1], xt[t]
            yb, w, r = YB.get()
            o = act(lambda e: e.activation(yb, y, ACT.Copy), m, *w)
            put(j, yb, r, [o])
            return [o]

        YG = view(5120, 4096, "p (n d) -> p n d", d=D)

        def returned(layer, copies, free):
            wait = list(ys_t) + free
            ys_t.clear()
            return {(c, t): gather(layer, c, t, f"yg{copies * t + c}", YG[:, copies * t + c, :], wait)
                    for t in range(NT) for c in range(copies)}

        def collect(got, dst, dst_t, gates, gate_t, first=False):
            for t in range(NT):
                for c, g in enumerate(gates):
                    n, tk = len(gates) * t + c, got[c, t]
                    if g is None:
                        fn = lambda e, n=n, t=t: e.tensor_tensor(dst[:, t, :], dst[:, t, :], YG[:, n, :], ALU.add)
                    elif first and c == 0:
                        fn = lambda e, n=n, t=t, g=g: e.tensor_scalar(dst[:, t, :], YG[:, n, :], g[:, t:t + 1], None,
                                                                      ALU.mult)
                    else:
                        fn = lambda e, n=n, t=t, g=g: e.scalar_tensor_tensor(
                            out=dst[:, t, :], in0=YG[:, n, :], scalar=g[:, t:t + 1], in1=dst[:, t, :], op0=ALU.mult,
                            op1=ALU.add)
                    dst_t[t] = dve(fn, tk, dst_t[t], *gate_t)
            return dst_t

        RW = view(6144, 256)
        LT = AF[0:8, 5120:6144]
        BCR = small(64, "p (t e) -> p t e", e=8)
        RWS = pairview(4096, 256, "p (k e) -> p k e", k=2)

        def finish(free):
            o = OUT.rearrange("b (t p) d -> p (b t) d", p=P)
            f = q.dma("out", lambda e: e.dma_start(o, X), list(xt) + list(free))
            q.add("sync", lambda e: e.nop(), [f])
            q.emit()

        def inputs(h, ring, free):
            nt = norm(X, XN, 4 * h, 4 * h + 4, xt, free)
            o, m = turn(XN, XNT, [h], nt, free, ring=ring)
            return nt, o, m

        def attention_inputs(before=None, bias_t=None, gain=None):
            def late(ring, free):
                if before:
                    before()
                halves = [(4 * h, 4 * h + 4) for h in range(2)]
                tk = [stats(X, lo, hi, xt, free) for lo, hi in halves]
                nt = {}
                for (lo, hi), t in zip(halves, list(tk)):
                    nt.update(scaled(X, XN, lo, hi, t))
                    if gain:
                        tk[lo // 4] = stats(XN, lo, hi, nt, [])
                out = []
                for h, (lo, hi) in enumerate(halves):
                    if bias_t:
                        for i in range(lo, hi):
                            xt[i] = pool(lambda e, i=i: e.tensor_tensor(X[:, i, :], X[:, i, :], BIAS, ALU.add),
                                         bias_t, nt[i], xt[i])
                    n2 = scaled(XN, XN, lo, hi, tk[h]) if gain else nt
                    o, m = turn(XN, XNT, [h], n2, free, gain, K32, ring)
                    out += o
                return out, m
            return late

        class Norms:

            def __init__(self):
                self.nt, self.lat = {}, []

            def half(self, h, ring, free):
                nt, o, self.lpe = inputs(h, ring, free)
                self.nt.update(nt)
                self.lat += o

        def context(gain, blocks, stage, tmp, free, ring=None):
            rel = list(free)
            for c in blocks:
                a, w, r = stage.get()
                ld = load(f"ctx{r}", a, T["ctx"][c // 2, 512 * (c % 2):512 * (c % 2) + 512].rearrange(
                    "(t p) d -> p t d", p=P), *w, *rel)
                yield
                nt = norm(a, a, 0, 4, [ld] * 4, rel)
                yield
                o, m = turn(a, [x[:, :, 512 * c:512 * c + 512] for x in C64], [0], nt, free, gain, tmp, ring)
                stage.done(r, m)
                ctx64[c // 2].extend(o)

        def stages(at, n):
            return Ring([view(at + 1024 * i, 1024, "p (t d) -> p t d", d=D) for i in range(n)])

        def raw_context(free):
            a = view(17424, 1024)
            rel = list(free)
            for b in range(B):
                for k in range(2):
                    ld = load("ctxT", a, T["ctxT"][b][:, 1024 * k:1024 * k + 1024], *rel)
                    yield
                    rel = split([x[:, k, 1024 * b:1024 * b + 1024] for x in C16], a, [ld], free)
                    ctx16.extend(rel)
                    yield

        ctx64, ctx16 = ([], []), []
        stage = stages(5120, 2)
        w0 = load("wa0", WR64[0], T["l0_w"][0])
        for _ in context((vec(V_CTXG), vec(V_CTXB)), [0, 1], stage, K32, []):
            pass
        tab = load("tab", TB, T["l0_tab"])
        bias_t = load("bias", BIAS, T["bc"][:, 0:256])
        xt += [load("x", X, xin)] * NT
        ZERO = view(15616, 1536)
        t_z = pool(lambda e: e.memset(ZERO, 0.0))
        for i in range(5):
            t_xs = load("zero", XS.rearrange("(p r) d -> p (r d)", p=P)[:, 1536 * i:1536 * i + 1536], ZERO, t_z)
        tab = dve(lambda e: e.tensor_scalar(TB[:, 1024:2048], TB[:, 1024:2048], SGN, None, ALU.mult), tab, t_vec)

        def second_batch(ring):
            for _ in context((vec(V_CTXG), vec(V_CTXB)), [2, 3], stage, K32, [], ring):
                pass

        nm = Norms()
        fr = attention64(0, attention_inputs(None, bias_t, (vec(V_LATG), vec(V_LATB))), ctx64, [tab], w0, [],
                         lambda ring, free: nm.half(0, ring, free), second_batch, [t_xs])
        if stop == 1:
            finish(fr)
            return

        def pre_ffn(fr, rw):
            w = load("rw", RW, rw, *fr)
            nm.half(1, RB4, fr)
            return nm.lat, nm.lpe, w, nm.nt

        lat, lpe, w, nt = pre_ffn(fr, T["l0_rw"])
        bt = load("rb", BCR, T["bc"][:, 1536:1600].rearrange("p (t e) -> p t e", e=8))
        o, o2 = logits(XNT, w, lat, fr, BCR, bt)
        o = top(LB, OH1, RT[:, 0, :], o2)
        ix, wx = route([OH1], 11, 4, o, fr)
        sc = scatter(XN, nt, ix)
        o = dve(lambda e: e.tensor_tensor(LB, LB, bc(RT[:, 0, :]), ALU.subtract), o)
        o = act(lambda e: e.activation(LB, LB, ACT.Exp), o)
        o = dve(lambda e: e.tensor_reduce(RT[:, 1, :], LB, AX.X, ALU.add), o)
        o = dve(lambda e: e.reciprocal(RT[:, 2, :], RT[:, 1, :]), o)
        w0 = load("wa0", WR64[0], T["l1_w"][0], *fr)
        ctx64 = ([], [])
        side = context((vec(V_GX), vec(V_BX)), range(4), stages(17424, 1), Ring([view(18448, 512)]), [*fr, wx])
        m = experts(0, 4, 11, sc, wx, [*fr, wx], put_plain, None, side)
        fr = [m, *ys_t]
        gates = [o]
        got = returned(0, 1, [m])

        def before():
            collect(got, X, xt, [RT[:, 2, :]], gates)

        if stop == 2:
            before()
            finish(fr)
            return

        tab = load("tab", TB, T["l1_tab"], *fr)
        nm = Norms()
        fr = attention64(1, attention_inputs(before, None, (vec(V_GL), vec(V_BL))), ctx64, [tab], w0, fr,
                         lambda ring, free: nm.half(0, ring, free))
        if stop == 3:
            finish(fr)
            return

        lat, lpe, w, nt = pre_ffn(fr, T["l1_rw"])
        o, _ = logits(XNT, w, lat, fr)
        o = top(LG, OH1, RT[:, 0, :], o)
        o = dve(lambda e: e.tensor_scalar(RT[:, 1, :], RT[:, 0, :], 0.0, None, ALU.min), o)
        o = dve(lambda e: e.scalar_tensor_tensor(out=RT[:, 2, :], in0=RT[:, 0, :], scalar=-1.0, in1=RT[:, 0, :],
                                                 op0=ALU.mult, op1=ALU.min), o)
        o = act(lambda e: e.activation(RT[:, 1:3, :], RT[:, 1:3, :], ACT.Exp), o)
        o = dve(lambda e: e.tensor_scalar(RT[:, 2, :], RT[:, 2, :], 1.0, None, ALU.add), o)
        o = dve(lambda e: e.reciprocal(RT[:, 2, :], RT[:, 2, :]), o)
        o = dve(lambda e: e.tensor_tensor(RT[:, 2, :], RT[:, 2, :], RT[:, 1, :], ALU.mult), o)
        ns = [dve(lambda e, i=i: e.tensor_scalar(XN[:, i, :], XN[:, i, :], RT[:, 2, i:i + 1], None, ALU.mult), o, lpe)
              for i in range(NT)]
        ix, wx = route([OH1], 11, 2, o, fr)
        sc = scatter(XN, ns, ix)
        w0 = first_weights(2, fr)
        bias_t = load("bias", BIAS, T["bc"][:, 256:512], *fr)
        m = experts(1, 2, 11, sc, wx, [*fr, wx], put_plain, lat, raw_context([*fr, wx]))
        fr = [m, *ys_t]
        got = returned(1, 1, [m])

        def before():
            collect(got, X, xt, [None], [])

        if stop == 4:
            before()
            finish(fr)
            return

        nm = Norms()
        fr = attention16(2, attention_inputs(before, bias_t), ctx16, w0, fr, lambda ring, free: nm.half(0, ring, free))
        if stop == 5:
            finish(fr)
            return

        lat, lpe, w, nt = pre_ffn(fr, T["l2_rw"])
        o, _ = logits(XNT, w, lat, fr)
        o = top(LG, OH1, RT[:, 0, :], o)
        o = second(LG, o)
        ix, wx = route([OH1, OH2], 15, 4, o, fr)
        sc = scatter(XN, nt, ix)
        gt = pair_gates(o)
        w0 = first_weights(3, fr)
        bias_t = load("bias", BIAS, T["bc"][:, 768:1024], *fr)
        m = experts(2, 4, 15, sc, wx, [*fr, wx], put_plain)
        fr = [m, *ys_t]
        got = returned(2, 2, [m])

        def before():
            collect(got, X, xt, [RT[:, 5, :], RT[:, 6, :]], [gt])

        if stop == 6:
            before()
            finish(fr)
            return

        nm = Norms()
        fr = attention16(3, attention_inputs(before, bias_t), ctx16, w0, fr, lambda ring, free: nm.half(0, ring, free))
        if stop == 7:
            finish(fr)
            return

        nm.half(1, RB4, fr)
        lat, lpe = nm.lat, nm.lpe
        WIO = view(17424, 1024)
        WIOS = pairview(23584, 1024, "p (a k n) -> p a k n", a=2, k=2)
        NW = view(18448, 512, "p (a n) -> p a n", a=2)
        JK = [view(18960 + 256 * i, 256) for i in range(2)]
        EN = Ring([view(19472 + 256 * i, 256) for i in range(2)])
        for i in range(2):
            EN.done(i, *fr)
        wio = load("wio", WIO, T["l3_wio"], *fr)
        wios = split([x.rearrange("p a k n -> p (a k n)") for x in WIOS], WIO, [wio], fr)
        nwt = load("nw", NW.rearrange("p a n -> p (a n)"), T["bc"][:, 1024:1536], *fr)
        w = load("rw", RW, T["l3_rw"], *fr)
        bt = load("rb", BCR, T["bc"][:, 1600:1664].rearrange("p (t e) -> p t e", e=8), *fr)

        def tokens(out, i, src, ww, waits):
            for k in range(2):
                m = mm3(out, [x[:, k, 128 * i:128 * i + 128] for x in src], [x[:, ww, k, :] for x in WIOS],
                        k == 0, k == 1, waits)
            return m

        def rms(src, i, col, tk, rel):
            return act(lambda e: e.activation(JK[i % 2], src, ACT.Square, accum_out=col), tk, *rel)

        def rsq(dst, src, tk):
            o = pool(lambda e: e.tensor_scalar(src, src, 1.0 / D, EPS3, ALU.mult, ALU.add), *tk)
            return pool(lambda e: e.tensor_tensor(dst, src, MHALF[:, 0:src.shape[1]], ALU.pow), o)

        jrel = [[], []]
        for i in range(NT):
            s, w_, r = RB.get()
            m = tokens(s[:, 0:256], i, XNT, 0, [*wios, *lat, *w_])
            a = dve(lambda e, s=s, i=i: e.tensor_copy(XN[:, i, :], s[:, 0:256]), m, lpe)
            RB.done(r, a)
            o = rms(XN[:, i, :], i, VE[:, i:i + 1], a, jrel[i % 2])
            jrel[i % 2] = [o]
        o = rsq(RS[:, 0:8], VE[:, 0:8], [o])
        hn = [dve(lambda e, i=i: e.scalar_tensor_tensor(out=XN[:, i, :], in0=XN[:, i, :], scalar=RS[:, i:i + 1],
                                                        in1=NW[:, 0, :], op0=ALU.mult, op1=ALU.mult), o, nwt)
              for i in range(NT)]
        lat, lpe = turn(XN, XNT, range(2), hn, [m])
        o, o2 = logits(XNT, w, lat, fr, BCR, bt)
        o = top(LB, OH1, RT[:, 0, :], o2)
        o = second(LB, o)
        ix, wx = route([OH1, OH2], 15, 4, o, fr)
        sc = scatter(XN, hn, ix)
        for n, oh in enumerate((OH1, OH2)):
            o = dve(lambda e, oh=oh: e.tensor_tensor(LB, oh, LG, ALU.mult), o)
            o = dve(lambda e, n=n: e.tensor_reduce(RT[:, n, :], LB, AX.X, ALU.add), o)
        gt = pair_gates(o)
        msrel = [[], []]

        def put_normed(j, y, m):
            u = j % 2
            ms, grr = MS[:, u, :], GR[:, u, :]
            en, w, er = EN.get()
            ent = q.dma(f"en{er}", lambda e: e.indirect_dma_start(
                en, None, T["l3_en"], bass.IndirectOffsetOnAxis(EIX[:, j:j + 1], 0)), [wx, *w], "gpsimd")
            for n in range(2):
                o = rms(y[:, n, :], n, ms[:, n:n + 1], m, jrel[n] + msrel[u])
                jrel[n] = [o]
            o = rsq(grr, ms, [o] + msrel[u])
            yb, w, r = YB.get()
            for n in range(2):
                d = dve(lambda e, n=n: e.scalar_tensor_tensor(
                    out=yb[:, n, :], in0=y[:, n, :], scalar=grr[:, n:n + 1], in1=en, op0=ALU.mult, op1=ALU.mult),
                    o, ent, *w)
            EN.done(er, d)
            msrel[u] = [d]
            put(j, yb, r, [d])
            return [d]

        m = experts(3, 4, 15, sc, wx, [*fr, wx], put_normed)
        ACC = view(9216, 2048, "p (t n) -> p t n", n=256)
        acct = collect(returned(3, 2, [m]), ACC, [None] * NT, [RT[:, 5, :], RT[:, 6, :]], [gt, m], True)
        for i in range(NT):
            o = rms(ACC[:, i, :], i, VE[:, i:i + 1], acct[i], jrel[i % 2])
            jrel[i % 2] = [o]
        o = rsq(RS[:, 0:8], VE[:, 0:8], [o])
        hn = [dve(lambda e, i=i: e.scalar_tensor_tensor(out=XN[:, i, :], in0=ACC[:, i, :], scalar=RS[:, i:i + 1],
                                                        in1=NW[:, 1, :], op0=ALU.mult, op1=ALU.mult), o, lpe, *sc)
              for i in range(NT)]
        lat, lpe = turn(XN, XNT, range(2), hn, [m])
        for i in range(NT):
            s, w_, r = RB.get()
            m = tokens(s[:, 0:256], i, XNT, 1, [*lat, *w_])
            xt[i] = dve(lambda e, s=s, i=i: e.tensor_tensor(X[:, i, :], X[:, i, :], s[:, 0:256], ALU.add), m, xt[i])
            RB.done(r, xt[i])
        finish([])


def rope_table(n, d, slot, copies):
    inv = (np.float32(1.0) / np.float32(10000.0) ** (np.arange(0, d, 2, dtype=np.float32) / np.float32(d)))
    ang = (np.arange(n, dtype=np.float32)[:, None] * inv.astype(np.float32)[None, :]).astype(np.float32)
    c, s = np.cos(ang).astype(np.float32).T, np.sin(ang).astype(np.float32).T
    cos, sin = np.zeros((copies, slot, n), np.float32), np.zeros((copies, slot, n), np.float32)
    h = d // 2
    cos[:, d:] = 1.0
    cos[:, 0:h], cos[:, h:d], sin[:, 0:h], sin[:, h:d] = c, c, -s, s
    return np.concatenate([cos.reshape(-1, n), sin.reshape(-1, n)], axis=1)


def layout(a):
    def f(n):
        return np.asarray(a[n])

    def rows(w):
        k = w.shape[0] // P
        return w.reshape(k, P, -1).transpose(1, 0, 2).reshape(P, -1)

    def swap(w, d):
        v = w.reshape(w.shape[0], -1, 2, d // 2)
        return np.concatenate([v[:, :, 1], v[:, :, 0]], axis=2).reshape(w.shape)

    def slots(w):
        o = np.zeros((w.shape[0], 16, 32), np.float32)
        o[:, :, 0:16] = w.reshape(w.shape[0], 16, 16)
        return o.reshape(w.shape[0], 512)

    T = {"x": f("x"), "ctx": f("ctx_1024")}
    v = np.zeros((P, 26), np.float32)
    for i, n in enumerate(("L0_xattn_ln_lat_g", "L0_xattn_ln_lat_b", "L0_xattn_ln_ctx_g", "L0_xattn_ln_ctx_b",
                           "L1_xattn_gamma_x", "L1_xattn_beta_x", "L1_xattn_gamma_l", "L1_xattn_beta_l")):
        v[:, 2 * i:2 * i + 2] = f(n).reshape(2, P).T
    bkv = f("L2_xattn_bkv")
    v[:, 16:20] = slots(f("L2_xattn_bq")[None]).reshape(4, P).T
    v[:, 20:24] = slots(bkv[None, 0:256]).reshape(4, P).T
    v[16::32, 20:24] = 1.0
    v[:, 24] = np.where(np.arange(P) % 64 < 32, -1.0, 1.0)
    v[16::32, 25] = 1.0
    T["vec"] = v
    T["rev"] = np.broadcast_to(np.tile(np.arange(8, 0, -1, dtype=np.float32), 8), (P, 64))
    row = np.concatenate([f("L0_xattn_bo"), f("L2_xattn_bp"), bkv[256:512], f("L3_xattn_bo"),
                          f("L3_ffn_in_norm_w"), f("L3_ffn_out_norm_w"), np.tile(f("L0_ffn_router_b"), 8),
                          np.tile(f("L3_ffn_expert_bias"), 8)])
    T["bc"] = np.broadcast_to(row, (P, row.size))
    sel = np.zeros((P, P), np.float32)
    for j in range(4):
        sel[32 * j + 16, 32 * j:32 * j + 32] = 1.0
    T["sel"] = sel
    T["ctxT"] = np.stack([rows(f("ctx_1024")[b].T) for b in range(2)])
    cs = [np.concatenate([f(n).T] * 4) for n in ("L0_xattn_cos", "L0_xattn_sin")]
    T["l0_tab"] = np.concatenate(cs, axis=1)
    T["l1_tab"] = rope_table(1024, 64, 64, 2)
    T["l3_tab"] = rope_table(1024, 16, 32, 4)

    for L, inner in ((0, 1024), (1, 512)):
        wq, wkv, wo = f(f"L{L}_xattn_Wq"), f(f"L{L}_xattn_Wkv"), f(f"L{L}_xattn_Wo")
        wk, wv = wkv[:, 0:inner], wkv[:, inner:]
        wr = swap(wk, 64)
        T[f"l{L}_w"] = np.stack([np.concatenate(
            [rows(w[:, 128 * g:128 * g + 128]) for w in (wq, wk, wr, wv)] + [wo[128 * g:128 * g + 128]],
            axis=1) for g in range(inner // 128)])

    for L, wo in ((2, "L2_xattn_Wp"), (3, "L3_xattn_Wo")):
        wq, wkv = f(f"L{L}_xattn_Wq"), f(f"L{L}_xattn_Wkv")
        wk, wv = wkv[:, 0:256], wkv[:, 256:512]
        parts = [slots(w) for w in (wq, swap(wq, 16), wk, swap(wk, 16))]
        T[f"l{L}_w"] = np.stack([np.concatenate([rows(w[:, 128 * g:128 * g + 128]) for w in parts], axis=1)
                                 for g in range(4)])
        T[f"l{L}_wv"] = rows(wv)
        o = np.zeros((16, 32, D), np.float32)
        o[:, 0:16] = f(wo).reshape(16, 16, D)
        T[f"l{L}_wo"] = o.reshape(4, P, D)

    def pieces(ups, dn):
        n = dn.shape[0] // P
        one = [np.concatenate([rows(w[:, P * i:P * i + P]) for w in ups] + [dn[P * i:P * i + P]], axis=1)
               for i in range(n)]
        return np.stack([np.concatenate(one[i:i + 2], axis=1) for i in range(0, n, 2)])

    def table(x):
        x = np.stack(x)
        return x.reshape(-1, x.shape[-1])

    w1, w2 = f("L0_ffn_w1"), f("L0_ffn_w2")
    T["l0_ffn"] = table([pieces((w1[e][:, 0:1024], w1[e][:, 1024:]), w2[e]) for e in range(8)])
    g, u, d = f("L1_ffn_expert_gate"), f("L1_ffn_expert_up"), f("L1_ffn_expert_down")
    T["l1_ffn"] = table([pieces((g[e], u[e]), d[e]) for e in range(8)])
    T["l1_shared"] = pieces((f("L1_ffn_shared_gate"), f("L1_ffn_shared_up")), f("L1_ffn_shared_down"))
    w1, w2 = f("L2_ffn_w1"), f("L2_ffn_w2")
    T["l2_ffn"] = table([pieces((w1[e].T,), w2[e].T) for e in range(8)])
    g, u, d = f("L3_ffn_Wg"), f("L3_ffn_Wu"), f("L3_ffn_Wd")
    T["l3_ffn"] = table([pieces((g[e].T, u[e].T), d[e].T) for e in range(8)])
    T["l3_en"] = f("L3_ffn_enorm_w")
    cst = np.zeros((P, 88), np.float32)
    cst[:, 0:16] = np.arange(16)
    cst[:, 16:20] = np.arange(P)[:, None] + P * np.arange(4)[None]
    cst[:, 20:24] = 256 * np.arange(4)
    cst[:, 24:88] = np.tril(np.ones((8, 8), np.float32)).reshape(-1)
    T["cst"] = cst
    T["l3_wio"] = np.concatenate([rows(f("L3_ffn_W_in").T), rows(f("L3_ffn_W_out").T)], axis=1)

    def rw(w):
        return rows(np.concatenate([w, np.zeros((D, P - 8), np.float32)], axis=1))

    T["l0_rw"] = rw(f("L0_ffn_router_w"))
    T["l1_rw"] = rw(f("L1_ffn_router_w").T)
    T["l2_rw"] = rw(f("L2_ffn_gate_w").T)
    T["l3_rw"] = rw(f("L3_ffn_Wr").T)
    return {n: np.ascontiguousarray(x) for n, x in T.items()}


def kernel(**inputs):
    import concourse.bacc as _bacc
    from concourse.bass_utils import run_bass_kernel_spmd as _run

    nc = _bacc.Bacc("TRN2", target_bir_lowering=False, num_devices=1)
    arrays = layout(inputs)
    T = {n: nc.dram_tensor(f"in_{n}", x.shape, F32, kind="ExternalInput").ap() for n, x in arrays.items()}
    out = nc.dram_tensor("out_x", (2, 512, 256), F32, kind="ExternalOutput").ap()
    build(nc, T, out)
    r = _run(nc, [{f"in_{n}": x for n, x in arrays.items()}], core_ids=[0])
    return r.results[0]["out_x"]
```
